# Optimizing a Trainium2 kernel written in Bass

```python
import numpy as np
import jax
import jax.numpy as jnp

def _softmax(x, axis=-1):
    return jax.nn.softmax(x, axis=axis)

def _gelu(x):
    return jax.nn.gelu(x, approximate=True)

def _silu(x):
    return jax.nn.silu(x)

def _sigmoid(x):
    return jax.nn.sigmoid(x)

def _layernorm(x, axis=-1, eps=1e-05):
    m = jnp.mean(x, axis=axis, keepdims=True)
    v = jnp.var(x, axis=axis, keepdims=True)
    return (x - m) / jnp.sqrt(v + eps)

def _scatter_add(tgt, idx, src, axis=0):
    return tgt.at[idx].add(src)

def _segment_sum(src, seg, n):
    return jax.ops.segment_sum(src, seg, n)
kernel_name = 'mk_conv_attn_hybrid_d4_conv_nhwc128_r2_65a61b'

def setup_inputs(seed: int=0):
    np.random.seed(seed)
    _w = jnp.asarray

    def _rec_inputs():
        import jax
        import jax.numpy as jnp
        _gk = jax.random.key(seed)
        x = -0.000929 + 1 * jax.random.normal(jax.random.fold_in(_gk, 1), (2, 32, 32, 64), jnp.float32)
        return x
    x = _rec_inputs()

    def _L0_conv_setup():
        import jax, jax.numpy as jnp
        import numpy as np
        D_MODEL = 64
        D_STATE = 16
        D_INNER = 128
        DT_RANK = 8
        K = 4
        B, H, W = (2, 32, 32)

        def silu(x):
            return x * jax.nn.sigmoid(x)

        def selective_scan(xs, dts, As, Bs, Cs, Ds, dt_bias):
            delta = jax.nn.softplus(dts + dt_bias[None, :, :, None])
            d_l = jnp.moveaxis(delta, -1, 0)
            x_l = jnp.moveaxis(xs, -1, 0)
            B_l = jnp.moveaxis(Bs, -1, 0)
            C_l = jnp.moveaxis(Cs, -1, 0)

            def step(h, inp):
                d_t, x_t, B_t, C_t = inp
                dA = jnp.exp(d_t[..., None] * As)
                h = dA * h + (d_t * x_t)[..., None] * B_t[:, :, None, :]
                y = jnp.einsum('bkdn,bkn->bkd', h, C_t)
                return (h, y)
            h0 = jnp.zeros((xs.shape[0], K, As.shape[1], As.shape[2]), xs.dtype)
            _, ys = jax.lax.scan(step, h0, (d_l, x_l, B_l, C_l))
            ys = jnp.moveaxis(ys, 0, -1)
            return ys + Ds[None, :, :, None] * xs
        key = jax.random.key(seed)
        ks = jax.random.split(key, 8)
        f = lambda k, s, scale=0.02: jax.random.normal(k, s, dtype=jnp.float32) * scale
        A = jnp.tile(jnp.arange(1, D_STATE + 1, dtype=jnp.float32)[None, :], (K * D_INNER, 1))
        return {'x': jax.random.normal(ks[0], (B, H, W, D_MODEL), dtype=jnp.float32), 'w_in': f(ks[1], (2 * D_INNER, D_MODEL)), 'conv_w': f(ks[2], (D_INNER, 1, 3, 3)), 'conv_b': jnp.zeros((D_INNER,), jnp.float32), 'x_proj_w': f(ks[3], (K, DT_RANK + 2 * D_STATE, D_INNER)), 'dt_w': f(ks[4], (K, D_INNER, DT_RANK)), 'dt_b': f(ks[5], (K, D_INNER), 0.1), 'A_logs': jnp.log(A), 'Ds': jnp.ones((K * D_INNER,), jnp.float32), 'ln_w': jnp.ones((D_INNER,), jnp.float32), 'ln_b': jnp.zeros((D_INNER,), jnp.float32), 'w_out': f(ks[6], (D_MODEL, D_INNER))}
    _L0_conv_all = _L0_conv_setup()
    _L0_conv_in = {k: v for k, v in _L0_conv_all.items() if k in ('w_in', 'conv_w', 'conv_b', 'x_proj_w', 'dt_w', 'dt_b', 'A_logs', 'Ds', 'ln_w', 'ln_b', 'w_out')}
    del _L0_conv_all

    def _L1_conv_setup():
        import jax, jax.numpy as jnp
        import numpy as np
        B, H, W, C, K, T = (16, 64, 64, 32, 7, 16)
        C2 = 2 * C

        def _pad_and_fft(kr, ki, h, w, k):
            kern = kr + 1j * ki
            ph = (h - k) // 2
            pw = (w - k) // 2
            padded = jnp.pad(kern, ((0, 0), (ph, h - k - ph), (pw, w - k - pw)))
            return jnp.fft.fft2(padded, axes=(-2, -1))
        key = jax.random.key(seed)
        ks = jax.random.split(key, 12)
        d = {'x_ri': jax.random.normal(ks[0], (B, H, W, C2), jnp.float32), 'Wf': jax.random.normal(ks[1], (C2, C2), jnp.float32) * 0.05, 'bf': jnp.zeros((C2,), jnp.float32), 'Wi': jax.random.normal(ks[2], (C2, C2), jnp.float32) * 0.05, 'bi': jnp.zeros((C2,), jnp.float32), 'Wd': jax.random.normal(ks[3], (C2, C2), jnp.float32) * 0.05, 'bd': jnp.zeros((C2,), jnp.float32), 'A_real': jax.random.normal(ks[4], (C, K, K), jnp.float32) * 0.02, 'A_imag': jax.random.normal(ks[5], (C, K, K), jnp.float32) * 0.02, 'B_real': jax.random.normal(ks[6], (C, K, K), jnp.float32) * 0.02, 'B_imag': jax.random.normal(ks[7], (C, K, K), jnp.float32) * 0.02}
        return d
    _L1_conv_all = _L1_conv_setup()
    _L1_conv_in = {k: v for k, v in _L1_conv_all.items() if k in ('Wf', 'bf', 'Wi', 'bi', 'Wd', 'bd', 'A_real', 'A_imag', 'B_real', 'B_imag')}
    del _L1_conv_all

    def _L2_attn_setup():
        import jax, jax.numpy as jnp
        import numpy as np
        HEADS = 4
        DIM_HEAD = 32
        EPS = 1e-05
        key = jax.random.key(seed)
        k1, k2, k3 = jax.random.split(key, 3)
        H, W, C = (256, 256, 64)
        dim = HEADS * DIM_HEAD
        x = jax.random.normal(k1, (H, W, C), dtype=jnp.float32)
        w_in = jax.random.normal(k2, (3 * dim, C), dtype=jnp.float32) / np.sqrt(C)
        w_out = jax.random.normal(k3, (C, dim), dtype=jnp.float32) / np.sqrt(dim)
        b_out = jnp.zeros((C,), dtype=jnp.float32)
        ln_w = jnp.ones((C,), dtype=jnp.float32)
        return {'x': x, 'w_in': w_in, 'w_out': w_out, 'b_out': b_out, 'ln_w': ln_w}
    _L2_attn_all = _L2_attn_setup()
    _L2_attn_in = {k: v for k, v in _L2_attn_all.items() if k in ('w_in', 'w_out', 'b_out', 'ln_w')}
    del _L2_attn_all

    def _L2_ffn_setup():
        import jax, jax.numpy as jnp
        import numpy as np
        B, N, D, C, E, K = (8, 4096, 64, 64, 8, 2)
        key = jax.random.key(seed)
        k0, k1, k2 = jax.random.split(key, 3)
        x = jax.random.normal(k0, (B, N, D), dtype=jnp.float32)
        router_w = jax.random.normal(k1, (D, E), dtype=jnp.float32) * 0.05
        router_b = jnp.zeros((E,), dtype=jnp.float32)
        expert_w = jax.random.normal(k2, (E, D, C), dtype=jnp.float32) * (1.0 / np.sqrt(D))
        expert_b = jnp.zeros((E, C), dtype=jnp.float32)
        return {'x': x, 'router_w': router_w, 'router_b': router_b, 'expert_w': expert_w, 'expert_b': expert_b}
    _L2_ffn_all = _L2_ffn_setup()
    _L2_ffn_in = {k: v for k, v in _L2_ffn_all.items() if k in ('router_w', 'router_b', 'expert_w', 'expert_b')}
    del _L2_ffn_all

    def _L3_attn_setup():
        import jax, jax.numpy as jnp
        import numpy as np
        B, N, D = (8, 1024, 64)
        N_LAYER, N_HEAD = (4, 8)
        PARAMS_STD = 0.05

        def _attention(V, Q, Z):
            n = Z.shape[1]
            Attn = jnp.einsum('bni,ij,bmj->bnm', Z, Q, Z)
            values = jnp.einsum('ij,bnj->bni', V, Z)
            return jnp.einsum('bnm,bmi->bni', Attn, values) / n
        key = jax.random.key(seed)
        kz, kv, kq = jax.random.split(key, 3)
        Z = jax.random.normal(kz, (B, N, D), dtype=jnp.float32)
        v_matrix = PARAMS_STD * jax.random.normal(kv, (N_LAYER, N_HEAD, 1, D, D), dtype=jnp.float32)
        q_matrix = PARAMS_STD * jax.random.normal(kq, (N_LAYER, N_HEAD, 1, D, D), dtype=jnp.float32)
        return {'Z': Z, 'v_matrix': v_matrix, 'q_matrix': q_matrix}
    _L3_attn_all = _L3_attn_setup()
    _L3_attn_in = {k: v for k, v in _L3_attn_all.items() if k in ('v_matrix', 'q_matrix')}
    del _L3_attn_all

    def _L3_ffn_setup():
        import jax, jax.numpy as jnp
        import numpy as np
        PADDED_SL = 4096
        TEMPERATURE = 1.0
        SIGMA_POW = 0.25

        def _stu_conv(phi, u, n):
            b, sl, d = u.shape
            sgn = jnp.where(jnp.arange(sl) % 2 == 0, 1.0, -1.0).astype(u.dtype)
            sgn3 = sgn[None, :, None]
            Vf = jnp.fft.rfft(phi, n=n, axis=0)
            Uf_p = jnp.fft.rfft(u, n=n, axis=1)
            Uf_m = jnp.fft.rfft(u * sgn3, n=n, axis=1)
            U_plus = jnp.fft.irfft(Vf[None, :, :, None] * Uf_p[:, :, None, :], n=n, axis=1)[:, :sl]
            U_minus = jnp.fft.irfft(Vf[None, :, :, None] * Uf_m[:, :, None, :], n=n, axis=1)[:, :sl]
            U_minus = U_minus * sgn[None, :, None, None]
            return (U_plus, U_minus)

        def _compute_spectral(u, sigma, phi, Mpp, Mpm):
            U_plus, U_minus = _stu_conv(phi, u, PADDED_SL)
            s = sigma ** SIGMA_POW
            out = jnp.einsum('btkd,k,kde->bte', U_plus, s, Mpp)
            out = out + jnp.einsum('btkd,k,kde->bte', U_minus, s, Mpm)
            return out

        def _compute_ar_u(Mu, u):
            sl = u.shape[1]
            out = jnp.zeros(u.shape[:2] + (Mu.shape[-1],), dtype=u.dtype)
            for i in range(Mu.shape[0]):
                ui = jnp.pad(u, ((0, 0), (i, 0), (0, 0)))[:, :sl]
                out = out + jnp.einsum('btd,de->bte', ui, Mu[i])
            return out

        def _stu(u, sigma, phi, Mu, Mpp, Mpm):
            return _compute_spectral(u, sigma, phi, Mpp, Mpm) + _compute_ar_u(Mu, u)
        key = jax.random.key(seed)
        ks = jax.random.split(key, 8)
        b, sl, d, K, k_u = (2, 2048, 64, 16, 3)
        x = jax.random.normal(ks[0], (b, sl, d), dtype=jnp.float32)
        sigma = jax.random.uniform(ks[1], (K,), dtype=jnp.float32, minval=0.001, maxval=1.0)
        phi = jax.random.normal(ks[2], (sl, K), dtype=jnp.float32) / np.sqrt(sl)
        M_u = jax.random.normal(ks[3], (4, k_u, d, d), dtype=jnp.float32) * 0.02
        M_phi_plus = jax.random.normal(ks[4], (4, K, d, d), dtype=jnp.float32) * 0.02
        M_phi_minus = jax.random.normal(ks[5], (4, K, d, d), dtype=jnp.float32) * 0.02
        log_weights = jnp.ones((4,), dtype=jnp.float32)
        u01 = jax.random.uniform(ks[6], (4,), dtype=jnp.float32, minval=1e-06, maxval=1.0 - 1e-06)
        gumbel = -jnp.log(-jnp.log(u01))
        return {'x': x, 'sigma': sigma, 'phi': phi, 'M_u': M_u, 'M_phi_plus': M_phi_plus, 'M_phi_minus': M_phi_minus, 'log_weights': log_weights, 'gumbel': gumbel}
    _L3_ffn_all = _L3_ffn_setup()
    _L3_ffn_in = {k: v for k, v in _L3_ffn_all.items() if k in ('sigma', 'phi', 'M_u', 'M_phi_plus', 'M_phi_minus', 'log_weights', 'gumbel')}
    del _L3_ffn_all
    return {'x': x, 'L0_conv_w_in': _L0_conv_in['w_in'], 'L0_conv_conv_w': _L0_conv_in['conv_w'], 'L0_conv_conv_b': _L0_conv_in['conv_b'], 'L0_conv_x_proj_w': _L0_conv_in['x_proj_w'], 'L0_conv_dt_w': _L0_conv_in['dt_w'], 'L0_conv_dt_b': _L0_conv_in['dt_b'], 'L0_conv_A_logs': _L0_conv_in['A_logs'], 'L0_conv_Ds': _L0_conv_in['Ds'], 'L0_conv_ln_w': _L0_conv_in['ln_w'], 'L0_conv_ln_b': _L0_conv_in['ln_b'], 'L0_conv_w_out': _L0_conv_in['w_out'], 'L1_conv_Wf': _L1_conv_in['Wf'], 'L1_conv_bf': _L1_conv_in['bf'], 'L1_conv_Wi': _L1_conv_in['Wi'], 'L1_conv_bi': _L1_conv_in['bi'], 'L1_conv_Wd': _L1_conv_in['Wd'], 'L1_conv_bd': _L1_conv_in['bd'], 'L1_conv_A_real': _L1_conv_in['A_real'], 'L1_conv_A_imag': _L1_conv_in['A_imag'], 'L1_conv_B_real': _L1_conv_in['B_real'], 'L1_conv_B_imag': _L1_conv_in['B_imag'], 'L2_attn_w_in': _L2_attn_in['w_in'], 'L2_attn_w_out': _L2_attn_in['w_out'], 'L2_attn_b_out': _L2_attn_in['b_out'], 'L2_attn_ln_w': _L2_attn_in['ln_w'], 'L2_ffn_router_w': _L2_ffn_in['router_w'], 'L2_ffn_router_b': _L2_ffn_in['router_b'], 'L2_ffn_expert_w': _L2_ffn_in['expert_w'], 'L2_ffn_expert_b': _L2_ffn_in['expert_b'], 'L3_attn_v_matrix': _L3_attn_in['v_matrix'], 'L3_attn_q_matrix': _L3_attn_in['q_matrix'], 'L3_ffn_sigma': _L3_ffn_in['sigma'], 'L3_ffn_phi': _L3_ffn_in['phi'], 'L3_ffn_M_u': _L3_ffn_in['M_u'], 'L3_ffn_M_phi_plus': _L3_ffn_in['M_phi_plus'], 'L3_ffn_M_phi_minus': _L3_ffn_in['M_phi_minus'], 'L3_ffn_log_weights': _L3_ffn_in['log_weights'], 'L3_ffn_gumbel': _L3_ffn_in['gumbel']}

def reference(x, L0_conv_w_in, L0_conv_conv_w, L0_conv_conv_b, L0_conv_x_proj_w, L0_conv_dt_w, L0_conv_dt_b, L0_conv_A_logs, L0_conv_Ds, L0_conv_ln_w, L0_conv_ln_b, L0_conv_w_out, L1_conv_Wf, L1_conv_bf, L1_conv_Wi, L1_conv_bi, L1_conv_Wd, L1_conv_bd, L1_conv_A_real, L1_conv_A_imag, L1_conv_B_real, L1_conv_B_imag, L2_attn_w_in, L2_attn_w_out, L2_attn_b_out, L2_attn_ln_w, L2_ffn_router_w, L2_ffn_router_b, L2_ffn_expert_w, L2_ffn_expert_b, L3_attn_v_matrix, L3_attn_q_matrix, L3_ffn_sigma, L3_ffn_phi, L3_ffn_M_u, L3_ffn_M_phi_plus, L3_ffn_M_phi_minus, L3_ffn_log_weights, L3_ffn_gumbel):
    import jax
    import jax.numpy as jnp

    def _L0_conv_ref(x, w_in, conv_w, conv_b, x_proj_w, dt_w, dt_b, A_logs, Ds, ln_w, ln_b, w_out):
        import jax, jax.numpy as jnp
        import numpy as np
        D_MODEL = 64
        D_STATE = 16
        D_INNER = 128
        DT_RANK = 8
        K = 4
        B, H, W = (2, 32, 32)

        def silu(x):
            return x * jax.nn.sigmoid(x)

        def selective_scan(xs, dts, As, Bs, Cs, Ds, dt_bias):
            delta = jax.nn.softplus(dts + dt_bias[None, :, :, None])
            d_l = jnp.moveaxis(delta, -1, 0)
            x_l = jnp.moveaxis(xs, -1, 0)
            B_l = jnp.moveaxis(Bs, -1, 0)
            C_l = jnp.moveaxis(Cs, -1, 0)

            def step(h, inp):
                d_t, x_t, B_t, C_t = inp
                dA = jnp.exp(d_t[..., None] * As)
                h = dA * h + (d_t * x_t)[..., None] * B_t[:, :, None, :]
                y = jnp.einsum('bkdn,bkn->bkd', h, C_t)
                return (h, y)
            h0 = jnp.zeros((xs.shape[0], K, As.shape[1], As.shape[2]), xs.dtype)
            _, ys = jax.lax.scan(step, h0, (d_l, x_l, B_l, C_l))
            ys = jnp.moveaxis(ys, 0, -1)
            return ys + Ds[None, :, :, None] * xs
        xz = x @ w_in.T
        xi, z = jnp.split(xz, 2, axis=-1)
        z = silu(z)
        xc = jnp.transpose(xi, (0, 3, 1, 2))
        xc = jax.lax.conv_general_dilated(xc, conv_w, (1, 1), 'SAME', feature_group_count=D_INNER, dimension_numbers=('NCHW', 'OIHW', 'NCHW')) + conv_b[None, :, None, None]
        xc = silu(xc)
        b, d, h, w = xc.shape
        L = h * w
        x_flat = xc.reshape(b, d, L)
        x_t = jnp.transpose(xc, (0, 1, 3, 2)).reshape(b, d, L)
        x_hwwh = jnp.stack([x_flat, x_t], axis=1)
        xs = jnp.concatenate([x_hwwh, jnp.flip(x_hwwh, axis=-1)], axis=1)
        x_dbl = jnp.einsum('bkdl,kcd->bkcl', xs, x_proj_w)
        dts, Bs, Cs = jnp.split(x_dbl, [DT_RANK, DT_RANK + D_STATE], axis=2)
        dts = jnp.einsum('bkrl,kdr->bkdl', dts, dt_w)
        As = -jnp.exp(A_logs).reshape(K, d, D_STATE)
        out_y = selective_scan(xs, dts, As, Bs, Cs, Ds.reshape(K, d), dt_b)
        inv_y = jnp.flip(out_y[:, 2:4], axis=-1)
        wh_y = jnp.transpose(out_y[:, 1].reshape(b, d, w, h), (0, 1, 3, 2)).reshape(b, d, L)
        invwh_y = jnp.transpose(inv_y[:, 1].reshape(b, d, w, h), (0, 1, 3, 2)).reshape(b, d, L)
        y = out_y[:, 0] + inv_y[:, 0] + wh_y + invwh_y
        y = jnp.transpose(y, (0, 2, 1))
        mu = y.mean(-1, keepdims=True)
        var = ((y - mu) ** 2).mean(-1, keepdims=True)
        y = (y - mu) / jnp.sqrt(var + 1e-05) * ln_w + ln_b
        y = y.reshape(b, h, w, d) * z
        return y @ w_out.T

    def _L1_conv_ref(x_ri, Wf, bf, Wi, bi, Wd, bd, A_real, A_imag, B_real, B_imag):
        import jax, jax.numpy as jnp
        import numpy as np
        B, H, W, C, K, T = (16, 64, 64, 32, 7, 16)
        C2 = 2 * C

        def _pad_and_fft(kr, ki, h, w, k):
            kern = kr + 1j * ki
            ph = (h - k) // 2
            pw = (w - k) // 2
            padded = jnp.pad(kern, ((0, 0), (ph, h - k - ph), (pw, w - k - pw)))
            return jnp.fft.fft2(padded, axes=(-2, -1))
        b, h, w, c2 = x_ri.shape
        c = c2 // 2
        k = A_real.shape[-1]
        forget_gate = jax.nn.sigmoid(x_ri @ Wf + bf + 2.0)
        input_gate = jax.nn.sigmoid(x_ri @ Wi + bi)
        delta = jax.nn.softplus(x_ri @ Wd + bd) * 0.1
        A_f = _pad_and_fft(A_real, A_imag, h, w, k)
        B_f = _pad_and_fft(B_real, B_imag, h, w, k)
        A_ri = jnp.concatenate([A_f.real, A_f.imag], 0).transpose(1, 2, 0)[None]
        B_ri = jnp.concatenate([B_f.real, B_f.imag], 0).transpose(1, 2, 0)[None]
        Ar, Ai = (A_ri[..., :c], A_ri[..., c:])
        mag = jnp.sqrt(Ar ** 2 + Ai ** 2 + 1e-08)
        scale = 0.95 * jax.nn.sigmoid(mag) / (mag + 1e-08)
        Ar = Ar * scale
        Ai = Ai * scale
        Br, Bi_ = (B_ri[..., :c], B_ri[..., c:])
        x_r, x_i = (x_ri[..., :c], x_ri[..., c:])
        Bx_r = Br * x_r - Bi_ * x_i
        Bx_i = Br * x_i + Bi_ * x_r
        inp_r = delta[..., :c] * input_gate[..., :c] * Bx_r
        inp_i = delta[..., c:] * input_gate[..., c:] * Bx_i
        fg_r, fg_i = (forget_gate[..., :c], forget_gate[..., c:])

        def step(h_state, _):
            h_r, h_i = h_state
            Ah_r = Ar * h_r - Ai * h_i
            Ah_i = Ar * h_i + Ai * h_r
            return ((fg_r * Ah_r + inp_r, fg_i * Ah_i + inp_i), None)
        h0 = (jnp.zeros_like(x_r), jnp.zeros_like(x_i))
        (h_r, h_i), _ = jax.lax.scan(step, h0, None, length=T)
        return jnp.concatenate([h_r, h_i], axis=-1)

    def _L2_attn_ref(x, w_in, w_out, b_out, ln_w):
        import jax, jax.numpy as jnp
        import numpy as np
        HEADS = 4
        DIM_HEAD = 32
        EPS = 1e-05
        H, W, C = x.shape
        N = H * W
        qkv = jnp.einsum('hwc,oc->hwo', x, w_in).reshape(N, 3, HEADS, DIM_HEAD)
        q, k, v = (qkv[:, 0], qkv[:, 1], qkv[:, 2])
        q = jax.nn.softmax(q, axis=-1) / np.sqrt(DIM_HEAD)
        k = jax.nn.softmax(k, axis=0)
        v = v / N
        context = jnp.einsum('nhd,nhe->hde', k, v)
        out = jnp.einsum('hde,nhd->nhe', context, q)
        out = out.reshape(H, W, HEADS * DIM_HEAD)
        out = jnp.einsum('hwd,cd->hwc', out, w_out) + b_out
        mean = out.mean(axis=-1, keepdims=True)
        var = out.var(axis=-1, keepdims=True)
        out = (out - mean) / jnp.sqrt(var + EPS) * ln_w
        return out

    def _L2_ffn_ref(x, router_w, router_b, expert_w, expert_b):
        import jax, jax.numpy as jnp
        import numpy as np
        B, N, D, C, E, K = (8, 4096, 64, 64, 8, 2)
        router_probs = jax.nn.softmax(x @ router_w + router_b, axis=-1)
        top_p, top_i = jax.lax.top_k(router_probs, K)
        top_p = top_p / jnp.sum(top_p, axis=-1, keepdims=True)
        expert_out = jnp.einsum('bnd,edc->bnec', x, expert_w) + expert_b
        gathered = jnp.take_along_axis(expert_out, top_i[..., None], axis=2)
        return jnp.einsum('bnk,bnkc->bnc', top_p, gathered)

    def _L3_attn_ref(Z, v_matrix, q_matrix):
        import jax, jax.numpy as jnp
        import numpy as np
        B, N, D = (8, 1024, 64)
        N_LAYER, N_HEAD = (4, 8)
        PARAMS_STD = 0.05

        def _attention(V, Q, Z):
            n = Z.shape[1]
            Attn = jnp.einsum('bni,ij,bmj->bnm', Z, Q, Z)
            values = jnp.einsum('ij,bnj->bni', V, Z)
            return jnp.einsum('bnm,bmi->bni', Attn, values) / n
        n_layer, n_head = (v_matrix.shape[0], v_matrix.shape[1])
        for i in range(n_layer):
            Zi = Z
            residues = jnp.zeros_like(Zi)
            for j in range(n_head):
                Vij = v_matrix[i, j, 0]
                Qij = q_matrix[i, j, 0]
                residues = residues + _attention(Vij, Qij, Zi)
            Z = Zi + residues / n_head
        return Z

    def _L3_ffn_ref(x, sigma, phi, M_u, M_phi_plus, M_phi_minus, log_weights, gumbel):
        import jax, jax.numpy as jnp
        import numpy as np
        PADDED_SL = 4096
        TEMPERATURE = 1.0
        SIGMA_POW = 0.25

        def _stu_conv(phi, u, n):
            b, sl, d = u.shape
            sgn = jnp.where(jnp.arange(sl) % 2 == 0, 1.0, -1.0).astype(u.dtype)
            sgn3 = sgn[None, :, None]
            Vf = jnp.fft.rfft(phi, n=n, axis=0)
            Uf_p = jnp.fft.rfft(u, n=n, axis=1)
            Uf_m = jnp.fft.rfft(u * sgn3, n=n, axis=1)
            U_plus = jnp.fft.irfft(Vf[None, :, :, None] * Uf_p[:, :, None, :], n=n, axis=1)[:, :sl]
            U_minus = jnp.fft.irfft(Vf[None, :, :, None] * Uf_m[:, :, None, :], n=n, axis=1)[:, :sl]
            U_minus = U_minus * sgn[None, :, None, None]
            return (U_plus, U_minus)

        def _compute_spectral(u, sigma, phi, Mpp, Mpm):
            U_plus, U_minus = _stu_conv(phi, u, PADDED_SL)
            s = sigma ** SIGMA_POW
            out = jnp.einsum('btkd,k,kde->bte', U_plus, s, Mpp)
            out = out + jnp.einsum('btkd,k,kde->bte', U_minus, s, Mpm)
            return out

        def _compute_ar_u(Mu, u):
            sl = u.shape[1]
            out = jnp.zeros(u.shape[:2] + (Mu.shape[-1],), dtype=u.dtype)
            for i in range(Mu.shape[0]):
                ui = jnp.pad(u, ((0, 0), (i, 0), (0, 0)))[:, :sl]
                out = out + jnp.einsum('btd,de->bte', ui, Mu[i])
            return out

        def _stu(u, sigma, phi, Mu, Mpp, Mpm):
            return _compute_spectral(u, sigma, phi, Mpp, Mpm) + _compute_ar_u(Mu, u)
        T = x.shape[1]
        outs = []
        for i, frac in enumerate((1, 2, 4, 8)):
            xi = x[:, :T // frac]
            si = _stu(xi, sigma, phi, M_u[i], M_phi_plus[i], M_phi_minus[i])
            si = jnp.pad(si, ((0, 0), (0, T - si.shape[1]), (0, 0)))
            outs.append(si)
        y_soft = jax.nn.softmax((log_weights + gumbel) / TEMPERATURE)
        y_hard = jax.nn.one_hot(jnp.argmax(y_soft), 4, dtype=y_soft.dtype)
        weights = y_hard - jax.lax.stop_gradient(y_soft) + y_soft
        stacked = jnp.stack(outs, axis=-1)
        return jnp.sum(stacked * weights, axis=-1)

    def _gn(v, G=32, eps=1e-05):
        B_, H_, W_, C_ = v.shape
        g = v.reshape(B_, H_, W_, G, C_ // G)
        m = jnp.mean(g, axis=(1, 2, 4), keepdims=True)
        s = jnp.var(g, axis=(1, 2, 4), keepdims=True)
        return ((g - m) / jnp.sqrt(s + eps)).reshape(v.shape)

    def _ln_c(v, eps=1e-06):
        m = jnp.mean(v, axis=-1, keepdims=True)
        s = jnp.var(v, axis=-1, keepdims=True)
        return (v - m) / jnp.sqrt(s + eps)

    def _ln_t(v, eps=1e-05):
        m = jnp.mean(v, axis=-1, keepdims=True)
        s = jnp.var(v, axis=-1, keepdims=True)
        return (v - m) / jnp.sqrt(s + eps)

    def _to_tokens(v):
        B_, H_, W_, C_ = v.shape
        return v.reshape(B_, H_ * W_, C_)

    def _from_tokens(t, like):
        return t.reshape(like.shape)
    x = x + _L0_conv_ref(_gn(x), L0_conv_w_in, L0_conv_conv_w, L0_conv_conv_b, L0_conv_x_proj_w, L0_conv_dt_w, L0_conv_dt_b, L0_conv_A_logs, L0_conv_Ds, L0_conv_ln_w, L0_conv_ln_b, L0_conv_w_out)
    x = x + _L1_conv_ref(_gn(x), L1_conv_Wf, L1_conv_bf, L1_conv_Wi, L1_conv_bi, L1_conv_Wd, L1_conv_bd, L1_conv_A_real, L1_conv_A_imag, L1_conv_B_real, L1_conv_B_imag)
    t = _to_tokens(x)
    t = t + _L2_attn_ref(_ln_t(t), L2_attn_w_in, L2_attn_w_out, L2_attn_b_out, L2_attn_ln_w)
    t = t + _L2_ffn_ref(_ln_t(t), L2_ffn_router_w, L2_ffn_router_b, L2_ffn_expert_w, L2_ffn_expert_b)
    t = t + _L3_attn_ref(_ln_t(t), L3_attn_v_matrix, L3_attn_q_matrix)
    t = t + _L3_ffn_ref(_ln_t(t), L3_ffn_sigma, L3_ffn_phi, L3_ffn_M_u, L3_ffn_M_phi_plus, L3_ffn_M_phi_minus, L3_ffn_log_weights, L3_ffn_gumbel)
    x = _from_tokens(t, x)
    return x

_drawn_inputs = setup_inputs


def setup_inputs(seed=0):
    import zlib

    import numpy as np

    out = dict(_drawn_inputs(seed))
    spreads = {'L0_conv_conv_b': (0.0, 0.1),
     'L0_conv_Ds': (1.0, 0.6),
     'L0_conv_ln_w': (1.0, 0.567),
     'L0_conv_ln_b': (0.0, 1.207),
     'L1_conv_bf': (0.0, 2.0),
     'L1_conv_bi': (0.0, 2.0),
     'L1_conv_bd': (0.0, 1.695),
     'L2_attn_b_out': (0.0, 0.1),
     'L2_attn_ln_w': (1.0, 0.2),
     'L2_ffn_router_b': (0.0, 0.1),
     'L2_ffn_expert_b': (0.0, 0.1),
     'L3_ffn_log_weights': (1.0, 0.2)}
    factors = {'L0_conv_conv_w': 3.232,
     'L0_conv_x_proj_w': 45.715,
     'L0_conv_dt_w': 64.0,
     'L0_conv_dt_b': 56.109,
     'L0_conv_A_logs': 200.0,
     'L1_conv_Wf': 8.0,
     'L1_conv_Wi': 5.547,
     'L1_conv_Wd': 2.956,
     'L1_conv_A_imag': 3.431,
     'L1_conv_B_real': 2.758,
     'L1_conv_B_imag': 2.842,
     'L2_attn_w_in': 8.0,
     'L2_attn_w_out': 8.0,
     'L1_conv_A_real': 3.057}
    for name, (base, spread) in spreads.items():
        noise = np.random.default_rng([zlib.crc32(name.encode()), seed]).standard_normal(out[name].shape)
        drawn = base * np.exp(spread * noise) if base else spread * noise
        out[name] = jnp.asarray(drawn.astype(out[name].dtype))
    for name, factor in factors.items():
        out[name] = (out[name] * factor).astype(out[name].dtype)
    return out
```

```python
from contextlib import ExitStack

import numpy as np

import concourse.bass as bass
from concourse import mybir

F32 = mybir.dt.float32
F32R = mybir.dt.float32r
ALU = mybir.AluOpType
ACT = mybir.ActivationFunctionType
AX = mybir.AxisListType
ADD, SUB, MUL, MAX, MIN = ALU.add, ALU.subtract, ALU.mult, ALU.max, ALU.min

P = 128
B, H, W, C = 2, 32, 32, 64
L = H * W
HALF = L // 2
DI, NS, RANK = 128, 16, 8
DIRS = (1, 2, 3, 0)
ND = len(DIRS)
GROUPS = DI // (P // NS)
UNITS = ND * B * GROUPS
PER = B * GROUPS
C2 = C // 2
KK = 49
T2 = 16
HEADS, DH = 4, 32
QKV = 3 * HEADS * DH
TILES = 8
UN = TILES * B
E = 8
LAYERS, LH = 4, 8
KF = 16
TAPS = 3
TOE = 2 * HALF + 1
SPANS = ((0, 64), (64, 128), (128, 256), (256, 512))

LOG_RATE_MAX, STEP_MIN = 69.0, 1e-28

_o = 0
CONST = {}
for _name, _n in (("ident", P), ("red", 4 * 32), ("pair", P), ("mean", P),
                  ("heads", P), ("images", P), ("split", P), ("merge", 4 * P), ("rank", E)):
    CONST[_name] = (_o, _o + _n)
    _o += _n
NCONST = _o
V_CONVB, V_D, V_LNW, V_LNB, V_BF, V_BI, V_BD, NVEC = 0, 1, 5, 6, 7, 9, 11, 13
R_BOUT, R_LNW, R_RB, R_LW, R_GU, NROW = 0, 64, 128, 136, 140, 144

STEPS = {
    "scalar": ("pick_exp", "k_exp", "q_exp", "k_tok_ready", "q_t_ready", "r_exp", "g_t_ready",
              "w_out_ready", "filters_out"),
    "vector": ("x2_ready", "pick_logits", "picked", "k_max", "q_shifted", "q_ready", "ctx_ready",
              "mix_ready", "attn_done", "r_shifted", "gates_ready", "moe_done", "is_zero", "lin_done"),
    "tensor": ("l0_done", "l1_done", "k_done", "k_turned", "ctx_done", "q_turned", "mix_done",
              "attn_out", "router_done", "g_turned", "bias_done", "gram_done", "w_turned", "lin_out",
              "ar_done"),
}


def wait(engine, sem, value):
    if isinstance(value, int) and value <= 0:
        return
    engine.wait_ge(sem, value)


def program(nc, x_cm, consts, vec, rows, sel_c, w_in, conv_w, w_dt, w_bc, par, w_out, w_gate, ab, dft,
            w_qv, w_k, w_attn, w_router, w_expert, b_expert, v_t, q_t, phi, sigma, m_phi, m_u, out):
    with ExitStack() as ctx:
        def sb(name, shape, dtype=F32):
            return ctx.enter_context(nc.sbuf_tensor(name, shape, dtype))

        sems = {}

        def sig(name):
            if name not in sems:
                sems[name] = ctx.enter_context(nc.semaphore(name))
            return sems[name]

        steps_made = {engine: 0 for engine in STEPS}

        def step_of(name):
            return next((engine, names.index(name) + 1) for engine, names in STEPS.items() if name in names)

        def reach(name):
            engine, value = step_of(name)
            steps_made[engine] += 1
            assert steps_made[engine] == value, name
            return sig(engine + "_steps")

        def after(name):
            engine, value = step_of(name)
            return sig(engine + "_steps"), value

        ps = ctx.enter_context(nc.psum_tensor("ps", [P, 8, HALF], F32))

        def banks(a, n=2):
            return ps[:, a:a + n, :].rearrange("p a n -> p (a n)")

        cst = sb("cst", [P, NCONST])
        vecs = sb("vecs", [P, NVEC])
        rowb = sb("rowb", [P, NROW])
        eps5 = sb("eps5", [P, 1])
        eps8 = sb("eps8", [P, 1])
        x_res = sb("x_res", [P, L])
        tok = sb("tok", [P, TILES, P])

        def con(name):
            return cst[:, CONST[name][0]:CONST[name][1]]

        ident = con("ident")
        sel = sb("sel", [P, 8, P], F32R)
        stack = sb("stack", [P, B, 2, 2, L], F32R)
        red = con("red").rearrange("p (v m) -> p v m", v=4)
        merge = con("merge").rearrange("p (h r m) -> p h r m", h=2, r=2)
        split = con("split").rearrange("p (r m) -> p r m", r=2)

        AREA = 36 * L + KF
        area = sb("area", [P, AREA])
        cut = [0]

        def take(n):
            a = cut[0]
            cut[0] += n
            assert cut[0] <= AREA, cut
            return area[:, a:a + n]

        xs = take(B * 4 * L).rearrange("p (b k n) -> p b k n", b=B, k=4)
        b_rep = take(B * L).rearrange("p (b n) -> p b n", b=B)
        c_rep = take(B * L).rearrange("p (b n) -> p b n", b=B)
        decay = take(2 * L).rearrange("p (s n) -> p s n", s=2)
        drive = take(4 * L).rearrange("p (s n) -> p s n", s=4)
        state = take(8 * L).rearrange("p (s n) -> p s n", s=8)
        tz, ta, te, tw = take(L), take(L), take(L), take(L)
        ysum = (tz, ta)
        tu = tok[:].rearrange("p j n -> p (j n)")
        high = lambda t: t.bitcast(F32R)
        spec = take(2 * L).rearrange("p (r n) -> p r n", r=4)
        ai2, bi2 = (take(L).rearrange("p (r n) -> p r n", r=2) for _ in range(2))
        w_all = take(ND * 3 * P).rearrange("p (k a m) -> p k a m", k=ND, a=3)
        w_now = take(3 * P).rearrange("p (a m) -> p a m", a=3)
        pads = [t[:, 0:2, :].rearrange("p s n -> p (s n)")[:, 0:34 * 34].rearrange("p (h w) -> p h w", h=34)
                for t in (state, drive)]
        sel_in = drive[:, 2, :]
        w_dt_sb = drive[0:RANK, 3, :].rearrange("p (a k m) -> p a k m", a=2, k=ND)
        w_taps, w_in_sb = (state[:, 2:4, :].rearrange("p s n -> p (s n)")[:, a:a + n]
                           for a, n in ((0, 9 * DI), (9 * DI, 2 * DI)))
        w_taps = w_taps.rearrange("p (t d) -> p t d", t=9)
        convw_b = state[:, 4:6, :].rearrange("p s n -> p (s n)")[:, 0:9 * DI]
        ab_sb = state[0:2 * KK, 4:6, :].rearrange("p s n -> p (s n)")[:, 9 * DI:9 * DI + P].rearrange(
            "p (f m) -> p f m", f=2)
        dft_sb = state[:, 6:8, :]
        cut[0] = 0
        xn1, sp_f, sp_i, sp_r, sp_a, sp_x, sp_d, sp_o, sp_v, sp_m, sp_n, sp_s = (take(L) for _ in range(12))
        cut[0] = 0
        toep = take(KF * TOE).rearrange("p (k n) -> p k n", k=KF)
        w_seg = take(KF * 512).rearrange("p (k s g e) -> p k s g e", k=KF, s=2, g=4)
        later = cut[0]
        m_in = take(4 * L).rearrange("p (i s n) -> p i s n", i=2, s=2)
        ln_c, ln_q, xn, xn_t = take(L), take(L), take(L), take(L)
        tail = cut[0]
        cut[0] = KF * TOE
        qv = take(4 * L).rearrange("p (u n) -> p u n", u=UN)
        q_e = take(2 * L)
        q_t_sb = take(2 * L)
        cut[0] = tail
        k_e = take(2 * L)
        w_qv_sb = take(2 * 256)
        w_k_sb = take(2 * P)
        w_attn_sb = take(C)
        ctx_m = take(P)
        mix_m = take(C)
        k_tok = m_in[:, 0].rearrange("p s n -> p (s n)")
        cut[0] = tail
        w_exp_sb = take(2 * 512)
        w_rt_sb = take(2 * E)
        b_exp_sb = take(UN * C)
        prod = take(2 * 512).rearrange("p (a n) -> p a n", a=2)
        gates = take(6 * P)
        cut[0] = tail
        v_sb = take(LAYERS * 512).rearrange("p (l n) -> p l n", l=LAYERS)
        q_sb = take(2 * LH * P).rearrange("p (a h m) -> p a h m", a=2, h=LH)
        t_sb = ln_q[:, 0:512]
        g_sb, is_sb, u_sb, wt_sb = (ln_q[:, 512 + P * a:512 + P * (a + 1)] for a in range(4))
        cut[0] = later
        w_work = take(2 * 8 * P).rearrange("p (a g b e) -> p a g b e", a=2, g=8, b=B)
        eo = take(2 * L).rearrange("p (s t n) -> p s t n", s=2, t=2)
        assert cut[0] <= later + 4 * L
        cut[0] = tail
        u_t = take(2 * (HALF + 1)).rearrange("p (t n) -> p t n", t=2)
        ar_in = take(2 * TAPS * P).rearrange("p (i n) -> p i n", i=2)
        w_ar = take(4 * TAPS * P).rearrange("p (g a m) -> p g a m", g=4, a=TAPS)
        fin = ln_c

        z_gate = sb("z_gate", [P, B, L])
        w_gate_sb = sb("w_gate_sb", [P, 3, 2, 64])
        par_sb = sb("par_sb", [P, ND, 17])
        par_now = sb("par_now", [P, 16])
        bias_now = sb("bias_now", [P, 1])
        w_out_sb = sb("w_out_sb", [P, C])
        small = sb("small", [P, 256])
        phi_sb = tok[0:2 * KF, 0:5, :].rearrange("p j n -> p (j n)")
        sig_sb = sb("sig_sb", [2 * KF, 4])
        phi_dram = nc.dram_tensor("phi_scaled", [2 * KF, 640], F32)


        def chainer(engine, sem):
            count = [0]

            def link(ins, hold=True):
                count[0] += 1
                ins.then_inc(sem, 1)
                if hold:
                    engine.wait_ge(sem, count[0])
            return link

        HEAD = 8

        def scan_loop(engine, slot):
            for s in range(HEAD):
                slot(0, s)
            with engine.Fori(0, ND - 1) as k:
                for s in range(HEAD, PER):
                    slot(k, s)
                for s in range(HEAD):
                    slot(k + 1, s)
            for s in range(HEAD, PER):
                slot(ND - 1, s)

        def split_slot(k, s):
            b, i = divmod(s, GROUPS)
            return B * k + b, b, i

        def following(k, b):
            return (k, 1) if b == 0 else (k + 1, 0)

        def ends(k, b):
            return isinstance(k, int) and k == ND - 1 and b == B - 1

        POOL_COLS = 160

        def recurrence(engine, link, cols):
            def pairs(t):
                return t.rearrange("p (r n) -> p r n", r=2)[:, :, cols]

            width = cols.stop - cols.start
            f, i, r, x, d, o, v, m, n = (pairs(t) for t in (sp_f, sp_i, sp_r, sp_x, sp_d, sp_o, sp_v, sp_m, sp_n))
            s, lg = pairs(sp_s), pairs(sp_a)

            def both(t):
                return t.unsqueeze(1).broadcast_to([P, 2, width])

            def tt(out, a, b, op, hold=True):
                link(engine.tensor_tensor(out, a, b, op), hold)

            engine.wait_ge(sig("gates_out"), 3)
            tt(m, both(spec[:, 2, cols]), x, MUL, False)
            tt(n, bi2[:, :, cols], x[:, ::-1, :], MUL, False)
            tt(v, r, lg, ADD)
            tt(m, m, n, ADD, False)
            engine.wait_ge(sig("gates_out"), 5)
            tt(v, v, i, MUL, False)
            tt(d, both(spec[:, 0, cols]), f, MUL, False)
            tt(o, ai2[:, :, cols], f, MUL)
            tt(v, v, m, MUL)
            for level in range(4):
                tt(m, d, v, MUL, False)
                tt(n, o, v[:, ::-1, :], MUL)
                tt(m, m, n, ADD)
                tt(v, v, m, ADD, level == 3)
                if level < 3:
                    tt(s[:, 0, :], d[:, 0, :], d[:, 1, :], ADD, False)
                    tt(s[:, 1, :], o[:, 0, :], o[:, 1, :], MUL, False)
                    tt(n, d, d, MUL)
                    tt(o, o, both(s[:, 0, :]), MUL, False)
                    tt(d, n, both(s[:, 1, :]), ADD)

        def units(t):
            return t.rearrange("p (u c) -> p u c", u=UN)

        def over(t, n):
            return t.unsqueeze(2).broadcast_to([P, t.shape[1], n])

        tok_flat = tok[:].rearrange("p j n -> p (j n)")
        st_sum, st_var, st_rstd = small[:, 64:80], small[:, 80:96], small[:, 96:112]

        def norm_dve(dve, link, n, src, dst):
            link(dve.tensor_reduce(st_sum, units(src), AX.X, ADD))
            dve.scalar_tensor_tensor(units(ln_c), over(st_sum, C), -1.0 / C, units(src),
                                     MUL, ADD).then_inc(sig("norm_centered"), 1)
            dve.wait_ge(sig("norm_squares"), n)
            dve.tensor_reduce(st_var, units(ln_q), AX.X, ADD).then_inc(sig("norm_var"), 1)
            dve.wait_ge(sig("norm_rstd"), n)
            dve.tensor_tensor(units(dst), units(ln_c), over(st_rstd, C), MUL).then_inc(sig("normed"), 1)

        def norm_act(act, link, n):
            act.wait_ge(sig("norm_centered"), n)
            act.activation(ln_q, ln_c, ACT.Square).then_inc(sig("norm_squares"), 1)
            act.wait_ge(sig("norm_var"), n)
            link(act.activation(st_rstd, st_var, ACT.Ln, bias=eps5[:], scale=1.0 / C))
            act.activation(st_rstd, st_rstd, ACT.Exp, scale=-0.5).then_inc(sig("norm_rstd"), 1)

        block = ctx.enter_context(nc.Block())

        @block.sync
        def _(sp):
            def load(name, dst, src):
                sp.dma_start(dst, src).then_inc(sig(name), 16)

            load("x_in", x_res[:], x_cm)
            load("consts_in", cst[:], consts)
            load("ab_in", ab_sb, ab)
            load("dft_in", dft_sb[0:2 * KK, :, :], dft)
            load("w_in_in", w_in_sb, w_in)
            load("sel_in", sel_in, sel_c)
            load("conv_w_in", convw_b, conv_w.broadcast_to([P, 9 * DI]))
            load("vecs_in", vecs[:], vec)
            load("par_in", par_sb[:], par)
            load("w_dt_in", w_dt_sb, w_dt)
            load("w_bc_in", w_all[:, :, 1:3, :], w_bc)
            load("w_out_in", w_out_sb[:], w_out)
            load("w_gate_in", w_gate_sb[:], w_gate)
            load("phi_in", phi_sb, phi)
            load("sigma_in", sig_sb[:, 0:1], sigma)
            load("rows_in", rowb[:], rows.broadcast_to([P, NROW]))

            sp.wait_ge(sig("phi_scaled"), 1)
            sp.dma_start(phi_dram.ap(), phi_sb).then_inc(sig("phi_out"), 16)

            def restack(n, b):
                for what, (ready, parts) in enumerate((("delta_split", (ta, te)), ("u_split", (tu, tw)))):
                    wait(sp, sig(ready), n + 1)
                    if what == 0:
                        wait(sp, sig("units_spread"), GROUPS * (n - 1))
                    for part, src in enumerate(parts):
                        for half in range(2):
                            sp.dma_start(stack[64 * part:64 * part + 64, b, what, half, :].bitcast(F32),
                                         src[64 * half:64 * half + 64]).then_inc(sig("stacked"), 16)

            for n in range(B * ND):
                restack(n, n % B)
            sp.wait_ge(*after("x2_ready"))
            sp.wait_ge(sig("phi_out"), 16)
            for odd, cols in ((0, HALF), (1, HALF + 1)):
                src = bass.AP(phi_dram, 640 * odd + 1 - odd, [[1, P], [2 * 640, KF], [1, cols]])
                sp.dma_start(toep[:, :, odd * HALF:odd * HALF + cols], src).then_inc(sig("toep_in"), 16)
            load("w_qv_in", w_qv_sb, w_qv)
            load("w_k_in", w_k_sb, w_k)
            load("w_attn_in", w_attn_sb, w_attn)
            sp.wait_ge(*after("attn_done"))
            load("w_exp_in", w_exp_sb, w_expert)
            load("w_rt_in", w_rt_sb, w_router)
            load("b_exp_in", b_exp_sb, b_expert)
            for i in range(4):
                if i >= 2:
                    sp.wait_ge(sig("m_added"), i - 1)
                sp.dma_start(m_in[:, i % 2], m_phi[:, i]).then_inc(sig(f"m_in_{i % 2}"), 16)
            sp.wait_ge(*after("moe_done"))
            load("v_in", v_sb, v_t)
            for l in range(LAYERS):
                if l >= 2:
                    sp.wait_ge(sig("s_done"), l - 1)
                sp.dma_start(q_sb[:, l % 2], q_t[:, l]).then_inc(sig(f"q_in_{l % 2}"), 16)
            sp.wait_ge(*after("lin_done"))
            for i in range(4):
                if i >= 2:
                    sp.wait_ge(sig("ar_added"), i - 1)
                sp.dma_start(ar_in[:, i % 2], m_u[:, i]).then_inc(sig(f"ar_in_{i % 2}"), 16)
            sp.wait_ge(sig("w_work_zero"), 1)

            def mixing(k, a):
                for b in range(B):
                    r = slice(64 * b, 64 * b + 64)
                    sp.dma_start(w_work[r, a, :, b, :],
                                 w_seg[r, k].rearrange("p s g e -> p (s g) e")).then_inc(sig(f"w_work_in_{a}"), 16)

            for k in range(KF):
                wait(sp, sig("mixed"), 2 * (k - 1))
                mixing(k, k % 2)
            for h in range(2):
                sp.wait_ge(sig("out_ready"), h + 1)
                sp.dma_start(out[:, h * HALF:(h + 1) * HALF], fin[:, h * HALF:(h + 1) * HALF]).then_inc(sig("stored"), 16)
            sp.wait_ge(sig("stored"), 32)

        @block.gpsimd
        def _(pool):
            link = chainer(pool, sig("pool_step"))
            for pad in pads:
                pool.memset(pad, 0.0).then_inc(sig("pad_zero"), 1)
            pool.memset(eps8[:], 1e-8)
            pool.memset(eps5[:], 1e-5).then_inc(sig("eps_set"), 1)
            pool.wait_ge(sig("w_in_in"), 16)
            pool.wait_ge(sig("conv_w_in"), 16)
            pool.tensor_tensor(w_taps, w_in_sb[:, 0:DI].unsqueeze(1).broadcast_to([P, 9, DI]),
                               convw_b.rearrange("p (t d) -> p t d", t=9), MUL).then_inc(sig("taps_ready"), 1)
            pool.memset(sig_sb[:, 1:2], 0.25).then_inc(sig("quarter"), 1)
            pool.wait_ge(sig("quarter"), 1)
            pool.wait_ge(sig("sigma_in"), 16)
            pool.wait_ge(sig("phi_in"), 16)
            link(pool.tensor_tensor(sig_sb[:, 2:3], sig_sb[:, 0:1], sig_sb[:, 1:2], ALU.pow))
            pool.tensor_scalar(phi_sb, phi_sb, sig_sb[:, 2:3], None, MUL).then_inc(sig("phi_scaled"), 1)
            pool.wait_ge(sig("spec_sq"), 1)
            pool.tensor_tensor(ta[:, 0:HALF], ta[:, 0:HALF], ta[:, HALF:L], ADD).then_inc(sig("mag_sq"), 1)
            pool.wait_ge(sig("scale_logs"), 3)
            pool.tensor_tensor(te[:, 0:HALF], te[:, 0:HALF], te[:, HALF:L], ADD).then_inc(sig("scale_sum"), 1)
            pool.wait_ge(sig("scale_exp"), 1)
            link(pool.tensor_scalar(te[:, 0:HALF], te[:, 0:HALF], 0.95, None, MUL))
            for r in range(2):
                link(pool.tensor_tensor(spec[:, r, :], spec[:, r, :], te[:, 0:HALF], MUL))
            for dst, src in ((ai2, spec[:, 1, :]), (bi2, spec[:, 3, :])):
                pool.tensor_scalar(dst[:, 0, :], src, -1.0, None, MUL)
                pool.tensor_copy(dst[:, 1, :], src).then_inc(sig("spec_ready"), 1)

            def rest(n):
                wait(pool, sig("w_rest"), n + 1)
                pool.tensor_tensor(te, te, tw, ADD).then_inc(sig("rest_ready"), 1)

            def low(n):
                wait(pool, sig("delta_high"), n + 1)
                pool.tensor_tensor(high(te), tz, ta, SUB).then_inc(sig("delta_split"), 1)

            def slot(k, s):
                n, b, i = split_slot(k, s)
                if i == 0:
                    wait(pool, sig("c_ready"), n + 1)
                wait(pool, sig("scanned"), GROUPS * n + i + 1)
                pool.tensor_tensor(state[:, i % 8, :], state[:, i % 8, :], c_rep[:, b, :],
                                   MUL).then_inc(sig("weighed"), 1)
                if i == 5 and not ends(k, b):
                    rest(n + 1)
                if i == 7 and not ends(k, b):
                    low(n + 1)

            rest(0)
            low(0)
            scan_loop(pool, slot)
            recurrence(pool, link, slice(HALF - POOL_COLS, HALF))
            pool.sem_inc(sig("pool_recurred"), 1)
            pool.wait_ge(*after("attn_done"))
            for i in range(4):
                plus, minus = (m_in[:, i % 2, s].rearrange("p (k e) -> p k e", k=KF) for s in range(2))
                pool.wait_ge(sig("m_weighted"), i + 1)
                for s, op in enumerate((ADD, SUB)):
                    link(pool.tensor_tensor(w_seg[:, :, s, 3 - i, :], plus, minus, op), s == 1)
                for s in range(2) if i else ():
                    link(pool.tensor_tensor(w_seg[:, :, s, 3 - i, :], w_seg[:, :, s, 3 - i, :],
                                            w_seg[:, :, s, 4 - i, :], ADD), s == 1)
                pool.sem_inc(sig("m_added"), 1)
            pool.memset(w_work[:, 0], 0.0)
            pool.memset(w_work[:, 1], 0.0).then_inc(sig("w_work_zero"), 1)
            pool.wait_ge(*after("lin_done"))
            pool.memset(u_t[:, :, 0:1], 0.0).then_inc(sig("u_t_zero"), 1)
            for i in range(4):
                pool.wait_ge(sig("ar_weighted"), i + 1)
                new = w_ar[:, 3 - i].rearrange("p a m -> p (a m)")
                if i == 0:
                    pool.tensor_copy(new, ar_in[:, 0, :]).then_inc(sig("ar_added"), 1)
                else:
                    pool.wait_ge(sig("ar_added"), i)
                    pool.tensor_tensor(new, w_ar[:, 4 - i].rearrange("p a m -> p (a m)"), ar_in[:, i % 2, :],
                                       ADD).then_inc(sig("ar_added"), 1)

        @block.scalar
        def _(act):
            link = chainer(act, sig("act_step"))
            act.preload_act_table_set("natural_log_exp_and_others")
            act.wait_ge(sig("eps_set"), 1)
            act.wait_ge(sig("spec_done"), 1)
            act.activation(spec[:, 0:2, :], ps[:, 0:2, :], ACT.Copy)
            act.activation(spec[:, 2:4, :], ps[:, 2:4, :], ACT.Copy, scale=0.1).then_inc(sig("spec_out"), 1)
            act.wait_ge(sig("spec_out"), 1)
            act.activation(ta, spec[:, 0:2, :].rearrange("p r n -> p (r n)"), ACT.Square).then_inc(sig("spec_sq"), 1)
            act.wait_ge(sig("gn_var"), 1)
            link(act.activation(small[:, 4:5], small[:, 3:4], ACT.Ln, bias=eps5[:]))
            act.activation(small[:, 5:6], small[:, 4:5], ACT.Exp, scale=-0.5).then_inc(sig("gn_rstd"), 1)
            act.wait_ge(sig("mag_sq"), 1)
            mag = ta[:, 0:HALF]
            link(act.activation(te[:, 0:HALF], mag, ACT.Ln, bias=eps8[:]))
            link(act.activation(mag, te[:, 0:HALF], ACT.Exp, scale=0.5))
            act.activation(te[:, 0:HALF], mag, ACT.Exp, scale=-1.0).then_inc(sig("scale_logs"), 1)
            act.wait_ge(sig("scale_logs"), 1)
            act.activation(te[:, 0:HALF], te[:, 0:HALF], ACT.Ln, bias=1.0).then_inc(sig("scale_logs"), 1)
            act.activation(te[:, HALF:L], mag, ACT.Ln, bias=eps8[:]).then_inc(sig("scale_logs"), 1)
            act.wait_ge(sig("scale_sum"), 1)
            act.activation(te[:, 0:HALF], te[:, 0:HALF], ACT.Exp, scale=-1.0).then_inc(sig("scale_exp"), 1)
            act.wait_ge(sig("par_min"), 1)
            act.activation(par_sb[:, :, 0:16], par_sb[:, :, 0:16], ACT.Exp).then_inc(sig("par_exp"), 1)
            act.wait_ge(sig("sel_in"), 16)
            act.activation(sel[:].rearrange("p v m -> p (v m)"), sel_in, ACT.Copy).then_inc(sig("sel_ready"), 1)
            act.preload_act_table_set("silu_and_others")
            act.wait_ge(sig("vecs_in"), 16)
            for b in range(B):
                act.wait_ge(sig("conv_done"), b + 1)
                act.activation(xs[:, b, 3, :], banks(2 * b), ACT.Silu,
                               bias=vecs[:, V_CONVB:V_CONVB + 1]).then_inc(sig("xc_ready"), 1)
            for b in range(B):
                act.wait_ge(sig("z_done"), b + 1)
                act.activation(z_gate[:, b, :], banks(4 + 2 * b), ACT.Silu).then_inc(sig("z_ready"), 1)
            act.wait_ge(sig("w_dt_done"), 1)
            act.activation(w_all[:, :, 0, :], ps[:, 0, :].rearrange("p (a m) -> p a m", a=ND),
                           ACT.Copy).then_inc(sig("w_dt_ready"), 1)
            act.preload_act_table_set("natural_log_exp_and_others")

            def set_weights(k):
                act.activation(w_now.unsqueeze(1), w_all[:, bass.ds(k, 1), :, :],
                               ACT.Copy).then_inc(sig("w_now_set"), 1)
                act.activation(bias_now[:].unsqueeze(1), par_sb[:, bass.ds(k, 1), 16:17],
                               ACT.Copy).then_inc(sig("bias_set"), 1)

            def set_rates(k):
                wait(act, sig("decayed"), PER * k)
                act.activation(par_now[:].unsqueeze(1), par_sb[:, bass.ds(k, 1), 0:16],
                               ACT.Copy).then_inc(sig("rates_set"), 1)

            def soft(n, k, b, step):
                if step == "z":
                    wait(act, sig("projected"), 3 * n + 1)
                    wait(act, sig("stacked"), 128 * n)
                    wait(act, sig("bias_set"), k + 1)
                    act.activation(tz, banks(6), ACT.Identity, bias=bias_now[:]).then_inc(sig("tz_ready"), 1)
                    act.activation(ta, banks(6), ACT.Abs, bias=bias_now[:]).then_inc(sig("abs_ready"), 1)
                elif step == "exp":
                    wait(act, sig("abs_ready"), n + 1)
                    act.activation(te, ta, ACT.Exp, scale=-1.0).then_inc(sig("exp_ready"), 1)
                elif step == "one_plus":
                    wait(act, sig("exp_ready"), n + 1)
                    act.activation(tw, te, ACT.Identity, bias=1.0).then_inc(sig("w_ready"), 1)
                elif step == "log":
                    wait(act, sig("w_ready"), n + 1)
                    act.activation(ta, tw, ACT.Ln).then_inc(sig("log_ready"), 1)
                elif step == "rest":
                    wait(act, sig("log_ready"), n + 1)
                    act.activation(tw, tw, ACT.Identity, bias=1.0, scale=-1.0).then_inc(sig("w_rest"), 1)
                elif step == "b":
                    wait(act, sig("projected"), 3 * n + 2)
                    act.activation(b_rep[:, b, :], banks(6), ACT.Copy).then_inc(sig("b_ready"), 1)
                elif step == "delta":
                    wait(act, sig("delta_ready"), n + 1)
                    act.activation(high(ta), tz, ACT.Copy).then_inc(sig("delta_high"), 1)
                elif step == "u":
                    wait(act, sig("u_ready"), n + 1)
                    act.activation(high(tu), tw, ACT.Copy).then_inc(sig("u_high"), 1)
                elif step == "c":
                    wait(act, sig("projected"), 3 * n + 3)
                    act.activation(c_rep[:, b, :], banks(6), ACT.Copy).then_inc(sig("c_ready"), 1)

            soft_at = {2: ["z"], 3: ["exp"], 4: ["one_plus"], 5: ["log"], 6: ["rest", "b"], 8: ["delta"],
                       9: ["u"], 10: ["c"]}

            def slot(k, s):
                n, b, i = split_slot(k, s)
                wait(act, sig("units_spread"), GROUPS * n + i + 1)
                wait(act, sig("scanned"), GROUPS * n + i - 1)
                if s == 0:
                    wait(act, sig("rates_set"), k + 1)
                act.activation(decay[:, i % 2, :], banks(0), ACT.Exp,
                               scale=par_now[:, i:i + 1]).then_inc(sig("decayed"), 1)
                nk, nb = following(k, b)
                for step in soft_at.get(i, []) if not ends(k, b) else []:
                    soft(n + 1, nk, nb, step)
                if i == 4:
                    pk, pb = (k - 1, 1) if b == 0 else (k, 0)
                    if not isinstance(pk, int) or 0 <= pk < ND - 1:
                        wait(act, sig("summed"), 4 * n)
                        act.activation(xs[:, pb, bass.ds(pk, 1), :], banks(4).unsqueeze(1),
                                       ACT.Copy).then_inc(sig("y_free"), 1)
                if s == 12 and not (isinstance(k, int) and k == ND - 1):
                    set_weights(k + 1)
                if s == PER - 1 and not (isinstance(k, int) and k == ND - 1):
                    set_rates(k + 1)

            act.wait_ge(sig("spec_ready"), 2)
            act.wait_ge(sig("w_bc_in"), 16)
            act.wait_ge(sig("w_dt_ready"), 1)
            act.wait_ge(sig("par_neg"), 1)
            act.wait_ge(sig("phi_out"), 16)
            act.sem_inc(sig("y_free"), 1)
            set_weights(0)
            set_rates(0)
            for steps in soft_at.values():
                for step in steps:
                    soft(0, 0, 0, step)
            scan_loop(act, slot)
            squares = (te, tw)
            for b in range(B):
                act.wait_ge(sig("y_centered"), b + 1)
                act.activation(squares[b], ysum[b], ACT.Square).then_inc(sig("y_squares"), 1)
            for b in range(B):
                act.wait_ge(sig("y_var"), b + 1)
                link(act.activation(squares[b], banks(4 + 2 * b), ACT.Ln, bias=eps5[:]))
                act.activation(squares[b], squares[b], ACT.Exp, scale=-0.5).then_inc(sig("y_rstd"), 1)
            for b in range(B):
                act.wait_ge(sig("y_normed"), b + 1)
                act.activation(ysum[b], ysum[b], ACT.Identity, bias=vecs[:, V_LNB:V_LNB + 1],
                               scale=vecs[:, V_LNW:V_LNW + 1]).then_inc(sig("y_affine"), 1)
            act.wait_ge(sig("gn_var"), 2)
            link(act.activation(small[:, 4:5], small[:, 3:4], ACT.Ln, bias=eps5[:]))
            act.activation(small[:, 5:6], small[:, 4:5], ACT.Exp, scale=-0.5).then_inc(sig("gn_rstd"), 1)

            def pairs(t):
                return t.rearrange("p (r n) -> p r n", r=2)

            act.wait_ge(sig("gates_done"), 1)
            for r in range(2):
                bias = vecs[:, V_BD + r:V_BD + r + 1]
                act.activation(pairs(sp_r)[:, r, :], ps[:, 4 + r, :], ACT.Relu, bias=bias)
                link(act.activation(pairs(sp_a)[:, r, :], ps[:, 4 + r, :], ACT.Abs, bias=bias))
            link(act.activation(sp_a, sp_a, ACT.Exp, scale=-1.0))
            act.activation(sp_a, sp_a, ACT.Ln, bias=1.0).then_inc(sig("gates_out"), 1)
            act.wait_ge(sig("gates_done"), 2)
            act.activation(sp_x, banks(6), ACT.Copy).then_inc(sig("gates_out"), 2)
            act.preload_act_table_set("sigmoid_and_others")
            for g, (dst, col) in enumerate(((sp_f, None), (sp_i, V_BI))):
                act.wait_ge(sig("gates_done"), 3 + g)
                for r in range(2):
                    bias = small[:, 26 + r:27 + r] if col is None else vecs[:, col + r:col + r + 1]
                    ins = act.activation(pairs(dst)[:, r, :], ps[:, 2 * g + r, :], ACT.Sigmoid, bias=bias)
                ins.then_inc(sig("gates_out"), 1)
            act.preload_act_table_set("natural_log_exp_and_others")

            def to_tokens(n, dst, first=2):
                act.wait_ge(sig("turned"), n)
                act.activation(dst, banks(first), ACT.Copy).then_inc(sig("turned_out"), 1)

            to_tokens(1, tok_flat)
            act.wait_ge(*after("pick_logits"))
            act.activation(small[:, 40:44], small[:, 36:40], ACT.Exp, bias=small[:, 45:46]).then_inc(reach("pick_exp"), 1)
            norm_act(act, link, 1)
            to_tokens(2, xn_t, 0)
            act.wait_ge(*after("k_max"))
            act.activation(k_e, ps[:, 4:8, :].rearrange("p a n -> p (a n)"), ACT.Exp, bias=small[:, 129:130],
                           accum_out=small[:, 130:131]).then_inc(reach("k_exp"), 1)
            for r in range(2):
                act.wait_ge(sig("qv_done"), r + 1)
                act.activation(qv[:, 8 * r:8 * r + 8, :].rearrange("p u n -> p (u n)"),
                               ps[:, 0:4, :].rearrange("p a n -> p (a n)"), ACT.Copy).then_inc(sig("qv_out"), 1)
            act.wait_ge(*after("q_shifted"))
            act.activation(q_e, q_e, ACT.Exp).then_inc(reach("q_exp"), 1)
            act.wait_ge(*after("k_turned"))
            act.activation(k_tok, ps[:, 4:8, :].rearrange("p a n -> p (a n)"), ACT.Copy).then_inc(reach("k_tok_ready"), 1)
            act.wait_ge(*after("q_turned"))
            act.activation(q_t_sb, ps[:, 0:4, :].rearrange("p a n -> p (a n)"), ACT.Copy).then_inc(reach("q_t_ready"), 1)
            norm_act(act, link, 2)
            norm_act(act, link, 3)
            to_tokens(3, xn_t, 0)
            act.wait_ge(*after("r_shifted"))
            act.activation(gates[:, 0:P], gates[:, 0:P], ACT.Exp).then_inc(reach("r_exp"), 1)
            for i in range(4):
                act.wait_ge(sig(f"m_in_{i % 2}"), 16 * (i // 2 + 1))
                act.wait_ge(*after("picked"))
                act.activation(m_in[:, i % 2], m_in[:, i % 2], ACT.Copy,
                               scale=small[:, 56 + i:57 + i]).then_inc(sig("m_weighted"), 1)
            act.wait_ge(*after("g_turned"))
            act.activation(gates[:, 5 * P:6 * P], ps[:, 3, 0:P], ACT.Copy).then_inc(reach("g_t_ready"), 1)
            norm_act(act, link, 4)
            to_tokens(4, xn_t, 0)
            for l in range(LAYERS):
                act.wait_ge(sig("t_done"), l + 1)
                act.activation(t_sb, ps[:, 3, :], ACT.Copy).then_inc(sig("t_out"), 1)
                act.wait_ge(sig("wt_done"), l + 1)
                act.activation(wt_sb, ps[:, 6, 0:P], ACT.Copy).then_inc(sig("wt_out"), 1)
            act.wait_ge(*after("w_turned"))
            act.activation(wt_sb, ps[:, 6, 0:P], ACT.Copy).then_inc(reach("w_out_ready"), 1)
            norm_act(act, link, 5)
            act.wait_ge(sig("turned"), 5)
            act.wait_ge(*after("lin_done"))
            for t in range(2):
                act.activation(u_t[:, t, 1:HALF + 1].rearrange("p (q n) -> p q n", q=4),
                               banks(2).rearrange("p (q t n) -> p t q n", q=4, t=2)[:, t, :, ::-1],
                               ACT.Copy).then_inc(sig("u_t_ready"), 1)
            for i in range(4):
                act.wait_ge(sig(f"ar_in_{i % 2}"), 16 * (i // 2 + 1))
                act.activation(ar_in[:, i % 2], ar_in[:, i % 2], ACT.Copy,
                               scale=small[:, 56 + i:57 + i]).then_inc(sig("ar_weighted"), 1)

            def filtered(h, s):
                wait(act, sig("convolved"), h + 1)
                if not isinstance(h, int) or h >= 2:
                    wait(act, sig("mixed"), h - 1)
                act.activation(eo[:, s].rearrange("p t n -> p (t n)"), banks(2 + 2 * s),
                               ACT.Copy).then_inc(sig("filtered"), 1)

            filtered(0, 0)
            filtered(1, 1)
            with act.Fori(1, KF) as k:
                filtered(2 * k, 0)
                filtered(2 * k + 1, 1)
            act.wait_ge(sig("mixed"), 2 * KF)
            act.wait_ge(*after("ar_done"))
            act.activation(eo[:, 0].rearrange("p t (g n) -> p (t g) n", g=4)[:, :, ::-1],
                           banks(0).rearrange("p (g n) -> p g n", n=P), ACT.Copy).then_inc(reach("filters_out"), 1)

        @block.vector
        def _(dve):
            link = chainer(dve, sig("dve_step"))
            pair_ps = ps[:, 7, 0:2]

            def group_norm(x, n):
                for h in range(2):
                    link(dve.bn_stats(small[:, 8 + 6 * h:14 + 6 * h], x[:, h * HALF:(h + 1) * HALF]))
                dve.bn_aggr(small[:, 0:2], small[:, 8:20]).then_inc(sig("gn_stats"), 1)
                dve.wait_ge(sig("gn_pair"), n)
                link(dve.tensor_copy(small[:, 20:22], pair_ps))
                link(dve.tensor_tensor(small[:, 2:3], small[:, 0:1], small[:, 20:21], SUB))
                dve.scalar_tensor_tensor(small[:, 3:4], small[:, 2:3], small[:, 2:3], small[:, 21:22],
                                         MUL, ADD).then_inc(sig("gn_var"), 1)
                dve.wait_ge(sig("gn_rstd"), n)

            dve.wait_ge(sig("x_in"), 16)
            group_norm(x_res, 1)
            dve.wait_ge(sig("pad_zero"), 2)
            for b in range(B):
                r = slice(64 * b, 64 * b + 64)
                dve.tensor_scalar(pads[b][r, 1:33, 1:33], x_res[r].rearrange("p (h w) -> p h w", h=H),
                                  small[r, 20:21], small[r, 5:6], SUB, MUL).then_inc(sig("gn_out"), 1)
            dve.wait_ge(sig("par_in"), 16)
            rates = par_sb[:, :, 0:16]
            dve.tensor_scalar(rates, rates, LOG_RATE_MAX, None, MIN).then_inc(sig("par_min"), 1)
            dve.wait_ge(sig("par_exp"), 1)
            dve.tensor_scalar(rates, rates, -1.0, None, MUL).then_inc(sig("par_neg"), 1)
            dve.wait_ge(sig("vecs_in"), 16)
            link(dve.tensor_reduce(small[:, 24:25], vecs[:, V_D:V_D + 4], AX.X, ADD))
            link(dve.tensor_scalar(small[:, 26:28], vecs[:, V_BF:V_BF + 2], 2.0, None, ADD))
            for b in range(B):
                dve.wait_ge(sig("xc_ready"), b + 1)
                nat = xs[:, b, 3, :]
                turned_grid = nat.rearrange("p (h w) -> p w h", h=H)
                dve.tensor_copy(xs[:, b, 0, :].rearrange("p (w h) -> p w h", w=W), turned_grid)
                dve.tensor_copy(xs[:, b, 1, :], nat[:, ::-1])
                dve.tensor_copy(xs[:, b, 2, :].rearrange("p (w h) -> p w h", w=W),
                                turned_grid[:, ::-1, ::-1]).then_inc(sig("orders_ready"), 1)

            def finish_soft(n, k, b, step):
                if step == 0:
                    wait(dve, sig("tz_ready"), n + 1)
                    wait(dve, sig("log_ready"), n + 1)
                    dve.scalar_tensor_tensor(tz, tz, STEP_MIN, ta, MAX, ADD).then_inc(sig("soft_sum"), 1)
                elif step == 1:
                    wait(dve, sig("soft_sum"), n + 1)
                    wait(dve, sig("rest_ready"), n + 1)
                    dve.tensor_tensor(tz, tz, te, ADD).then_inc(sig("delta_ready"), 1)
                elif step == 2:
                    wait(dve, sig("delta_ready"), n + 1)
                    dve.tensor_tensor(tw.unsqueeze(1), tz.unsqueeze(1),
                                      xs[:, b, bass.ds(k, 1), :], MUL).then_inc(sig("u_ready"), 1)
                elif step == 3:
                    wait(dve, sig("u_high"), n + 1)
                    dve.tensor_tensor(high(tw), tw, tu, SUB).then_inc(sig("u_split"), 1)

            def drive_unit(n, b, i):
                if i == 0:
                    wait(dve, sig("b_ready"), n + 1)
                wait(dve, sig("units_spread"), GROUPS * n + i + 1)
                wait(dve, sig("scanned"), GROUPS * n + i - 3)
                dve.tensor_tensor(drive[:, i % 4, :], banks(2), b_rep[:, b, :], MUL).then_inc(sig("driven"), 1)

            def slot(k, s):
                n, b, i = split_slot(k, s)
                nk, nb = following(k, b)
                if i < GROUPS - 1:
                    drive_unit(n, b, i + 1)
                elif not ends(k, b):
                    drive_unit(n + 1, nb, 0)
                wait(dve, sig("decayed"), GROUPS * n + i + 1)
                wait(dve, sig("driven"), GROUPS * n + i + 1)
                wait(dve, sig("summed"), 4 * n + i // 4 - 1)
                dve.tensor_tensor_scan(state[:, i % 8, :], decay[:, i % 2, :], drive[:, i % 4, :], 0.0,
                                       MUL, ADD).then_inc(sig("scanned"), 1)
                if i in (6, 7, 8, 10) and not ends(k, b):
                    finish_soft(n + 1, nk, nb, {6: 0, 7: 1, 8: 2, 10: 3}[i])
                if isinstance(k, int) and k == ND - 1 and s == GROUPS + 5:
                    outputs(0)

            def outputs(b):
                dve.wait_ge(sig("summed"), 4 * (B * (ND - 1) + b + 1))
                dve.scalar_tensor_tensor(ysum[b], xs[:, b, 3, :], small[:, 24:25], banks(4),
                                         MUL, ADD).then_inc(sig("y_last"), 1)

            dve.wait_ge(sig("orders_ready"), 2)
            for step in range(4):
                finish_soft(0, 0, 0, step)
            drive_unit(0, 0, 0)
            scan_loop(dve, slot)
            outputs(1)
            dve.wait_ge(sig("y_free"), B * (ND - 1) + 1)
            for b in range(B):
                y = ysum[b]
                grid = y.rearrange("p (h w) -> p h w", h=H)
                turned = xs[:, b, 0, :].rearrange("p (w h) -> p h w", w=W)
                turned_back = xs[:, b, 2, :].rearrange("p (w h) -> p h w", w=W)[:, ::-1, ::-1]
                link(dve.tensor_tensor(grid, grid, turned, ADD))
                link(dve.tensor_tensor(y, y, xs[:, b, 1, ::-1], ADD))
                dve.tensor_tensor(grid, grid, turned_back, ADD).then_inc(sig("y_ready"), 1)
            for b in range(B):
                dve.wait_ge(sig("y_mean"), b + 1)
                dve.tensor_tensor(ysum[b], ysum[b], banks(2 * b), SUB).then_inc(sig("y_centered"), 1)
            for b in range(B):
                dve.wait_ge(sig("y_rstd"), b + 1)
                dve.tensor_tensor(ysum[b], ysum[b], (te, tw)[b], MUL).then_inc(sig("y_normed"), 1)
            for b in range(B):
                dve.wait_ge(sig("y_affine"), b + 1)
                dve.tensor_tensor(ysum[b], ysum[b], z_gate[:, b, :], MUL).then_inc(sig("y_gated"), 1)
            dve.wait_ge(*after("l0_done"))
            link(dve.tensor_tensor(x_res[:], x_res[:], banks(0), ADD))
            group_norm(x_res, 2)
            dve.tensor_scalar(xn1, x_res[:], small[:, 20:21], small[:, 5:6], SUB, MUL).then_inc(sig("gn_out"), 1)
            recurrence(dve, link, slice(0, HALF - POOL_COLS))
            dve.sem_inc(sig("dve_recurred"), 1)
            dve.wait_ge(*after("l1_done"))
            quarters = lambda t: t.rearrange("p (q n t) -> p q n t", q=4, t=2)
            dve.tensor_tensor(quarters(xn_t)[:, :, ::-1, :], quarters(x_res[:]), quarters(banks(0)),
                              ADD).then_inc(reach("x2_ready"), 1)
            logits, peak, probs, hard = small[:, 36:40], small[:, 44:45], small[:, 40:44], small[:, 48:52]
            rank = con("rank")
            link(dve.tensor_tensor(logits, rowb[:, R_LW:R_LW + 4], rowb[:, R_GU:R_GU + 4], ADD))
            link(dve.tensor_reduce(peak, logits, AX.X, MAX))
            dve.tensor_scalar(small[:, 45:46], peak, -1.0, None, MUL).then_inc(reach("pick_logits"), 1)
            dve.wait_ge(*after("pick_exp"))
            link(dve.tensor_reduce(peak, probs, AX.X, ADD))
            link(dve.reciprocal(peak, peak))
            link(dve.tensor_scalar(probs, probs, peak, None, MUL))
            link(dve.tensor_reduce(peak, probs, AX.X, MAX))
            link(dve.tensor_scalar(hard, probs, peak, None, ALU.is_equal))
            link(dve.tensor_tensor(hard, hard, rank[:, 4:8], MUL))
            link(dve.tensor_reduce(peak, hard, AX.X, MAX))
            link(dve.tensor_scalar(hard, hard, peak, None, ALU.is_equal))
            link(dve.tensor_tensor(hard, hard, probs, SUB))
            dve.tensor_tensor(small[:, 56:60], hard, probs, ADD).then_inc(reach("picked"), 1)
            dve.wait_ge(sig("turned_out"), 1)
            norm_dve(dve, link, 1, tok_flat, xn)
            dve.wait_ge(*after("k_done"))
            link(dve.tensor_reduce(small[:, 128:129], ps[:, 4:8, :].rearrange("p a n -> p (a n)"), AX.X, MAX))
            dve.tensor_scalar(small[:, 129:130], small[:, 128:129], -1.0, None, MUL).then_inc(reach("k_max"), 1)
            q_heads = qv[:, :, 0:P].rearrange("p u (h d) -> p u h d", h=HEADS)
            q_st = small[:, 136:200]
            q_rep = q_st.rearrange("p (u h) -> p u h", u=UN).unsqueeze(3).broadcast_to([P, UN, HEADS, DH])
            q_sh = q_e.rearrange("p (u h d) -> p u h d", u=UN, h=HEADS)
            dve.wait_ge(sig("qv_out"), 2)
            link(dve.tensor_reduce(q_st.rearrange("p (u h) -> p u h", u=UN), q_heads, AX.X, MAX))
            dve.tensor_tensor(q_sh, q_heads, q_rep, SUB).then_inc(reach("q_shifted"), 1)
            dve.wait_ge(*after("q_exp"))
            link(dve.tensor_reduce(q_st, q_e.rearrange("p (g d) -> p g d", d=DH), AX.X, ADD))
            link(dve.reciprocal(q_st, q_st))
            dve.tensor_tensor(q_sh, q_sh, q_rep, MUL).then_inc(reach("q_ready"), 1)
            dve.wait_ge(*after("k_exp"))
            link(dve.tensor_scalar(small[:, 131:132], small[:, 130:131], float(B * L * np.sqrt(DH)), None, MUL))
            link(dve.reciprocal(small[:, 131:132], small[:, 131:132]))
            dve.wait_ge(*after("ctx_done"))
            dve.tensor_tensor(ctx_m, ps[:, 4, 0:P], con("heads"), MUL).then_inc(reach("ctx_ready"), 1)
            dve.wait_ge(*after("mix_done"))
            dve.tensor_scalar(mix_m, ps[:, 5, 0:C], small[:, 131:132], None, MUL).then_inc(reach("mix_ready"), 1)

            def row(col, n=C):
                return rowb[:, col:col + n].unsqueeze(1).broadcast_to([P, UN, n])

            dve.wait_ge(*after("attn_out"))
            link(dve.tensor_tensor(units(xn), units(banks(6)), row(R_BOUT), ADD))
            norm_dve(dve, link, 2, xn, xn_t)
            dve.wait_ge(sig("normed"), 2)
            link(dve.tensor_tensor(units(xn_t), units(xn_t), row(R_LNW), MUL))
            link(dve.tensor_tensor(tok_flat, tok_flat, xn_t, ADD))
            dve.sem_inc(reach("attn_done"), 1)
            norm_dve(dve, link, 3, tok_flat, xn)
            lg, g2, g3 = (gates[:, P * a:P * (a + 1)].rearrange("p (u e) -> p u e", u=UN) for a in range(3))
            top, top2, den = gates[:, 3 * P:3 * P + UN], gates[:, 3 * P + UN:3 * P + 2 * UN], gates[:, 4 * P:4 * P + UN]
            ranks = rank.unsqueeze(1).broadcast_to([P, UN, E])
            dve.wait_ge(*after("router_done"))
            link(dve.tensor_tensor(lg, ps[:, 2, 0:P].rearrange("p (u e) -> p u e", u=UN), row(R_RB, E), ADD))
            link(dve.tensor_reduce(top, lg, AX.X, MAX))
            dve.tensor_tensor(lg, lg, over(top, E), SUB).then_inc(reach("r_shifted"), 1)
            dve.wait_ge(*after("r_exp"))

            def first_best(dst, src, best):
                link(dve.tensor_reduce(best, src, AX.X, MAX))
                link(dve.tensor_tensor(dst, src, over(best, E), ALU.is_equal))
                link(dve.tensor_tensor(dst, dst, ranks, MUL))
                link(dve.tensor_reduce(den, dst, AX.X, MAX))
                link(dve.tensor_tensor(dst, dst, over(den, E), ALU.is_equal))

            first_best(g2, lg, top)
            link(dve.scalar_tensor_tensor(lg, g2, -2.0, lg, MUL, ADD))
            first_best(g3, lg, top2)
            link(dve.tensor_tensor(g3, g3, over(top2, E), MUL))
            link(dve.tensor_tensor(g2, g2, g3, ADD))
            link(dve.tensor_scalar(den, top2, 1.0, None, ADD))
            link(dve.reciprocal(den, den))
            dve.tensor_tensor(g2, g2, over(den, E), MUL).then_inc(reach("gates_ready"), 1)
            dve.wait_ge(*after("gates_ready"))
            for u in range(UN):
                dve.wait_ge(sig("expert_done"), u + 1)
                dve.tensor_tensor(prod[:, u % 2, :].rearrange("p (e c) -> p e c", e=E),
                                  ps[:, 4 + u % 4, :].rearrange("p (e c) -> p e c", e=E),
                                  g2[:, u, :].unsqueeze(2).broadcast_to([P, E, C]), MUL).then_inc(sig("weighted"), 1)
                if u >= 1:
                    dve.wait_ge(sig("weighted"), u)
                    dve.tensor_reduce(units(xn)[:, u - 1, :], prod[:, (u - 1) % 2, :].rearrange(
                        "p (e c) -> p c e", e=E), AX.X, ADD).then_inc(sig("expert_sum"), 1)
                    dve.wait_ge(sig("expert_sum"), u)
            dve.wait_ge(sig("weighted"), UN)
            link(dve.tensor_reduce(units(xn)[:, UN - 1, :], prod[:, (UN - 1) % 2, :].rearrange(
                "p (e c) -> p c e", e=E), AX.X, ADD))
            link(dve.tensor_tensor(tok_flat, tok_flat, xn, ADD))
            dve.wait_ge(*after("bias_done"))
            link(dve.tensor_tensor(tok_flat, tok_flat, banks(0), ADD))
            dve.sem_inc(reach("moe_done"), 1)
            norm_dve(dve, link, 4, tok_flat, xn)
            dve.memset(is_sb, 0.0).then_inc(reach("is_zero"), 1)
            dve.wait_ge(*after("gram_done"))
            dve.tensor_tensor(g_sb, ps[:, 2, 0:P], con("images"), MUL).then_inc(sig("g_ready"), 1)
            dve.wait_ge(*after("is_zero"))
            for l in range(LAYERS):
                dve.wait_ge(sig("s_done"), l + 1)
                wait(dve, sig("wt_done"), l)
                for b in range(B):
                    r = slice(64 * b, 64 * b + 64)
                    ins = dve.scalar_tensor_tensor(is_sb[r, r], ps[r, 4, 0:C], 1.0 / (L * LH), con("ident")[r, r],
                                                   MUL, ADD)
                ins.then_inc(sig("is_ready"), 1)
                if l < LAYERS - 1:
                    dve.wait_ge(sig("gs_done"), l + 1)
                    dve.tensor_copy(u_sb, ps[:, 5, 0:P]).then_inc(sig("gs_out"), 1)
                    dve.wait_ge(sig("g_done"), l + 1)
                    dve.tensor_copy(g_sb, ps[:, 7, 0:P]).then_inc(sig("g_ready"), 1)
            dve.wait_ge(*after("lin_out"))
            link(dve.tensor_tensor(tok_flat, tok_flat, banks(0), ADD))
            dve.sem_inc(reach("lin_done"), 1)
            norm_dve(dve, link, 5, tok_flat, xn)
            for h in range(2):
                dve.wait_ge(sig("out_turned"), h + 1)
                dve.tensor_tensor(fin[:, h * HALF:(h + 1) * HALF], tok_flat[:, h * HALF:(h + 1) * HALF],
                                  ps[:, 2 + h, :], ADD).then_inc(sig("out_ready"), 1)

        @block.tensor
        def _(pe):
            def half(ap, h):
                return ap[:, h * HALF:(h + 1) * HALF]

            pe.wait_ge(sig("ab_in"), 16)
            pe.wait_ge(sig("dft_in"), 16)
            for f in range(2):
                for r in range(2):
                    for h in range(2):
                        mm = pe.matmul(ps[64 * h:64 * h + 64, 2 * f + r, :], ab_sb[:, f, :],
                                       dft_sb[0:2 * KK, r, h * HALF:(h + 1) * HALF], start=True, stop=True)
            mm.then_inc(sig("spec_done"), 1)

            def pair_mean(n):
                pe.wait_ge(sig("gn_stats"), n)
                pe.matmul(ps[:, 7, 0:2], con("pair"), small[:, 0:2], start=True, stop=True).then_inc(sig("gn_pair"), 1)

            pe.wait_ge(sig("consts_in"), 16)
            pair_mean(1)
            pe.wait_ge(sig("spec_out"), 1)
            pe.wait_ge(sig("taps_ready"), 1)
            for b in range(B):
                pe.wait_ge(sig("gn_out"), b + 1)
                for h in range(2):
                    for t in range(9):
                        dy, dx = divmod(t, 3)
                        mm = pe.matmul(ps[:, 2 * b + h, :], w_taps[:, t, :],
                                       pads[b][:, 16 * h + dy:16 * h + dy + 16, dx:dx + W],
                                       start=(t == 0), stop=(t == 8))
                mm.then_inc(sig("conv_done"), 1)
            for b in range(B):
                for h in range(2):
                    mm = pe.matmul(ps[:, 4 + 2 * b + h, :], w_in_sb[:, DI:2 * DI],
                                   pads[b][:, 16 * h + 1:16 * h + 17, 1:1 + W], start=True, stop=True)
                mm.then_inc(sig("z_done"), 1)
            pe.wait_ge(sig("w_dt_in"), 16)
            pe.wait_ge(sig("xc_ready"), 1)
            for k in range(ND):
                mm = pe.matmul(ps[:, 0, k * P:(k + 1) * P], w_dt_sb[:, 0, k, :], w_dt_sb[:, 1, k, :],
                               start=True, stop=True)
            mm.then_inc(sig("w_dt_done"), 1)

            def project(n, k, b, what, h):
                if h == 0:
                    if what == 0:
                        wait(pe, sig("w_now_set"), k + 1)
                        wait(pe, sig("c_ready"), n)
                    else:
                        wait(pe, sig(("abs_ready", "b_ready")[what - 1]), n + 1)
                mm = pe.matmul(ps[:, 6 + h, :].unsqueeze(1), w_now[:, what, :],
                               xs[:, b, bass.ds(k, 1), h * HALF:(h + 1) * HALF], start=True, stop=True)
                if h == 1:
                    mm.then_inc(sig("projected"), 1)

            def spread(n, b, i):
                u = GROUPS * n + i
                if i == 0:
                    wait(pe, sig("stacked"), 128 * (n + 1))
                wait(pe, sig("decayed"), u)
                wait(pe, sig("driven"), u)
                j, v = i % 4, i // 4
                for q in range(4):
                    mm = pe.matmul(ps[:, q, :], sel[:, 4 * (j % 2) + v, :],
                                   stack[:, b, q // 2, j // 2, (q % 2) * HALF:(q % 2 + 1) * HALF],
                                   start=True, stop=True)
                mm.then_inc(sig("units_spread"), 1)

            def sum_states(n, b, v, h, free=None):
                if h == 0:
                    wait(pe, sig("weighed"), GROUPS * n + 4 * v + 4)
                    if v == 0:
                        free()
                for j in range(4):
                    mm = pe.matmul(ps[32 * j:32 * j + 32, 4 + h, :], red[:, v, :],
                                   state[:, (4 * v + j) % 8, h * HALF:(h + 1) * HALF],
                                   start=(v == 0), stop=(v == 3))
                if h == 1:
                    mm.then_inc(sig("summed"), 1)

            def slot(k, s):
                n, b, i = split_slot(k, s)
                spread(n, b, i)
                nk, nb = following(k, b)

                def free():
                    if ends(k, b):
                        pe.wait_ge(sig("y_last"), 1)
                    else:
                        wait(pe, sig("y_free"), n + 1)
                if i in (0, 1, 4, 5, 8, 9) and not ends(k, b):
                    project(n + 1, nk, nb, i // 4, i % 4)
                elif i in (2, 3) and not (isinstance(k, int) and s < GROUPS and k == 0):
                    sum_states(n - 1, 1 - b, 3, i - 2)
                elif i in (6, 7, 10, 11, 14, 15):
                    sum_states(n, b, (i - 6) // 4, (i - 6) % 4, free)

            for what in range(3):
                if what == 0:
                    pe.wait_ge(sig("orders_ready"), 1)
                    pe.wait_ge(sig("z_ready"), 2)
                for h in range(2):
                    project(0, 0, 0, what, h)
            pe.wait_ge(sig("orders_ready"), 2)
            scan_loop(pe, slot)
            for h in range(2):
                sum_states(B * ND - 1, 1, 3, h)
            for b in range(B):
                pe.wait_ge(sig("y_ready"), b + 1)
                for h in range(2):
                    mm = pe.matmul(ps[:, 2 * b + h, :], con("mean"), half(ysum[b], h), start=True, stop=True)
                mm.then_inc(sig("y_mean"), 1)
            for b in range(B):
                pe.wait_ge(sig("y_squares"), b + 1)
                for h in range(2):
                    mm = pe.matmul(ps[:, 4 + 2 * b + h, :], con("mean"), half((te, tw)[b], h), start=True, stop=True)
                mm.then_inc(sig("y_var"), 1)
            pe.wait_ge(sig("w_out_in"), 16)
            for b in range(B):
                pe.wait_ge(sig("y_gated"), b + 1)
                for h in range(2):
                    mm = pe.matmul(ps[64 * b:64 * b + 64, h, :], w_out_sb[:], half(ysum[b], h), start=True, stop=True)
            mm.then_inc(reach("l0_done"), 1)
            pair_mean(2)
            pe.wait_ge(sig("gn_out"), 3)
            pe.wait_ge(sig("w_gate_in"), 16)
            for bank, lhs in ((4, w_gate_sb[:, 2]), (6, split), (0, w_gate_sb[:, 0]), (2, w_gate_sb[:, 1])):
                for r in range(2):
                    for h in range(2):
                        mm = pe.matmul(ps[64 * h:64 * h + 64, bank + r, :], lhs[:, r, :], half(xn1, h),
                                       start=True, stop=True)
                mm.then_inc(sig("gates_done"), 1)
            pe.wait_ge(sig("dve_recurred"), 1)
            pe.wait_ge(sig("pool_recurred"), 1)
            for h in range(2):
                for r in range(2):
                    mm = pe.matmul(ps[:, h, :], merge[:, h, r, :], sp_v[:, r * HALF:(r + 1) * HALF],
                                   start=(r == 0), stop=(r == 1))
            mm.then_inc(reach("l1_done"), 1)

            def turn(src, bank):
                for j in range(TILES):
                    mm = pe.transpose(ps[:, bank + j // 4, (j % 4) * P:(j % 4 + 1) * P], src(j), ident)
                mm.then_inc(sig("turned"), 1)

            def tile(t):
                return lambda j: t[:, j * P:(j + 1) * P]

            pe.wait_ge(*after("x2_ready"))
            turn(lambda j: xn_t.rearrange("p (q n t) -> p q t n", q=4, t=2)[:, j // 2, j % 2, :], 2)
            pe.wait_ge(sig("normed"), 1)
            turn(tile(xn), 0)
            pe.wait_ge(sig("turned_out"), 2)
            pe.wait_ge(sig("w_k_in"), 16)
            for b in range(B):
                for h in range(2):
                    mm = pe.matmul(ps[:, 4 + 2 * b + h, :], w_k_sb[:, b * P:(b + 1) * P], half(xn_t, h),
                                   start=True, stop=True)
            mm.then_inc(reach("k_done"), 1)
            pe.wait_ge(sig("w_qv_in"), 16)
            for j in range(TILES):
                if j == 4:
                    pe.wait_ge(sig("qv_out"), 1)
                mm = pe.matmul(ps[:, j % 4, :], tile(xn_t)(j), w_qv_sb, start=True, stop=True)
                if j % 4 == 3:
                    mm.then_inc(sig("qv_done"), 1)
            pe.wait_ge(*after("k_exp"))
            for u in range(UN):
                mm = pe.transpose(ps[:, 4 + u // 4, (u % 4) * P:(u % 4 + 1) * P], tile(k_e)(u), ident)
            mm.then_inc(reach("k_turned"), 1)
            pe.wait_ge(*after("k_tok_ready"))
            for u in range(UN):
                j, b = divmod(u, B)
                mm = pe.matmul(ps[:, 4, 0:P], qv[:, u, P:2 * P], tile(k_tok)(b * TILES + j),
                               start=(u == 0), stop=(u == UN - 1))
            mm.then_inc(reach("ctx_done"), 1)
            pe.wait_ge(*after("q_ready"))
            for u in range(UN):
                mm = pe.transpose(ps[:, u // 4, (u % 4) * P:(u % 4 + 1) * P], tile(q_e)(u), ident)
            mm.then_inc(reach("q_turned"), 1)
            pe.wait_ge(sig("w_attn_in"), 16)
            pe.wait_ge(*after("ctx_ready"))
            pe.matmul(ps[:, 5, 0:C], ctx_m, w_attn_sb, start=True, stop=True).then_inc(reach("mix_done"), 1)
            pe.wait_ge(*after("mix_ready"))
            pe.wait_ge(*after("q_t_ready"))
            for u in range(UN):
                mm = pe.matmul(ps[:, 6 + u // 8, (u % 8) * C:(u % 8 + 1) * C], tile(q_t_sb)(u), mix_m,
                               start=True, stop=True)
            mm.then_inc(reach("attn_out"), 1)
            pe.wait_ge(sig("normed"), 3)
            turn(tile(xn), 0)
            pe.wait_ge(sig("turned_out"), 3)
            pe.wait_ge(sig("w_rt_in"), 16)
            for j in range(TILES):
                mm = pe.matmul(ps[:, 2, j * 16:(j + 1) * 16], tile(xn_t)(j), w_rt_sb, start=True, stop=True)
            mm.then_inc(reach("router_done"), 1)
            pe.wait_ge(sig("w_exp_in"), 16)
            for u in range(UN):
                if u == 4:
                    pe.wait_ge(*after("gates_ready"))
                    pe.transpose(ps[:, 3, 0:P], gates[:, P:2 * P], ident).then_inc(reach("g_turned"), 1)
                if u >= 4:
                    pe.wait_ge(sig("weighted"), u - 3)
                pe.matmul(ps[:, 4 + u % 4, :], tile(xn_t)(u // B), w_exp_sb[:, (u % B) * 512:(u % B + 1) * 512],
                          start=True, stop=True).then_inc(sig("expert_done"), 1)
            pe.wait_ge(*after("g_t_ready"))
            pe.wait_ge(sig("b_exp_in"), 16)
            for h in range(2):
                mm = pe.matmul(ps[:, h, :], gates[:, 5 * P:6 * P], half(b_exp_sb, h), start=True, stop=True)
            mm.then_inc(reach("bias_done"), 1)
            pe.wait_ge(sig("normed"), 4)
            for j in range(TILES):
                mm = pe.matmul(ps[:, 2, 0:P], tile(xn)(j), tile(xn)(j), start=(j == 0), stop=(j == TILES - 1))
            mm.then_inc(reach("gram_done"), 1)
            turn(tile(xn), 0)
            pe.wait_ge(sig("v_in"), 16)
            for l in range(LAYERS):
                pe.wait_ge(sig("g_ready"), l + 1)
                pe.matmul(ps[:, 3, :], g_sb, v_sb[:, l, :], start=True, stop=True).then_inc(sig("t_done"), 1)
                pe.wait_ge(sig("t_out"), l + 1)
                pe.wait_ge(sig(f"q_in_{l % 2}"), 16 * (l // 2 + 1))
                for h in range(LH):
                    mm = pe.matmul(ps[:, 4, 0:C], q_sb[:, l % 2, h, :], t_sb[:, h * C:(h + 1) * C],
                                   start=(h == 0), stop=(h == LH - 1))
                mm.then_inc(sig("s_done"), 1)
                pe.wait_ge(sig("is_ready"), l + 1)
                if l < LAYERS - 1:
                    pe.matmul(ps[:, 5, 0:P], g_sb, is_sb, start=True, stop=True).then_inc(sig("gs_done"), 1)
                wait(pe, sig("wt_out"), l)
                pe.matmul(ps[:, 6, 0:P], is_sb, wt_sb if l else ident, start=True, stop=True).then_inc(sig("wt_done"), 1)
                if l < LAYERS - 1:
                    pe.wait_ge(sig("gs_out"), l + 1)
                    pe.matmul(ps[:, 7, 0:P], is_sb, u_sb, start=True, stop=True).then_inc(sig("g_done"), 1)
            pe.wait_ge(sig("wt_out"), LAYERS)
            pe.transpose(ps[:, 6, 0:P], wt_sb, ident).then_inc(reach("w_turned"), 1)
            pe.wait_ge(*after("w_out_ready"))
            pe.wait_ge(sig("turned_out"), 4)
            for j in range(TILES):
                mm = pe.matmul(ps[:, j // 4, (j % 4) * P:(j % 4 + 1) * P], tile(xn_t)(j), wt_sb, start=True, stop=True)
            mm.then_inc(reach("lin_out"), 1)
            pe.wait_ge(sig("normed"), 5)
            turn(tile(xn), 2)
            pe.wait_ge(sig("u_t_ready"), 2)
            pe.wait_ge(sig("toep_in"), 32)

            def convolve(k, s):
                h = 2 * k + s
                if not isinstance(h, int) or h >= 2:
                    wait(pe, sig("filtered"), h - 1)
                for t in range(2):
                    for q in range(4):
                        n = HALF - P * q
                        first = 0 if s == 0 else HALF + t
                        mm = pe.matmul(ps[:, 2 + 2 * s + t, P * q:HALF].unsqueeze(1), tile(xn)(2 * q + (t ^ s)),
                                       toep[:, bass.ds(k, 1), first:first + n], start=(q == 0), stop=(q == 3))
                mm.then_inc(sig("convolved"), 1)

            def mix(pair, a, s, first=False):
                wait(pe, sig("filtered"), 4 * pair + 2 * a + s + 1)
                if s == 0:
                    wait(pe, sig(f"w_work_in_{a}"), 32 * (pair + 1))
                for g in (3, 2, 1, 0):
                    lo, hi = SPANS[g]
                    bank = lo // 256
                    mm = pe.matmul(ps[:, bank, :].rearrange("p (t n) -> p t n", t=2)[:, :, lo % 256:lo % 256 + hi - lo],
                                   w_work[:, a, 4 * s + g].rearrange("p b e -> p (b e)"), eo[:, s, :, lo:hi],
                                   start=first and g >= 2, stop=False, skip_group_check=True)
                mm.then_inc(sig("mixed"), 1)

            convolve(0, 0)
            convolve(0, 1)
            mix(0, 0, 0, True)
            convolve(1, 0)
            mix(0, 0, 1)
            convolve(1, 1)
            mix(0, 1, 0)
            with pe.Fori(1, KF // 2) as p:
                convolve(2 * p, 0)
                mix(p - 1, 1, 1)
                convolve(2 * p, 1)
                mix(p, 0, 0)
                convolve(2 * p + 1, 0)
                mix(p, 0, 1)
                convolve(2 * p + 1, 1)
                mix(p, 1, 0)
            mix(KF // 2 - 1, 1, 1)
            pe.wait_ge(sig("ar_added"), 4)
            pe.wait_ge(sig("u_t_zero"), 1)
            for g in (3, 2, 1, 0):
                lo, hi = SPANS[g]
                bank, at = lo // 256, lo % 256
                out_v = ps[:, bank, :].rearrange("p (t n) -> p t n", t=2)[:, :, at:at + hi - lo]
                for a, dst, src in ((0, out_v, u_t[:, :, 1 + lo:1 + hi]), (2, out_v, u_t[:, :, lo:hi]),
                                    (1, out_v[:, 0, :], u_t[:, 1, lo:hi]), (1, out_v[:, 1, :], u_t[:, 0, 1 + lo:1 + hi])):
                    mm = pe.matmul(dst, w_ar[:, g, a, :], src, start=False, stop=(g % 2 == 0 and a == 1),
                                   skip_group_check=True)
            mm.then_inc(reach("ar_done"), 1)
            pe.wait_ge(*after("filters_out"))
            flat = eo[:, 0].rearrange("p t n -> p (t n)").rearrange("p (h t q n) -> p h t q n", h=2, t=2, q=2)
            for q in range(4):
                for t in range(2):
                    j = 2 * q + t
                    mm = pe.transpose(ps[:, 2 + j // 4, (j % 4) * P:(j % 4 + 1) * P], flat[:, q // 2, t, q % 2, :], ident)
                if q % 2 == 1:
                    mm.then_inc(sig("out_turned"), 1)


def constants():
    c = np.zeros((P, NCONST), np.float32)

    def part(name):
        return c[:, CONST[name][0]:CONST[name][1]]

    p = np.arange(P)
    part("ident")[:] = np.eye(P)
    for v in range(4):
        part("red")[:, v * 32:(v + 1) * 32] = (p[:, None] // NS + 8 * v) == np.arange(32)[None, :]
    sel = np.stack([(p[:, None] % 64 - 8 * v) == p[None, :] // NS for v in range(8)], 1).astype(np.float32)
    part("pair")[:] = 0.5 * (p[:, None] // 2 == p[None, :] // 2)
    part("mean")[:] = 1.0 / P
    part("heads")[:] = p[:, None] // DH == p[None, :] // DH
    part("images")[:] = p[:, None] // C == p[None, :] // C
    part("rank")[:] = np.arange(E, 0, -1)
    q = np.arange(64)
    for r in range(2):
        part("split")[:, r * 64:(r + 1) * 64] = p[:, None] == (q // 32 * 64 + r * 32 + q % 32)[None, :]
        for h in range(2):
            at = part("merge")[64 * h:64 * h + 64, (2 * h + r) * P:(2 * h + r + 1) * P]
            at[:] = (q // 32 * 64 + r * 32 + q % 32)[:, None] == p[None, :]
    k, t = np.arange(KK), np.arange(L)
    at = (12 + k[:, None] // 7) * (t[None, :] // W) + (12 + k[:, None] % 7) * (t[None, :] % W)
    cos, sin = np.cos(2 * np.pi * at / 32), np.sin(2 * np.pi * at / 32)
    dft = np.stack([np.concatenate([cos, sin]), np.concatenate([-sin, cos])], 1)
    return c, sel.reshape(P, 8 * P), dft.astype(np.float32)


def layouts(i):
    two = lambda a: np.concatenate([a, a], 0)
    d = list(DIRS)

    def blocks(a):
        out = np.zeros((B, C) + a.shape[1:-1] + (B, a.shape[-1]), np.float32)
        for b in range(B):
            out[b, ..., b, :] = a
        return out.reshape((P,) + a.shape[1:-1] + (B * a.shape[-1],))

    w_qkv = i["L2_attn_w_in"].T
    consts, sel, dft = constants()
    vec = np.zeros((P, NVEC), np.float32)
    vec[:, V_CONVB] = i["L0_conv_conv_b"]
    vec[:, V_D:V_D + 4] = i["L0_conv_Ds"].reshape(4, DI).T
    vec[:, V_LNW] = i["L0_conv_ln_w"]
    vec[:, V_LNB] = i["L0_conv_ln_b"]
    for col, name in ((V_BF, "bf"), (V_BI, "bi"), (V_BD, "bd")):
        vec[:, col:col + 2] = np.tile(i["L1_conv_" + name].reshape(2, C2).T, (4, 1))
    rows = np.concatenate([i["L2_attn_b_out"], i["L2_attn_ln_w"], i["L2_ffn_router_b"],
                           i["L3_ffn_log_weights"], i["L3_ffn_gumbel"]])[None]
    xp = i["L0_conv_x_proj_w"][d]
    w_dt = np.stack([xp[:, :RANK].transpose(1, 0, 2), i["L0_conv_dt_w"][d].transpose(2, 0, 1)], 1)
    bc = xp[:, RANK:].reshape(ND, 2, 1, NS, DI)
    w_bc = np.broadcast_to(bc, (ND, 2, 8, NS, DI)).reshape(ND, 2, P, DI).transpose(3, 0, 1, 2)
    par = np.zeros((P, ND, 17), np.float32)
    rates = i["L0_conv_A_logs"].reshape(4, 4, 4, 8, NS)[d]
    par[:, :, 0:16] = rates.transpose(3, 4, 0, 2, 1).reshape(P, ND, 16)
    par[:, :, 16] = i["L0_conv_dt_b"][d].T
    w_gate = np.zeros((B, C, 3, 2, B, C2), np.float32)
    for g, name in enumerate(("Wf", "Wi", "Wd")):
        for b in range(B):
            w_gate[b, :, g, :, b, :] = i["L1_conv_" + name].reshape(C, 2, C2)
    ab = np.stack([np.concatenate([i[f"L1_conv_{n}_real"].reshape(C2, KK).T,
                                   i[f"L1_conv_{n}_imag"].reshape(C2, KK).T]) for n in "AB"], 1)
    b_expert = np.zeros((UN, E, UN, C), np.float32)
    for u in range(UN):
        b_expert[u, :, u, :] = i["L2_ffn_expert_b"]
    phi = np.zeros((KF, 2, 640), np.float32)
    phi[:, :, 128:] = i["L3_ffn_phi"][:L].reshape(HALF, 2, KF).transpose(2, 1, 0)
    m_phi = np.stack([i["L3_ffn_M_phi_plus"], i["L3_ffn_M_phi_minus"]], 1)
    return {
        "x_cm": i["x"].reshape(B, L, C).transpose(0, 2, 1).reshape(P, L),
        "consts": consts, "vec": vec, "rows": rows, "sel_c": sel,
        "w_in": two(i["L0_conv_w_in"].T),
        "conv_w": i["L0_conv_conv_w"].reshape(DI, 9).T.reshape(1, 9 * DI),
        "w_dt": w_dt, "w_bc": w_bc, "par": par,
        "w_out": i["L0_conv_w_out"].T,
        "w_gate": w_gate.reshape(P, 3, 2, 64), "ab": np.concatenate([ab, ab], 2), "dft": dft,
        "w_qv": blocks(np.concatenate([w_qkv[:, :P], w_qkv[:, 2 * P:]], 1)), "w_k": blocks(w_qkv[:, P:2 * P]),
        "w_attn": i["L2_attn_w_out"].T,
        "w_router": blocks(i["L2_ffn_router_w"]),
        "w_expert": blocks(i["L2_ffn_expert_w"].transpose(1, 0, 2).reshape(C, E * C)),
        "b_expert": b_expert.reshape(P, UN * C),
        "v_t": two(i["L3_attn_v_matrix"][:, :, 0].transpose(3, 0, 1, 2)).reshape(P, LAYERS, LH * C),
        "q_t": blocks(i["L3_attn_q_matrix"][:, :, 0].transpose(3, 0, 1, 2)),
        "phi": phi.reshape(2 * KF, 640), "sigma": np.repeat(i["L3_ffn_sigma"], 2)[:, None],
        "m_phi": two(m_phi.transpose(3, 0, 1, 2, 4).reshape(C, 4, 2, KF * C)),
        "m_u": blocks(i["L3_ffn_M_u"].transpose(2, 0, 1, 3)).reshape(P, 4, TAPS * P),
    }


_OUT = ((P, TILES * P), "float32")


def kernel(**inputs):
    import concourse.bacc as _bacc
    from concourse.bass_utils import run_bass_kernel_spmd as _run

    arrays = {f"in_{k}_dram": np.ascontiguousarray(v) for k, v in
              layouts({k: np.asarray(v) for k, v in inputs.items()}).items()}
    nc = _bacc.Bacc("TRN2", target_bir_lowering=False, num_devices=1)
    args = [nc.dram_tensor(k, a.shape, mybir.dt.from_np(a.dtype), kind="ExternalInput").ap()
            for k, a in arrays.items()]
    out = nc.dram_tensor("out_0_dram", _OUT[0], F32, kind="ExternalOutput").ap()
    program(nc, *args, out)
    got = _run(nc, [arrays], core_ids=[0]).results[0]["out_0_dram"]
    return got[::-1].reshape(P, 4, 2, B, C).transpose(3, 1, 0, 2, 4).reshape(B, H, W, C)
```

```python
from contextlib import ExitStack

import numpy as np

import concourse.bass as bass
from concourse import mybir

F32 = mybir.dt.float32
F32R = mybir.dt.float32r
ALU = mybir.AluOpType
ACT = mybir.ActivationFunctionType
AX = mybir.AxisListType
ADD, SUB, MUL, MAX, MIN = ALU.add, ALU.subtract, ALU.mult, ALU.max, ALU.min

P = 128
B, H, W, C = 2, 32, 32, 64
L = H * W
HALF = L // 2
DI, NS, RANK = 128, 16, 8
DIRS = (1, 2, 3, 0)
ND = len(DIRS)
GROUPS = DI // (P // NS)
UNITS = ND * B * GROUPS
PER = B * GROUPS
C2 = C // 2
KK = 49
T2 = 16
HEADS, DH = 4, 32
QKV = 3 * HEADS * DH
TILES = 8
UN = TILES * B
E = 8
LAYERS, LH = 4, 8
KF = 16
TAPS = 3
TOE = 2 * HALF + 1
SPANS = ((0, 64), (64, 128), (128, 256), (256, 512))

LOG_RATE_MAX, STEP_MIN = 69.0, 1e-28

_o = 0
CONST = {}
for _name, _n in (("ident", P), ("red", 4 * 32), ("pair", P), ("mean", P),
                  ("heads", P), ("split", P), ("merge", 4 * P), ("rank", E), ("sign", 1)):
    CONST[_name] = (_o, _o + _n)
    _o += _n
NCONST = _o
V_CONVB, V_D, V_LNW, V_LNB, V_BF, V_BI, V_BD, NVEC = 0, 1, 5, 6, 7, 9, 11, 13
R_BOUT, R_LNW, R_RB, R_LW, R_GU, NROW = 0, 64, 128, 136, 140, 144

STEPS = {
    "scalar": ("pick_exp", "k_exp", "q_exp", "k_tok_ready", "q_t_ready", "r_exp", "g_t_ready",
              "w_out_ready", "filters_out"),
    "vector": ("pick_logits", "picked", "x2_ready", "k_max", "q_shifted", "q_ready", "ctx_ready",
              "mix_ready", "attn_done", "r_shifted", "gates_ready", "moe_done", "zeroed", "lin_done"),
    "tensor": ("l0_done", "l1_done", "k_done", "k_turned", "ctx_done", "q_turned", "mix_done",
              "attn_out", "router_done", "g_turned", "bias_done", "w_turned", "lin_out",
              "ar_done"),
}


def wait(engine, sem, value):
    if isinstance(value, int) and value <= 0:
        return
    engine.wait_ge(sem, value)


def program(nc, x_cm, consts, vec, rows, sel_c, w_in, conv_w, w_dt, w_bc, par, w_out, w_gate, ab, dft,
            w_qv, w_k, w_attn, w_router, w_expert, b_expert, v_t, q_t, phi, sigma, m_phi, m_u, out):
    with ExitStack() as ctx:
        def sb(name, shape, dtype=F32):
            return ctx.enter_context(nc.sbuf_tensor(name, shape, dtype))

        sems = {}

        def sig(name):
            if name not in sems:
                sems[name] = ctx.enter_context(nc.semaphore(name))
            return sems[name]

        steps_made = {engine: 0 for engine in STEPS}

        def step_of(name):
            return next((engine, names.index(name) + 1) for engine, names in STEPS.items() if name in names)

        def reach(name):
            engine, value = step_of(name)
            steps_made[engine] += 1
            assert steps_made[engine] == value, name
            return sig(engine + "_steps")

        def after(name):
            engine, value = step_of(name)
            return sig(engine + "_steps"), value

        ps = ctx.enter_context(nc.psum_tensor("ps", [P, 8, HALF], F32))

        def banks(a, n=2):
            return ps[:, a:a + n, :].rearrange("p a n -> p (a n)")

        cst = sb("cst", [P, NCONST])
        vecs = sb("vecs", [P, NVEC])
        rowb = sb("rowb", [P, NROW])
        eps5 = sb("eps5", [P, 1])
        eps8 = sb("eps8", [P, 1])
        x_res = sb("x_res", [P, L])
        tok = sb("tok", [P, TILES, P])

        def con(name):
            return cst[:, CONST[name][0]:CONST[name][1]]

        ident = con("ident")
        sel = sb("sel", [P, 8, P], F32R)
        stack = sb("stack", [P, B, 2, 2, L], F32R)
        red = con("red").rearrange("p (v m) -> p v m", v=4)
        merge = con("merge").rearrange("p (h r m) -> p h r m", h=2, r=2)
        split = con("split").rearrange("p (r m) -> p r m", r=2)

        AREA = 36 * L + KF
        area = sb("area", [P, AREA])
        cut = [0]

        def take(n):
            a = cut[0]
            cut[0] += n
            assert cut[0] <= AREA, cut
            return area[:, a:a + n]

        xs = take(B * 4 * L).rearrange("p (b k n) -> p b k n", b=B, k=4)
        b_rep = take(B * L).rearrange("p (b n) -> p b n", b=B)
        c_rep = take(B * L).rearrange("p (b n) -> p b n", b=B)
        decay = take(2 * L).rearrange("p (s n) -> p s n", s=2)
        drive = take(4 * L).rearrange("p (s n) -> p s n", s=4)
        state = take(8 * L).rearrange("p (s n) -> p s n", s=8)
        tz, ta, te, tw = take(L), take(L), take(L), take(L)
        ysum = (tz, ta)
        tu = tok[:].rearrange("p j n -> p (j n)")
        high = lambda t: t.bitcast(F32R)
        spec = take(2 * L).rearrange("p (r n) -> p r n", r=4)
        ai2, bi2 = (take(L).rearrange("p (r n) -> p r n", r=2) for _ in range(2))
        w_all = take(ND * 3 * P).rearrange("p (k a m) -> p k a m", k=ND, a=3)
        w_now = take(3 * P).rearrange("p (a m) -> p a m", a=3)
        pads = [t[:, 0:2, :].rearrange("p s n -> p (s n)")[:, 0:34 * 34].rearrange("p (h w) -> p h w", h=34)
                for t in (state, drive)]
        sel_in = drive[:, 2, :]
        w_dt_sb = drive[0:RANK, 3, :].rearrange("p (a k m) -> p a k m", a=2, k=ND)
        w_taps, w_in_sb = (state[:, 2:4, :].rearrange("p s n -> p (s n)")[:, a:a + n]
                           for a, n in ((0, 9 * DI), (9 * DI, 2 * DI)))
        w_taps = w_taps.rearrange("p (t d) -> p t d", t=9)
        convw_b = state[:, 4:6, :].rearrange("p s n -> p (s n)")[:, 0:9 * DI]
        ab_sb = state[0:2 * KK, 4:6, :].rearrange("p s n -> p (s n)")[:, 9 * DI:9 * DI + P].rearrange(
            "p (f m) -> p f m", f=2)
        dft_sb = state[:, 6:8, :]
        cut[0] = 0
        xn1, sp_f, sp_i, sp_r, sp_a, sp_x, sp_d, sp_o, sp_v, sp_m, sp_n, sp_s = (take(L) for _ in range(12))
        cut[0] = 0
        toep = take(KF * TOE).rearrange("p (k n) -> p k n", k=KF)
        w_seg = take(KF * 256).rearrange("p (k n) -> p k n", k=KF)
        filt = take(4 * L).rearrange("p (a b n) -> p a b n", a=2, b=B)
        later = cut[0]
        m_in = take(4 * L).rearrange("p (i s n) -> p i s n", i=2, s=2)
        ln_c, ln_q, xn, xn_t = take(L), take(L), take(L), take(L)
        tail = cut[0]
        cut[0] = KF * TOE
        qv = take(4 * L).rearrange("p (u n) -> p u n", u=UN)
        q_e = take(2 * L)
        q_t_sb = take(2 * L)
        cut[0] = tail
        k_e = take(2 * L)
        w_qv_sb = take(2 * 256)
        w_k_sb = take(2 * P)
        w_attn_sb = take(C)
        ctx_m = take(P)
        mix_m = take(C)
        k_tok = m_in[:, 0].rearrange("p s n -> p (s n)")
        cut[0] = tail
        w_exp_sb = take(2 * 512)
        w_rt_sb = take(2 * E)
        b_exp_sb = take(UN * C)
        prod = take(2 * 512).rearrange("p (a n) -> p a n", a=2)
        gates = take(6 * P)
        cut[0] = KF * TOE + 4 * L
        v_sb = take(LAYERS * 256).rearrange("p (l n) -> p l n", l=LAYERS)
        q_sb = take(LAYERS * 4 * P).rearrange("p (l h m) -> p l h m", l=LAYERS, h=4)
        g_two = take(2 * P).rearrange("p (b m) -> p b m", b=B)
        t_sb = ln_q[:, 0:512]
        g_sb, is_sb, u_sb, wt_sb = (ln_q[:, 512 + P * a:512 + P * (a + 1)] for a in range(4))
        cut[0] = later
        w_work = take(2 * 256).rearrange("p (a n) -> p a n", a=2)
        ar_in = take(4 * TAPS * P).rearrange("p (i n) -> p i n", i=4)
        w_ar = take(4 * TAPS * P).rearrange("p (g a m) -> p g a m", g=4, a=TAPS)
        y_back = ln_q
        cut[0] = tail
        u_t = take(2 * (HALF + 1)).rearrange("p (t n) -> p t n", t=2)
        fin = ln_c

        z_gate = sb("z_gate", [P, B, L])
        w_gate_sb = sb("w_gate_sb", [P, 3, 2, 64])
        par_sb = sb("par_sb", [P, ND, 17])
        par_now = sb("par_now", [P, 16])
        bias_now = sb("bias_now", [P, 1])
        w_out_sb = sb("w_out_sb", [P, C])
        small = sb("small", [P, 352])
        phi_sb = tok[0:2 * KF, 0:5, :].rearrange("p j n -> p (j n)")
        spare = stack[:].rearrange("p b w h n -> p (b w h n)")
        xn_hl = spare[:, 0:2 * L].rearrange("p (s n) -> p s n", s=2)
        toep_hl = spare[:, 2 * L:2 * L + 4 * TOE].rearrange("p (a s n) -> p a s n", a=2, s=2)
        sig_sb = sb("sig_sb", [2 * KF, 4])
        phi_dram = nc.dram_tensor("phi_scaled", [2 * KF, 640], F32)


        def chainer(engine, sem):
            count = [0]

            def link(ins, hold=True):
                count[0] += 1
                ins.then_inc(sem, 1)
                if hold:
                    engine.wait_ge(sem, count[0])
            return link

        HEAD = 8

        def scan_loop(engine, slot):
            for s in range(HEAD):
                slot(0, s)
            with engine.Fori(0, ND - 1) as k:
                for s in range(HEAD, PER):
                    slot(k, s)
                for s in range(HEAD):
                    slot(k + 1, s)
            for s in range(HEAD, PER):
                slot(ND - 1, s)

        def split_slot(k, s):
            b, i = divmod(s, GROUPS)
            return B * k + b, b, i

        def following(k, b):
            return (k, 1) if b == 0 else (k + 1, 0)

        def ends(k, b):
            return isinstance(k, int) and k == ND - 1 and b == B - 1

        POOL_COLS = 160

        def recurrence(engine, link, cols):
            def pairs(t):
                return t.rearrange("p (r n) -> p r n", r=2)[:, :, cols]

            width = cols.stop - cols.start
            f, i, r, x, d, o, v, m, n = (pairs(t) for t in (sp_f, sp_i, sp_r, sp_x, sp_d, sp_o, sp_v, sp_m, sp_n))
            s, lg = pairs(sp_s), pairs(sp_a)

            def both(t):
                return t.unsqueeze(1).broadcast_to([P, 2, width])

            def tt(out, a, b, op, hold=True):
                link(engine.tensor_tensor(out, a, b, op), hold)

            engine.wait_ge(sig("gates_out"), 3)
            tt(m, both(spec[:, 2, cols]), x, MUL, False)
            tt(n, bi2[:, :, cols], x[:, ::-1, :], MUL, False)
            tt(v, r, lg, ADD)
            tt(m, m, n, ADD, False)
            engine.wait_ge(sig("gates_out"), 5)
            tt(v, v, i, MUL, False)
            tt(d, both(spec[:, 0, cols]), f, MUL, False)
            tt(o, ai2[:, :, cols], f, MUL)
            tt(v, v, m, MUL)
            for level in range(4):
                tt(m, d, v, MUL, False)
                tt(n, o, v[:, ::-1, :], MUL)
                tt(m, m, n, ADD)
                tt(v, v, m, ADD, level == 3)
                if level < 3:
                    tt(s[:, 0, :], d[:, 0, :], d[:, 1, :], ADD, False)
                    tt(s[:, 1, :], o[:, 0, :], o[:, 1, :], MUL, False)
                    tt(n, d, d, MUL)
                    tt(o, o, both(s[:, 0, :]), MUL, False)
                    tt(d, n, both(s[:, 1, :]), ADD)

        def units(t):
            return t.rearrange("p (u c) -> p u c", u=UN)

        def over(t, n):
            return t.unsqueeze(2).broadcast_to([P, t.shape[1], n])

        tok_flat = tok[:].rearrange("p j n -> p (j n)")
        st_sum, st_var, st_rstd, st_dif = (small[:, a:a + UN] for a in (64, 80, 96, 112))
        bn = small[:, 256:352].rearrange("p (u s) -> p u s", u=UN)

        def norm_dve(dve, link, n, src, dst):
            for u in range(UN):
                ins = dve.bn_stats(bn[:, u, :], units(src)[:, u, :])
            link(ins)
            dve.tensor_tensor(st_sum, bn[:, :, 1], bn[:, :, 4], ADD)
            link(dve.tensor_tensor(st_dif, bn[:, :, 1], bn[:, :, 4], SUB), False)
            link(dve.tensor_tensor(st_var, bn[:, :, 2], bn[:, :, 5], ADD))
            link(dve.tensor_tensor(st_dif, st_dif, st_dif, MUL))
            dve.scalar_tensor_tensor(st_var, st_dif, C / 4, st_var, MUL, ADD).then_inc(sig("norm_var"), 1)
            link(dve.scalar_tensor_tensor(units(ln_c), over(st_sum, C), -0.5, units(src), MUL, ADD))
            dve.wait_ge(sig("norm_rstd"), n)
            dve.tensor_tensor(units(dst), units(ln_c), over(st_rstd, C), MUL).then_inc(sig("normed"), 1)

        def norm_act(act, link, n):
            act.wait_ge(sig("norm_var"), n)
            link(act.activation(st_rstd, st_var, ACT.Ln, bias=eps5[:], scale=1.0 / C))
            act.activation(st_rstd, st_rstd, ACT.Exp, scale=-0.5).then_inc(sig("norm_rstd"), 1)

        def filtered(engine, k, a, s):
            wait(engine, sig("convolved"), 2 * k + s + 1)
            if s == 0 and (not isinstance(k, int) or k >= 2):
                engine.wait_ge(sig("mixed"), k - 1)
            b = 0 if engine is nc.scalar else 1
            dst, src = filt[64 * s:64 * s + 64, a, b, :], banks(2 + 2 * s)[64 * b:64 * b + 64]
            if b == 0:
                engine.activation(dst, src, ACT.Copy).then_inc(sig("filtered_0"), 1)
            else:
                engine.tensor_copy(dst, src).then_inc(sig("filtered_1"), 1)

        def filter_loop(engine, split_rows):
            def pair_of(k0, more):
                for a in range(2):
                    for s in range(2):
                        filtered(engine, k0 + a, a, s)
                    if more:
                        split_rows(k0 + 2 + a, a)
            pair_of(0, True)
            with engine.Fori(1, KF // 2 - 1) as pair:
                pair_of(2 * pair, True)
            pair_of(KF - 2, False)

        def copy_g(engine, l, copy, src):
            b = 0 if engine is nc.vector else 1
            engine.wait_ge(sig("g_done"), l + 1)
            own = slice(64 * b, 64 * b + 64)
            extra = () if b == 0 else (ACT.Copy,)
            for row in range(2):
                at = slice(64 * row, 64 * row + 64)
                copy(g_two[at, b, at], src[own, own], *extra)
            copy(g_sb[own, own], src[own, own], *extra).then_inc(sig(f"g_ready_{b}"), 1)

        block = ctx.enter_context(nc.Block())

        @block.sync
        def _(sp):
            def load(name, dst, src):
                sp.dma_start(dst, src).then_inc(sig(name), 16)

            load("x_in", x_res[:], x_cm)
            load("consts_in", cst[:], consts)
            load("ab_in", ab_sb, ab)
            load("dft_in", dft_sb[0:2 * KK, :, :], dft)
            load("w_in_in", w_in_sb, w_in)
            load("sel_in", sel_in, sel_c)
            load("conv_w_in", convw_b, conv_w.broadcast_to([P, 9 * DI]))
            load("vecs_in", vecs[:], vec)
            load("par_in", par_sb[:], par)
            load("w_dt_in", w_dt_sb, w_dt)
            load("w_bc_in", w_all[:, :, 1:3, :], w_bc)
            load("w_out_in", w_out_sb[:], w_out)
            load("w_gate_in", w_gate_sb[:], w_gate)
            load("phi_in", phi_sb, phi)
            load("sigma_in", sig_sb[:, 0:1], sigma)
            load("rows_in", rowb[:], rows.broadcast_to([P, NROW]))

            sp.wait_ge(sig("phi_scaled"), 1)
            sp.dma_start(phi_dram.ap(), phi_sb).then_inc(sig("phi_out"), 16)

            def restack(n, b):
                for what, (ready, parts) in enumerate((("delta_split", (ta, te)), ("u_split", (tu, tw)))):
                    wait(sp, sig(ready), n + 1)
                    if what == 0:
                        wait(sp, sig("steps_spread"), GROUPS * (n - 1))
                    for part, src in enumerate(parts):
                        for half in range(2):
                            sp.dma_start(stack[64 * part:64 * part + 64, b, what, half, :].bitcast(F32),
                                         src[64 * half:64 * half + 64]).then_inc(sig("stacked"), 16)

            for n in range(B * ND):
                restack(n, n % B)
            sp.wait_ge(*after("x2_ready"))
            load("w_qv_in", w_qv_sb, w_qv)
            load("w_k_in", w_k_sb, w_k)
            load("w_attn_in", w_attn_sb, w_attn)
            sp.wait_ge(sig("phi_out"), 16)
            for odd, cols in ((0, HALF), (1, HALF + 1)):
                src = bass.AP(phi_dram, 640 * odd + 1 - odd, [[1, P], [2 * 640, KF], [1, cols]])
                sp.dma_start(toep[:, :, odd * HALF:odd * HALF + cols], src).then_inc(sig("toep_in"), 16)
            sp.wait_ge(*after("attn_done"))
            load("w_exp_in", w_exp_sb, w_expert)
            load("w_rt_in", w_rt_sb, w_router)
            load("b_exp_in", b_exp_sb, b_expert)
            load("v_in", v_sb, v_t)
            load("q_in", q_sb, q_t)
            for i in range(4):
                if i >= 2:
                    sp.wait_ge(sig("m_added"), i - 1)
                sp.dma_start(m_in[:, i % 2], m_phi[:, i]).then_inc(sig(f"m_in_{i % 2}"), 16)
            sp.wait_ge(sig("m_added"), 4)
            load("ar_in", ar_in, m_u)
            for h in range(2):
                sp.wait_ge(sig("out_ready"), h + 1)
                sp.dma_start(out[:, h * HALF:(h + 1) * HALF], fin[:, h * HALF:(h + 1) * HALF]).then_inc(sig("stored"), 16)
            sp.wait_ge(sig("stored"), 32)

        @block.gpsimd
        def _(pool):
            link = chainer(pool, sig("pool_step"))
            for pad in pads:
                pool.memset(pad, 0.0).then_inc(sig("pad_zero"), 1)
            pool.memset(eps8[:], 1e-8)
            pool.memset(eps5[:], 1e-5).then_inc(sig("eps_set"), 1)
            pool.wait_ge(sig("w_in_in"), 16)
            pool.wait_ge(sig("conv_w_in"), 16)
            pool.tensor_tensor(w_taps, w_in_sb[:, 0:DI].unsqueeze(1).broadcast_to([P, 9, DI]),
                               convw_b.rearrange("p (t d) -> p t d", t=9), MUL).then_inc(sig("taps_ready"), 1)
            pool.memset(sig_sb[:, 1:2], 0.25).then_inc(sig("quarter"), 1)
            pool.wait_ge(sig("quarter"), 1)
            pool.wait_ge(sig("sigma_in"), 16)
            pool.wait_ge(sig("phi_in"), 16)
            link(pool.tensor_tensor(sig_sb[:, 2:3], sig_sb[:, 0:1], sig_sb[:, 1:2], ALU.pow))
            pool.tensor_scalar(phi_sb, phi_sb, sig_sb[:, 2:3], None, MUL).then_inc(sig("phi_scaled"), 1)
            pool.wait_ge(sig("spec_sq"), 1)
            pool.tensor_tensor(ta[:, 0:HALF], ta[:, 0:HALF], ta[:, HALF:L], ADD).then_inc(sig("mag_sq"), 1)
            pool.wait_ge(sig("scale_logs"), 3)
            pool.tensor_tensor(te[:, 0:HALF], te[:, 0:HALF], te[:, HALF:L], ADD).then_inc(sig("scale_sum"), 1)
            pool.wait_ge(sig("scale_exp"), 1)
            link(pool.tensor_scalar(te[:, 0:HALF], te[:, 0:HALF], 0.95, None, MUL))
            for r in range(2):
                link(pool.tensor_tensor(spec[:, r, :], spec[:, r, :], te[:, 0:HALF], MUL))
            for dst, src in ((ai2, spec[:, 1, :]), (bi2, spec[:, 3, :])):
                pool.tensor_scalar(dst[:, 0, :], src, -1.0, None, MUL)
                pool.tensor_copy(dst[:, 1, :], src).then_inc(sig("spec_ready"), 1)

            def rest(n):
                wait(pool, sig("w_rest"), n + 1)
                pool.tensor_tensor(te, te, tw, ADD).then_inc(sig("rest_ready"), 1)

            def low(n):
                wait(pool, sig("delta_high"), n + 1)
                pool.tensor_tensor(high(te), tz, ta, SUB).then_inc(sig("delta_split"), 1)

            def slot(k, s):
                n, b, i = split_slot(k, s)
                if i == 0:
                    wait(pool, sig("c_ready"), n + 1)
                wait(pool, sig("scanned"), GROUPS * n + i + 1)
                pool.tensor_tensor(state[:, i % 8, :], state[:, i % 8, :], c_rep[:, b, :],
                                   MUL).then_inc(sig("weighed"), 1)
                if i == 5 and not ends(k, b):
                    rest(n + 1)
                if i == 7 and not ends(k, b):
                    low(n + 1)

            rest(0)
            low(0)
            scan_loop(pool, slot)
            recurrence(pool, link, slice(HALF - POOL_COLS, HALF))
            pool.sem_inc(sig("pool_recurred"), 1)
            def of_span(g):
                return w_seg.rearrange("p k (g e) -> p k g e", g=4)[:, :, g, :]

            pool.wait_ge(*after("attn_done"))
            for i in range(4):
                plus, minus = (m_in[:, i % 2, s].rearrange("p (k e) -> p k e", k=KF) for s in range(2))
                pool.wait_ge(sig("m_weighted"), 2 * (i + 1))
                ins = pool.tensor_tensor(of_span(3 - i), plus, minus, ADD)
                if i:
                    link(ins)
                    ins = pool.tensor_tensor(of_span(3 - i), of_span(3 - i), of_span(4 - i), ADD)
                ins.then_inc(sig("m_added"), 1)
            for i in range(4):
                pool.wait_ge(sig("ar_weighted"), i + 1)
                new = w_ar[:, 3 - i].rearrange("p a m -> p (a m)")
                if i == 0:
                    pool.tensor_copy(new, ar_in[:, 0, :]).then_inc(sig("ar_added"), 1)
                else:
                    pool.wait_ge(sig("ar_added"), i)
                    pool.tensor_tensor(new, w_ar[:, 4 - i].rearrange("p a m -> p (a m)"), ar_in[:, i, :],
                                       ADD).then_inc(sig("ar_added"), 1)
            pool.wait_ge(*after("lin_done"))
            pool.memset(u_t[:, :, 0:1], 0.0).then_inc(sig("u_t_zero"), 1)

            def weights(k, a):
                if not isinstance(k, int) or k >= 2:
                    pool.wait_ge(sig("mixed"), k - 1)
                pool.tensor_copy(w_work[:, a:a + 1, :], w_seg[:, bass.ds(k, 1), :]).then_inc(sig("w_work_set"), 1)

            pool.wait_ge(sig("m_added"), 4)
            for a in range(2):
                weights(a, a)
            with pool.Fori(1, KF // 2) as pair:
                for a in range(2):
                    weights(2 * pair + a, a)

        @block.scalar
        def _(act):
            link = chainer(act, sig("act_step"))
            act.preload_act_table_set("natural_log_exp_and_others")
            act.wait_ge(sig("eps_set"), 1)
            act.wait_ge(sig("spec_done"), 1)
            act.activation(spec[:, 0:2, :], ps[:, 0:2, :], ACT.Copy)
            act.activation(spec[:, 2:4, :], ps[:, 2:4, :], ACT.Copy, scale=0.1).then_inc(sig("spec_out"), 1)
            act.wait_ge(sig("spec_out"), 1)
            act.activation(ta, spec[:, 0:2, :].rearrange("p r n -> p (r n)"), ACT.Square).then_inc(sig("spec_sq"), 1)
            act.wait_ge(sig("gn_var"), 1)
            link(act.activation(small[:, 4:5], small[:, 3:4], ACT.Ln, bias=eps5[:]))
            act.activation(small[:, 5:6], small[:, 4:5], ACT.Exp, scale=-0.5).then_inc(sig("gn_rstd"), 1)
            act.wait_ge(sig("mag_sq"), 1)
            mag = ta[:, 0:HALF]
            link(act.activation(te[:, 0:HALF], mag, ACT.Ln, bias=eps8[:]))
            link(act.activation(mag, te[:, 0:HALF], ACT.Exp, scale=0.5))
            act.activation(te[:, 0:HALF], mag, ACT.Exp, scale=-1.0).then_inc(sig("scale_logs"), 1)
            act.wait_ge(sig("scale_logs"), 1)
            act.activation(te[:, 0:HALF], te[:, 0:HALF], ACT.Ln, bias=1.0).then_inc(sig("scale_logs"), 1)
            act.activation(te[:, HALF:L], mag, ACT.Ln, bias=eps8[:]).then_inc(sig("scale_logs"), 1)
            act.wait_ge(sig("scale_sum"), 1)
            act.activation(te[:, 0:HALF], te[:, 0:HALF], ACT.Exp, scale=-1.0).then_inc(sig("scale_exp"), 1)
            act.wait_ge(sig("par_min"), 1)
            act.activation(par_sb[:, :, 0:16], par_sb[:, :, 0:16], ACT.Exp).then_inc(sig("par_exp"), 1)
            act.wait_ge(sig("sel_in"), 16)
            act.activation(sel[:].rearrange("p v m -> p (v m)"), sel_in, ACT.Copy).then_inc(sig("sel_ready"), 1)
            act.wait_ge(*after("pick_logits"))
            act.activation(small[:, 40:44], small[:, 36:40], ACT.Exp, bias=small[:, 45:46]).then_inc(reach("pick_exp"), 1)
            act.preload_act_table_set("silu_and_others")
            act.wait_ge(sig("vecs_in"), 16)
            for b in range(B):
                act.wait_ge(sig("conv_done"), b + 1)
                act.activation(xs[:, b, 3, :], banks(2 * b), ACT.Silu,
                               bias=vecs[:, V_CONVB:V_CONVB + 1]).then_inc(sig("xc_ready"), 1)
            for b in range(B):
                act.wait_ge(sig("z_done"), b + 1)
                act.activation(z_gate[:, b, :], banks(4 + 2 * b), ACT.Silu).then_inc(sig("z_ready"), 1)
            act.wait_ge(sig("w_dt_done"), 1)
            act.activation(w_all[:, :, 0, :], ps[:, 0, :].rearrange("p (a m) -> p a m", a=ND),
                           ACT.Copy).then_inc(sig("w_dt_ready"), 1)
            act.preload_act_table_set("natural_log_exp_and_others")

            def set_weights(k):
                act.activation(w_now.unsqueeze(1), w_all[:, bass.ds(k, 1), :, :],
                               ACT.Copy).then_inc(sig("w_now_set"), 1)
                act.activation(bias_now[:].unsqueeze(1), par_sb[:, bass.ds(k, 1), 16:17],
                               ACT.Copy).then_inc(sig("bias_set"), 1)

            def set_rates(k):
                wait(act, sig("decayed"), PER * k)
                act.activation(par_now[:].unsqueeze(1), par_sb[:, bass.ds(k, 1), 0:16],
                               ACT.Copy).then_inc(sig("rates_set"), 1)

            def soft(n, k, b, step):
                if step == "z":
                    wait(act, sig("projected"), 3 * n + 1)
                    wait(act, sig("stacked"), 128 * n)
                    wait(act, sig("bias_set"), k + 1)
                    act.activation(tz, banks(6), ACT.Identity, bias=bias_now[:]).then_inc(sig("tz_ready"), 1)
                    act.activation(ta, banks(6), ACT.Abs, bias=bias_now[:]).then_inc(sig("abs_ready"), 1)
                elif step == "exp":
                    wait(act, sig("abs_ready"), n + 1)
                    act.activation(te, ta, ACT.Exp, scale=-1.0).then_inc(sig("exp_ready"), 1)
                elif step == "one_plus":
                    wait(act, sig("exp_ready"), n + 1)
                    act.activation(tw, te, ACT.Identity, bias=1.0).then_inc(sig("w_ready"), 1)
                elif step == "log":
                    wait(act, sig("w_ready"), n + 1)
                    act.activation(ta, tw, ACT.Ln).then_inc(sig("log_ready"), 1)
                elif step == "rest":
                    wait(act, sig("log_ready"), n + 1)
                    act.activation(tw, tw, ACT.Identity, bias=1.0, scale=-1.0).then_inc(sig("w_rest"), 1)
                elif step == "b":
                    wait(act, sig("projected"), 3 * n + 2)
                    act.activation(b_rep[:, b, :], banks(6), ACT.Copy).then_inc(sig("b_ready"), 1)
                elif step == "delta":
                    wait(act, sig("delta_ready"), n + 1)
                    act.activation(high(ta), tz, ACT.Copy).then_inc(sig("delta_high"), 1)
                elif step == "u":
                    wait(act, sig("u_ready"), n + 1)
                    act.activation(high(tu), tw, ACT.Copy).then_inc(sig("u_high"), 1)
                elif step == "c":
                    wait(act, sig("projected"), 3 * n + 3)
                    act.activation(c_rep[:, b, :], banks(6), ACT.Copy).then_inc(sig("c_ready"), 1)

            soft_at = {2: ["z"], 3: ["exp"], 4: ["one_plus"], 5: ["log"], 6: ["rest", "b"], 8: ["delta"],
                       9: ["u"], 10: ["c"]}

            def slot(k, s):
                n, b, i = split_slot(k, s)
                wait(act, sig("steps_spread"), GROUPS * n + i + 1)
                wait(act, sig("scanned"), GROUPS * n + i - 1)
                if s == 0:
                    wait(act, sig("rates_set"), k + 1)
                act.activation(decay[:, i % 2, :], banks(0), ACT.Exp,
                               scale=par_now[:, i:i + 1]).then_inc(sig("decayed"), 1)
                nk, nb = following(k, b)
                for step in soft_at.get(i, []) if not ends(k, b) else []:
                    soft(n + 1, nk, nb, step)
                if i == 4:
                    pk, pb = (k - 1, 1) if b == 0 else (k, 0)
                    if not isinstance(pk, int) or 0 <= pk < ND - 1:
                        wait(act, sig("summed"), 4 * n)
                        act.activation(xs[:, pb, bass.ds(pk, 1), :], banks(4).unsqueeze(1),
                                       ACT.Copy).then_inc(sig("y_free"), 1)
                if s == 12 and not (isinstance(k, int) and k == ND - 1):
                    set_weights(k + 1)
                if s == PER - 1 and not (isinstance(k, int) and k == ND - 1):
                    set_rates(k + 1)

            act.wait_ge(sig("spec_ready"), 2)
            act.wait_ge(sig("w_bc_in"), 16)
            act.wait_ge(sig("w_dt_ready"), 1)
            act.wait_ge(sig("par_neg"), 1)
            act.wait_ge(sig("phi_out"), 16)
            act.sem_inc(sig("y_free"), 1)
            set_weights(0)
            set_rates(0)
            for steps in soft_at.values():
                for step in steps:
                    soft(0, 0, 0, step)
            scan_loop(act, slot)
            squares = (te, tw)
            for b in range(B):
                act.wait_ge(sig("y_centered"), b + 1)
                act.activation(squares[b], ysum[b], ACT.Square).then_inc(sig("y_squares"), 1)
            for b in range(B):
                act.wait_ge(sig("y_var"), b + 1)
                link(act.activation(squares[b], banks(4 + 2 * b), ACT.Ln, bias=eps5[:]))
                act.activation(squares[b], squares[b], ACT.Exp, scale=-0.5).then_inc(sig("y_rstd"), 1)
            for b in range(B):
                act.wait_ge(sig("y_normed"), b + 1)
                act.activation(ysum[b], ysum[b], ACT.Identity, bias=vecs[:, V_LNB:V_LNB + 1],
                               scale=vecs[:, V_LNW:V_LNW + 1]).then_inc(sig("y_affine"), 1)
            act.wait_ge(sig("gn_var"), 2)
            link(act.activation(small[:, 4:5], small[:, 3:4], ACT.Ln, bias=eps5[:]))
            act.activation(small[:, 5:6], small[:, 4:5], ACT.Exp, scale=-0.5).then_inc(sig("gn_rstd"), 1)

            def pairs(t):
                return t.rearrange("p (r n) -> p r n", r=2)

            act.wait_ge(sig("gates_done"), 1)
            for r in range(2):
                bias = vecs[:, V_BD + r:V_BD + r + 1]
                act.activation(pairs(sp_r)[:, r, :], ps[:, 4 + r, :], ACT.Relu, bias=bias)
                link(act.activation(pairs(sp_a)[:, r, :], ps[:, 4 + r, :], ACT.Abs, bias=bias))
            link(act.activation(sp_a, sp_a, ACT.Exp, scale=-1.0))
            act.activation(sp_a, sp_a, ACT.Ln, bias=1.0).then_inc(sig("gates_out"), 1)
            act.wait_ge(sig("gates_done"), 2)
            act.activation(sp_x, banks(6), ACT.Copy).then_inc(sig("gates_out"), 2)
            act.preload_act_table_set("sigmoid_and_others")
            for g, (dst, col) in enumerate(((sp_f, None), (sp_i, V_BI))):
                act.wait_ge(sig("gates_done"), 3 + g)
                for r in range(2):
                    bias = small[:, 26 + r:27 + r] if col is None else vecs[:, col + r:col + r + 1]
                    ins = act.activation(pairs(dst)[:, r, :], ps[:, 2 * g + r, :], ACT.Sigmoid, bias=bias)
                ins.then_inc(sig("gates_out"), 1)
            act.preload_act_table_set("natural_log_exp_and_others")

            def to_tokens(n, dst, first=2):
                act.wait_ge(sig("turned"), n)
                act.activation(dst, banks(first), ACT.Copy).then_inc(sig("turned_out"), 1)

            to_tokens(1, tok_flat)
            norm_act(act, link, 1)
            to_tokens(2, xn_t, 0)
            act.wait_ge(*after("k_max"))
            act.activation(k_e, ps[:, 4:8, :].rearrange("p a n -> p (a n)"), ACT.Exp, bias=small[:, 129:130],
                           accum_out=small[:, 130:131]).then_inc(reach("k_exp"), 1)
            for r in range(2):
                act.wait_ge(sig("qv_done"), r + 1)
                act.activation(qv[:, 8 * r:8 * r + 8, :].rearrange("p u n -> p (u n)"),
                               ps[:, 0:4, :].rearrange("p a n -> p (a n)"), ACT.Copy).then_inc(sig("qv_out"), 1)
            act.wait_ge(*after("q_shifted"))
            act.activation(q_e, q_e, ACT.Exp).then_inc(reach("q_exp"), 1)
            act.wait_ge(*after("k_turned"))
            act.activation(k_tok, ps[:, 4:8, :].rearrange("p a n -> p (a n)"), ACT.Copy).then_inc(reach("k_tok_ready"), 1)
            act.wait_ge(*after("q_turned"))
            act.activation(q_t_sb, ps[:, 0:4, :].rearrange("p a n -> p (a n)"), ACT.Copy).then_inc(reach("q_t_ready"), 1)
            norm_act(act, link, 2)
            norm_act(act, link, 3)
            to_tokens(3, xn_t, 0)
            act.wait_ge(*after("r_shifted"))
            act.activation(gates[:, 0:P], gates[:, 0:P], ACT.Exp).then_inc(reach("r_exp"), 1)
            for i in range(4):
                act.wait_ge(sig(f"m_in_{i % 2}"), 16 * (i // 2 + 1))
                act.wait_ge(*after("picked"))
                for s in range(2):
                    at = 56 + 4 * s + i
                    act.activation(m_in[:, i % 2, s], m_in[:, i % 2, s], ACT.Copy,
                                   scale=small[:, at:at + 1]).then_inc(sig("m_weighted"), 1)
            act.wait_ge(*after("g_turned"))
            act.activation(gates[:, 5 * P:6 * P], ps[:, 3, 0:P], ACT.Copy).then_inc(reach("g_t_ready"), 1)
            norm_act(act, link, 4)
            to_tokens(4, xn_t, 0)
            act.wait_ge(*after("zeroed"))
            copy_g(act, 0, act.activation, ps[:, 2, 0:P])
            for l in range(LAYERS):
                act.wait_ge(sig("t_done"), l + 1)
                act.activation(t_sb, ps[:, 3, :], ACT.Copy).then_inc(sig("t_out"), 1)
                act.wait_ge(sig("wt_done"), l + 1)
                act.activation(wt_sb, ps[:, 6, 0:P], ACT.Copy).then_inc(sig("wt_out"), 1)
                if l == 0:
                    act.wait_ge(sig("ar_in"), 16)
                    for i in range(4):
                        act.activation(ar_in[:, i, :], ar_in[:, i, :], ACT.Copy,
                                       scale=small[:, 56 + i:57 + i]).then_inc(sig("ar_weighted"), 1)
                if l < LAYERS - 1:
                    copy_g(act, l + 1, act.activation, ps[:, 7, 0:P])
            act.wait_ge(*after("w_turned"))
            act.activation(wt_sb, ps[:, 6, 0:P], ACT.Copy).then_inc(reach("w_out_ready"), 1)
            norm_act(act, link, 5)
            act.wait_ge(sig("turned"), 5)
            act.wait_ge(*after("lin_done"))
            for t in range(2):
                act.activation(u_t[:, t, 1:HALF + 1].rearrange("p (q n) -> p q n", q=4),
                               banks(2).rearrange("p (q t n) -> p t q n", q=4, t=2)[:, t, :, ::-1],
                               ACT.Copy).then_inc(sig("u_t_ready"), 1)
            def toep_high(k, a):
                if not isinstance(k, int) or k >= 2:
                    act.wait_ge(sig("convolved"), 2 * k - 2)
                act.activation(toep_hl[:, a, 0:1, :], toep[:, bass.ds(k, 1), :], ACT.Copy).then_inc(sig("toep_high"), 1)

            act.wait_ge(sig("normed"), 5)
            act.activation(xn_hl[:, 0, :], xn, ACT.Copy).then_inc(sig("xn_high"), 1)
            act.wait_ge(sig("toep_in"), 32)
            for a in range(2):
                toep_high(a, a)
            filter_loop(act, toep_high)
            act.wait_ge(sig("mixed"), KF)
            act.wait_ge(*after("ar_done"))
            act.activation(y_back.rearrange("p (t g n) -> p (t g) n", t=4, g=2)[:, :, ::-1],
                           banks(0).rearrange("p (g n) -> p g n", n=P), ACT.Copy).then_inc(reach("filters_out"), 1)

        @block.vector
        def _(dve):
            link = chainer(dve, sig("dve_step"))
            pair_ps = ps[:, 7, 0:2]

            def group_norm(x, n):
                for h in range(2):
                    link(dve.bn_stats(small[:, 8 + 6 * h:14 + 6 * h], x[:, h * HALF:(h + 1) * HALF]))
                dve.bn_aggr(small[:, 0:2], small[:, 8:20]).then_inc(sig("gn_stats"), 1)
                dve.wait_ge(sig("gn_pair"), n)
                link(dve.tensor_copy(small[:, 20:22], pair_ps))
                link(dve.tensor_tensor(small[:, 2:3], small[:, 0:1], small[:, 20:21], SUB))
                dve.scalar_tensor_tensor(small[:, 3:4], small[:, 2:3], small[:, 2:3], small[:, 21:22],
                                         MUL, ADD).then_inc(sig("gn_var"), 1)
                dve.wait_ge(sig("gn_rstd"), n)

            dve.wait_ge(sig("x_in"), 16)
            group_norm(x_res, 1)
            dve.wait_ge(sig("pad_zero"), 2)
            for b in range(B):
                r = slice(64 * b, 64 * b + 64)
                dve.tensor_scalar(pads[b][r, 1:33, 1:33], x_res[r].rearrange("p (h w) -> p h w", h=H),
                                  small[r, 20:21], small[r, 5:6], SUB, MUL).then_inc(sig("gn_out"), 1)
            dve.wait_ge(sig("par_in"), 16)
            rates = par_sb[:, :, 0:16]
            dve.tensor_scalar(rates, rates, LOG_RATE_MAX, None, MIN).then_inc(sig("par_min"), 1)
            dve.wait_ge(sig("par_exp"), 1)
            dve.tensor_scalar(rates, rates, -1.0, None, MUL).then_inc(sig("par_neg"), 1)
            dve.wait_ge(sig("vecs_in"), 16)
            link(dve.tensor_reduce(small[:, 24:25], vecs[:, V_D:V_D + 4], AX.X, ADD))
            link(dve.tensor_scalar(small[:, 26:28], vecs[:, V_BF:V_BF + 2], 2.0, None, ADD))
            logits, peak, probs, hard = small[:, 36:40], small[:, 44:45], small[:, 40:44], small[:, 48:52]
            rank = con("rank")
            dve.wait_ge(sig("rows_in"), 16)
            link(dve.tensor_tensor(logits, rowb[:, R_LW:R_LW + 4], rowb[:, R_GU:R_GU + 4], ADD))
            link(dve.tensor_reduce(peak, logits, AX.X, MAX))
            dve.tensor_scalar(small[:, 45:46], peak, -1.0, None, MUL).then_inc(reach("pick_logits"), 1)
            dve.wait_ge(*after("pick_exp"))
            link(dve.tensor_reduce(peak, probs, AX.X, ADD))
            link(dve.reciprocal(peak, peak))
            link(dve.tensor_scalar(probs, probs, peak, None, MUL))
            link(dve.tensor_reduce(peak, probs, AX.X, MAX))
            link(dve.tensor_scalar(hard, probs, peak, None, ALU.is_equal))
            link(dve.tensor_tensor(hard, hard, rank[:, 4:8], MUL))
            link(dve.tensor_reduce(peak, hard, AX.X, MAX))
            link(dve.tensor_scalar(hard, hard, peak, None, ALU.is_equal))
            link(dve.tensor_tensor(hard, hard, probs, SUB))
            link(dve.tensor_tensor(small[:, 56:60], hard, probs, ADD))
            dve.tensor_scalar(small[:, 60:64], small[:, 56:60], con("sign"), None, MUL).then_inc(reach("picked"), 1)
            for b in range(B):
                dve.wait_ge(sig("xc_ready"), b + 1)
                nat = xs[:, b, 3, :]
                turned_grid = nat.rearrange("p (h w) -> p w h", h=H)
                dve.tensor_copy(xs[:, b, 0, :].rearrange("p (w h) -> p w h", w=W), turned_grid)
                dve.tensor_copy(xs[:, b, 1, :], nat[:, ::-1])
                dve.tensor_copy(xs[:, b, 2, :].rearrange("p (w h) -> p w h", w=W),
                                turned_grid[:, ::-1, ::-1]).then_inc(sig("orders_ready"), 1)

            def finish_soft(n, k, b, step):
                if step == 0:
                    wait(dve, sig("tz_ready"), n + 1)
                    wait(dve, sig("log_ready"), n + 1)
                    dve.scalar_tensor_tensor(tz, tz, STEP_MIN, ta, MAX, ADD).then_inc(sig("soft_sum"), 1)
                elif step == 1:
                    wait(dve, sig("soft_sum"), n + 1)
                    wait(dve, sig("rest_ready"), n + 1)
                    dve.tensor_tensor(tz, tz, te, ADD).then_inc(sig("delta_ready"), 1)
                elif step == 2:
                    wait(dve, sig("delta_ready"), n + 1)
                    dve.tensor_tensor(tw.unsqueeze(1), tz.unsqueeze(1),
                                      xs[:, b, bass.ds(k, 1), :], MUL).then_inc(sig("u_ready"), 1)
                elif step == 3:
                    wait(dve, sig("u_high"), n + 1)
                    dve.tensor_tensor(high(tw), tw, tu, SUB).then_inc(sig("u_split"), 1)

            def drive_unit(n, b, i):
                if i == 0:
                    wait(dve, sig("b_ready"), n + 1)
                wait(dve, sig("drives_spread"), GROUPS * n + i + 1)
                wait(dve, sig("scanned"), GROUPS * n + i - 3)
                dve.tensor_tensor(drive[:, i % 4, :], banks(2), b_rep[:, b, :], MUL).then_inc(sig("driven"), 1)

            def slot(k, s):
                n, b, i = split_slot(k, s)
                nk, nb = following(k, b)
                if i < GROUPS - 1:
                    drive_unit(n, b, i + 1)
                elif not ends(k, b):
                    drive_unit(n + 1, nb, 0)
                wait(dve, sig("decayed"), GROUPS * n + i + 1)
                wait(dve, sig("driven"), GROUPS * n + i + 1)
                wait(dve, sig("summed"), 4 * n + i // 4 - 1)
                dve.tensor_tensor_scan(state[:, i % 8, :], decay[:, i % 2, :], drive[:, i % 4, :], 0.0,
                                       MUL, ADD).then_inc(sig("scanned"), 1)
                if i in (6, 7, 8, 10) and not ends(k, b):
                    finish_soft(n + 1, nk, nb, {6: 0, 7: 1, 8: 2, 10: 3}[i])
                if isinstance(k, int) and k == ND - 1 and s == GROUPS + 5:
                    outputs(0)

            def outputs(b):
                dve.wait_ge(sig("summed"), 4 * (B * (ND - 1) + b + 1))
                dve.scalar_tensor_tensor(ysum[b], xs[:, b, 3, :], small[:, 24:25], banks(4),
                                         MUL, ADD).then_inc(sig("y_last"), 1)

            dve.wait_ge(sig("orders_ready"), 2)
            for step in range(4):
                finish_soft(0, 0, 0, step)
            drive_unit(0, 0, 0)
            scan_loop(dve, slot)
            outputs(1)
            dve.wait_ge(sig("y_free"), B * (ND - 1) + 1)
            for b in range(B):
                y = ysum[b]
                grid = y.rearrange("p (h w) -> p h w", h=H)
                turned = xs[:, b, 0, :].rearrange("p (w h) -> p h w", w=W)
                turned_back = xs[:, b, 2, :].rearrange("p (w h) -> p h w", w=W)[:, ::-1, ::-1]
                link(dve.tensor_tensor(grid, grid, turned, ADD))
                link(dve.tensor_tensor(y, y, xs[:, b, 1, ::-1], ADD))
                dve.tensor_tensor(grid, grid, turned_back, ADD).then_inc(sig("y_ready"), 1)
            for b in range(B):
                dve.wait_ge(sig("y_mean"), b + 1)
                dve.tensor_tensor(ysum[b], ysum[b], banks(2 * b), SUB).then_inc(sig("y_centered"), 1)
            for b in range(B):
                dve.wait_ge(sig("y_rstd"), b + 1)
                dve.tensor_tensor(ysum[b], ysum[b], (te, tw)[b], MUL).then_inc(sig("y_normed"), 1)
            for b in range(B):
                dve.wait_ge(sig("y_affine"), b + 1)
                dve.tensor_tensor(ysum[b], ysum[b], z_gate[:, b, :], MUL).then_inc(sig("y_gated"), 1)
            dve.wait_ge(*after("l0_done"))
            link(dve.tensor_tensor(x_res[:], x_res[:], banks(0), ADD))
            group_norm(x_res, 2)
            dve.tensor_scalar(xn1, x_res[:], small[:, 20:21], small[:, 5:6], SUB, MUL).then_inc(sig("gn_out"), 1)
            recurrence(dve, link, slice(0, HALF - POOL_COLS))
            dve.sem_inc(sig("dve_recurred"), 1)
            dve.wait_ge(*after("l1_done"))
            quarters = lambda t: t.rearrange("p (q n t) -> p q n t", q=4, t=2)
            dve.tensor_tensor(quarters(xn_t)[:, :, ::-1, :], quarters(x_res[:]), quarters(banks(0)),
                              ADD).then_inc(reach("x2_ready"), 1)
            dve.wait_ge(sig("turned_out"), 1)
            norm_dve(dve, link, 1, tok_flat, xn)
            dve.wait_ge(*after("k_done"))
            link(dve.tensor_reduce(small[:, 128:129], ps[:, 4:8, :].rearrange("p a n -> p (a n)"), AX.X, MAX))
            dve.tensor_scalar(small[:, 129:130], small[:, 128:129], -1.0, None, MUL).then_inc(reach("k_max"), 1)
            q_heads = qv[:, :, 0:P].rearrange("p u (h d) -> p u h d", h=HEADS)
            q_st = small[:, 136:200]
            q_rep = q_st.rearrange("p (u h) -> p u h", u=UN).unsqueeze(3).broadcast_to([P, UN, HEADS, DH])
            q_sh = q_e.rearrange("p (u h d) -> p u h d", u=UN, h=HEADS)
            dve.wait_ge(sig("qv_out"), 2)
            link(dve.tensor_reduce(q_st.rearrange("p (u h) -> p u h", u=UN), q_heads, AX.X, MAX))
            dve.tensor_tensor(q_sh, q_heads, q_rep, SUB).then_inc(reach("q_shifted"), 1)
            dve.wait_ge(*after("q_exp"))
            link(dve.tensor_reduce(q_st, q_e.rearrange("p (g d) -> p g d", d=DH), AX.X, ADD))
            link(dve.reciprocal(q_st, q_st))
            dve.tensor_tensor(q_sh, q_sh, q_rep, MUL).then_inc(reach("q_ready"), 1)
            dve.wait_ge(*after("k_exp"))
            link(dve.tensor_scalar(small[:, 131:132], small[:, 130:131], float(B * L * np.sqrt(DH)), None, MUL))
            link(dve.reciprocal(small[:, 131:132], small[:, 131:132]))
            dve.wait_ge(*after("ctx_done"))
            dve.tensor_tensor(ctx_m, ps[:, 4, 0:P], con("heads"), MUL).then_inc(reach("ctx_ready"), 1)
            dve.wait_ge(*after("mix_done"))
            dve.tensor_scalar(mix_m, ps[:, 5, 0:C], small[:, 131:132], None, MUL).then_inc(reach("mix_ready"), 1)

            def row(col, n=C):
                return rowb[:, col:col + n].unsqueeze(1).broadcast_to([P, UN, n])

            dve.wait_ge(*after("attn_out"))
            link(dve.tensor_tensor(units(xn), units(banks(6)), row(R_BOUT), ADD))
            norm_dve(dve, link, 2, xn, xn_t)
            dve.wait_ge(sig("normed"), 2)
            link(dve.tensor_tensor(units(xn_t), units(xn_t), row(R_LNW), MUL))
            link(dve.tensor_tensor(tok_flat, tok_flat, xn_t, ADD))
            dve.sem_inc(reach("attn_done"), 1)
            norm_dve(dve, link, 3, tok_flat, xn)
            lg, g2, g3 = (gates[:, P * a:P * (a + 1)].rearrange("p (u e) -> p u e", u=UN) for a in range(3))
            top, top2, den = gates[:, 3 * P:3 * P + UN], gates[:, 3 * P + UN:3 * P + 2 * UN], gates[:, 4 * P:4 * P + UN]
            ranks = rank.unsqueeze(1).broadcast_to([P, UN, E])
            dve.wait_ge(*after("router_done"))
            link(dve.tensor_tensor(lg, ps[:, 2, 0:P].rearrange("p (u e) -> p u e", u=UN), row(R_RB, E), ADD))
            link(dve.tensor_reduce(top, lg, AX.X, MAX))
            dve.tensor_tensor(lg, lg, over(top, E), SUB).then_inc(reach("r_shifted"), 1)
            dve.wait_ge(*after("r_exp"))

            def first_best(dst, src, best):
                link(dve.tensor_reduce(best, src, AX.X, MAX))
                link(dve.tensor_tensor(dst, src, over(best, E), ALU.is_equal))
                link(dve.tensor_tensor(dst, dst, ranks, MUL))
                link(dve.tensor_reduce(den, dst, AX.X, MAX))
                link(dve.tensor_tensor(dst, dst, over(den, E), ALU.is_equal))

            first_best(g2, lg, top)
            link(dve.scalar_tensor_tensor(lg, g2, -2.0, lg, MUL, ADD))
            first_best(g3, lg, top2)
            link(dve.tensor_tensor(g3, g3, over(top2, E), MUL))
            link(dve.tensor_tensor(g2, g2, g3, ADD))
            link(dve.tensor_scalar(den, top2, 1.0, None, ADD))
            link(dve.reciprocal(den, den))
            dve.tensor_tensor(g2, g2, over(den, E), MUL).then_inc(reach("gates_ready"), 1)
            dve.wait_ge(*after("gates_ready"))
            for u in range(UN):
                dve.wait_ge(sig("expert_done"), u + 1)
                dve.tensor_tensor(prod[:, u % 2, :].rearrange("p (e c) -> p e c", e=E),
                                  ps[:, 4 + u % 4, :].rearrange("p (e c) -> p e c", e=E),
                                  g2[:, u, :].unsqueeze(2).broadcast_to([P, E, C]), MUL).then_inc(sig("weighted"), 1)
                if u >= 1:
                    dve.wait_ge(sig("weighted"), u)
                    dve.tensor_reduce(units(xn)[:, u - 1, :], prod[:, (u - 1) % 2, :].rearrange(
                        "p (e c) -> p c e", e=E), AX.X, ADD).then_inc(sig("expert_sum"), 1)
                    dve.wait_ge(sig("expert_sum"), u)
            dve.wait_ge(sig("weighted"), UN)
            link(dve.tensor_reduce(units(xn)[:, UN - 1, :], prod[:, (UN - 1) % 2, :].rearrange(
                "p (e c) -> p c e", e=E), AX.X, ADD))
            link(dve.tensor_tensor(tok_flat, tok_flat, xn, ADD))
            dve.wait_ge(*after("bias_done"))
            link(dve.tensor_tensor(tok_flat, tok_flat, banks(0), ADD))
            dve.sem_inc(reach("moe_done"), 1)
            norm_dve(dve, link, 4, tok_flat, xn)
            dve.memset(is_sb, 0.0)
            dve.memset(g_sb, 0.0)
            dve.memset(g_two, 0.0).then_inc(reach("zeroed"), 1)
            dve.wait_ge(*after("zeroed"))
            copy_g(dve, 0, dve.tensor_copy, ps[:, 2, 0:P])
            for l in range(LAYERS):
                dve.wait_ge(sig("s_done"), l + 1)
                wait(dve, sig("wt_done"), l)
                for b in range(B):
                    r = slice(64 * b, 64 * b + 64)
                    ins = dve.scalar_tensor_tensor(is_sb[r, r], ps[r, 4, r], 1.0 / (L * LH), con("ident")[r, r],
                                                   MUL, ADD)
                ins.then_inc(sig("is_ready"), 1)
                if l < LAYERS - 1:
                    dve.wait_ge(sig("gs_done"), l + 1)
                    dve.tensor_copy(u_sb, ps[:, 5, 0:P]).then_inc(sig("gs_out"), 1)
                    copy_g(dve, l + 1, dve.tensor_copy, ps[:, 7, 0:P])
            dve.wait_ge(*after("lin_out"))
            link(dve.tensor_tensor(tok_flat, tok_flat, banks(0), ADD))
            dve.sem_inc(reach("lin_done"), 1)
            norm_dve(dve, link, 5, tok_flat, xn)
            dve.wait_ge(sig("xn_high"), 1)
            dve.tensor_tensor(xn_hl[:, 1, :], xn, xn_hl[:, 0, :].bitcast(F32), SUB).then_inc(sig("xn_low"), 1)

            def toep_low(k, a):
                dve.wait_ge(sig("toep_high"), k + 1)
                dve.tensor_tensor(toep_hl[:, a, 1:2, :], toep[:, bass.ds(k, 1), :],
                                  toep_hl[:, a, 0:1, :].bitcast(F32), SUB).then_inc(sig("toep_low"), 1)

            for a in range(2):
                toep_low(a, a)
            filter_loop(dve, toep_low)
            for h in range(2):
                dve.wait_ge(sig("out_turned"), h + 1)
                dve.tensor_tensor(fin[:, h * HALF:(h + 1) * HALF], tok_flat[:, h * HALF:(h + 1) * HALF],
                                  ps[:, 2 + h, :], ADD).then_inc(sig("out_ready"), 1)

        @block.tensor
        def _(pe):
            def half(ap, h):
                return ap[:, h * HALF:(h + 1) * HALF]

            pe.wait_ge(sig("ab_in"), 16)
            pe.wait_ge(sig("dft_in"), 16)
            for f in range(2):
                for r in range(2):
                    for h in range(2):
                        mm = pe.matmul(ps[64 * h:64 * h + 64, 2 * f + r, :], ab_sb[:, f, :],
                                       dft_sb[0:2 * KK, r, h * HALF:(h + 1) * HALF], start=True, stop=True)
            mm.then_inc(sig("spec_done"), 1)

            def pair_mean(n):
                pe.wait_ge(sig("gn_stats"), n)
                pe.matmul(ps[:, 7, 0:2], con("pair"), small[:, 0:2], start=True, stop=True).then_inc(sig("gn_pair"), 1)

            pe.wait_ge(sig("consts_in"), 16)
            pair_mean(1)
            pe.wait_ge(sig("spec_out"), 1)
            pe.wait_ge(sig("taps_ready"), 1)
            for b in range(B):
                pe.wait_ge(sig("gn_out"), b + 1)
                for h in range(2):
                    for t in range(9):
                        dy, dx = divmod(t, 3)
                        mm = pe.matmul(ps[:, 2 * b + h, :], w_taps[:, t, :],
                                       pads[b][:, 16 * h + dy:16 * h + dy + 16, dx:dx + W],
                                       start=(t == 0), stop=(t == 8))
                mm.then_inc(sig("conv_done"), 1)
            for b in range(B):
                for h in range(2):
                    mm = pe.matmul(ps[:, 4 + 2 * b + h, :], w_in_sb[:, DI:2 * DI],
                                   pads[b][:, 16 * h + 1:16 * h + 17, 1:1 + W], start=True, stop=True)
                mm.then_inc(sig("z_done"), 1)
            pe.wait_ge(sig("w_dt_in"), 16)
            pe.wait_ge(sig("xc_ready"), 1)
            for k in range(ND):
                mm = pe.matmul(ps[:, 0, k * P:(k + 1) * P], w_dt_sb[:, 0, k, :], w_dt_sb[:, 1, k, :],
                               start=True, stop=True)
            mm.then_inc(sig("w_dt_done"), 1)

            def project(n, k, b, what, h):
                if h == 0:
                    if what == 0:
                        wait(pe, sig("w_now_set"), k + 1)
                        wait(pe, sig("c_ready"), n)
                    else:
                        wait(pe, sig(("abs_ready", "b_ready")[what - 1]), n + 1)
                mm = pe.matmul(ps[:, 6 + h, :].unsqueeze(1), w_now[:, what, :],
                               xs[:, b, bass.ds(k, 1), h * HALF:(h + 1) * HALF], start=True, stop=True)
                if h == 1:
                    mm.then_inc(sig("projected"), 1)

            def spread(n, b, i):
                u = GROUPS * n + i
                if i == 0:
                    wait(pe, sig("stacked"), 128 * (n + 1))
                j, v = i % 4, i // 4
                for what, used, spread_out in ((1, "driven", "drives_spread"), (0, "decayed", "steps_spread")):
                    wait(pe, sig(used), u)
                    for h in range(2):
                        mm = pe.matmul(ps[:, 2 * what + h, :], sel[:, 4 * (j % 2) + v, :],
                                       stack[:, b, what, j // 2, h * HALF:(h + 1) * HALF],
                                       start=True, stop=True)
                    mm.then_inc(sig(spread_out), 1)

            def sum_states(n, b, v, h, free=None):
                if h == 0:
                    wait(pe, sig("weighed"), GROUPS * n + 4 * v + 4)
                    if v == 0:
                        free()
                for j in range(4):
                    mm = pe.matmul(ps[32 * j:32 * j + 32, 4 + h, :], red[:, v, :],
                                   state[:, (4 * v + j) % 8, h * HALF:(h + 1) * HALF],
                                   start=(v == 0), stop=(v == 3))
                if h == 1:
                    mm.then_inc(sig("summed"), 1)

            def slot(k, s):
                n, b, i = split_slot(k, s)
                spread(n, b, i)
                nk, nb = following(k, b)

                def free():
                    if ends(k, b):
                        pe.wait_ge(sig("y_last"), 1)
                    else:
                        wait(pe, sig("y_free"), n + 1)
                if i in (0, 1, 4, 5, 8, 9) and not ends(k, b):
                    project(n + 1, nk, nb, i // 4, i % 4)
                elif i in (2, 3) and not (isinstance(k, int) and s < GROUPS and k == 0):
                    sum_states(n - 1, 1 - b, 3, i - 2)
                elif i in (6, 7, 10, 11, 14, 15):
                    sum_states(n, b, (i - 6) // 4, (i - 6) % 4, free)

            for what in range(3):
                if what == 0:
                    pe.wait_ge(sig("orders_ready"), 1)
                    pe.wait_ge(sig("z_ready"), 2)
                for h in range(2):
                    project(0, 0, 0, what, h)
            pe.wait_ge(sig("orders_ready"), 2)
            scan_loop(pe, slot)
            for h in range(2):
                sum_states(B * ND - 1, 1, 3, h)
            for b in range(B):
                pe.wait_ge(sig("y_ready"), b + 1)
                for h in range(2):
                    mm = pe.matmul(ps[:, 2 * b + h, :], con("mean"), half(ysum[b], h), start=True, stop=True)
                mm.then_inc(sig("y_mean"), 1)
            for b in range(B):
                pe.wait_ge(sig("y_squares"), b + 1)
                for h in range(2):
                    mm = pe.matmul(ps[:, 4 + 2 * b + h, :], con("mean"), half((te, tw)[b], h), start=True, stop=True)
                mm.then_inc(sig("y_var"), 1)
            pe.wait_ge(sig("w_out_in"), 16)
            for b in range(B):
                pe.wait_ge(sig("y_gated"), b + 1)
                for h in range(2):
                    mm = pe.matmul(ps[64 * b:64 * b + 64, h, :], w_out_sb[:], half(ysum[b], h), start=True, stop=True)
            mm.then_inc(reach("l0_done"), 1)
            pair_mean(2)
            pe.wait_ge(sig("gn_out"), 3)
            pe.wait_ge(sig("w_gate_in"), 16)
            for bank, lhs in ((4, w_gate_sb[:, 2]), (6, split), (0, w_gate_sb[:, 0]), (2, w_gate_sb[:, 1])):
                for r in range(2):
                    for h in range(2):
                        mm = pe.matmul(ps[64 * h:64 * h + 64, bank + r, :], lhs[:, r, :], half(xn1, h),
                                       start=True, stop=True)
                mm.then_inc(sig("gates_done"), 1)
            pe.wait_ge(sig("dve_recurred"), 1)
            pe.wait_ge(sig("pool_recurred"), 1)
            for h in range(2):
                for r in range(2):
                    mm = pe.matmul(ps[:, h, :], merge[:, h, r, :], sp_v[:, r * HALF:(r + 1) * HALF],
                                   start=(r == 0), stop=(r == 1))
            mm.then_inc(reach("l1_done"), 1)

            def turn(src, bank):
                for j in range(TILES):
                    mm = pe.transpose(ps[:, bank + j // 4, (j % 4) * P:(j % 4 + 1) * P], src(j), ident)
                mm.then_inc(sig("turned"), 1)

            def tile(t):
                return lambda j: t[:, j * P:(j + 1) * P]

            pe.wait_ge(*after("x2_ready"))
            turn(lambda j: xn_t.rearrange("p (q n t) -> p q t n", q=4, t=2)[:, j // 2, j % 2, :], 2)
            pe.wait_ge(sig("normed"), 1)
            turn(tile(xn), 0)
            pe.wait_ge(sig("turned_out"), 2)
            pe.wait_ge(sig("w_k_in"), 16)
            for b in range(B):
                for h in range(2):
                    mm = pe.matmul(ps[:, 4 + 2 * b + h, :], w_k_sb[:, b * P:(b + 1) * P], half(xn_t, h),
                                   start=True, stop=True)
            mm.then_inc(reach("k_done"), 1)
            pe.wait_ge(sig("w_qv_in"), 16)
            for j in range(TILES):
                if j == 4:
                    pe.wait_ge(sig("qv_out"), 1)
                mm = pe.matmul(ps[:, j % 4, :], tile(xn_t)(j), w_qv_sb, start=True, stop=True)
                if j % 4 == 3:
                    mm.then_inc(sig("qv_done"), 1)
            pe.wait_ge(*after("k_exp"))
            for u in range(UN):
                mm = pe.transpose(ps[:, 4 + u // 4, (u % 4) * P:(u % 4 + 1) * P], tile(k_e)(u), ident)
            mm.then_inc(reach("k_turned"), 1)
            pe.wait_ge(*after("k_tok_ready"))
            for u in range(UN):
                j, b = divmod(u, B)
                mm = pe.matmul(ps[:, 4, 0:P], qv[:, u, P:2 * P], tile(k_tok)(b * TILES + j),
                               start=(u == 0), stop=(u == UN - 1))
            mm.then_inc(reach("ctx_done"), 1)
            pe.wait_ge(*after("q_ready"))
            for u in range(UN):
                mm = pe.transpose(ps[:, u // 4, (u % 4) * P:(u % 4 + 1) * P], tile(q_e)(u), ident)
            mm.then_inc(reach("q_turned"), 1)
            pe.wait_ge(sig("w_attn_in"), 16)
            pe.wait_ge(*after("ctx_ready"))
            pe.matmul(ps[:, 5, 0:C], ctx_m, w_attn_sb, start=True, stop=True).then_inc(reach("mix_done"), 1)
            pe.wait_ge(*after("mix_ready"))
            pe.wait_ge(*after("q_t_ready"))
            for u in range(UN):
                mm = pe.matmul(ps[:, 6 + u // 8, (u % 8) * C:(u % 8 + 1) * C], tile(q_t_sb)(u), mix_m,
                               start=True, stop=True)
            mm.then_inc(reach("attn_out"), 1)
            pe.wait_ge(sig("normed"), 3)
            turn(tile(xn), 0)
            pe.wait_ge(sig("turned_out"), 3)
            pe.wait_ge(sig("w_rt_in"), 16)
            for j in range(TILES):
                mm = pe.matmul(ps[:, 2, j * 16:(j + 1) * 16], tile(xn_t)(j), w_rt_sb, start=True, stop=True)
            mm.then_inc(reach("router_done"), 1)
            pe.wait_ge(sig("w_exp_in"), 16)
            for u in range(UN):
                if u == 4:
                    pe.wait_ge(*after("gates_ready"))
                    pe.transpose(ps[:, 3, 0:P], gates[:, P:2 * P], ident).then_inc(reach("g_turned"), 1)
                if u >= 4:
                    pe.wait_ge(sig("weighted"), u - 3)
                pe.matmul(ps[:, 4 + u % 4, :], tile(xn_t)(u // B), w_exp_sb[:, (u % B) * 512:(u % B + 1) * 512],
                          start=True, stop=True).then_inc(sig("expert_done"), 1)
            pe.wait_ge(*after("g_t_ready"))
            pe.wait_ge(sig("b_exp_in"), 16)
            for h in range(2):
                mm = pe.matmul(ps[:, h, :], gates[:, 5 * P:6 * P], half(b_exp_sb, h), start=True, stop=True)
            mm.then_inc(reach("bias_done"), 1)
            pe.wait_ge(sig("normed"), 4)
            for j in range(TILES):
                mm = pe.matmul(ps[:, 2, 0:P], tile(xn)(j), tile(xn)(j), start=(j == 0), stop=(j == TILES - 1))
            mm.then_inc(sig("g_done"), 1)
            turn(tile(xn), 0)
            pe.wait_ge(sig("v_in"), 16)
            pe.wait_ge(sig("q_in"), 16)
            for l in range(LAYERS):
                for b in range(B):
                    pe.wait_ge(sig(f"g_ready_{b}"), l + 1)
                    mm = pe.matmul(ps[:, 3, b * 256:(b + 1) * 256], g_two[:, b, :], v_sb[:, l, :],
                                   start=True, stop=True)
                mm.then_inc(sig("t_done"), 1)
                pe.wait_ge(sig("t_out"), l + 1)
                t_pairs = t_sb.rearrange("p (b h e) -> p b h e", b=B, h=4)
                for h in range(4):
                    mm = pe.matmul(ps[:, 4, 0:P].rearrange("p (b e) -> p b e", b=B), q_sb[:, l, h, :],
                                   t_pairs[:, :, h, :], start=(h == 0), stop=(h == 3))
                mm.then_inc(sig("s_done"), 1)
                pe.wait_ge(sig("is_ready"), l + 1)
                if l < LAYERS - 1:
                    pe.matmul(ps[:, 5, 0:P], g_sb, is_sb, start=True, stop=True).then_inc(sig("gs_done"), 1)
                wait(pe, sig("wt_out"), l)
                pe.matmul(ps[:, 6, 0:P], is_sb, wt_sb if l else ident, start=True, stop=True).then_inc(sig("wt_done"), 1)
                if l < LAYERS - 1:
                    pe.wait_ge(sig("gs_out"), l + 1)
                    pe.matmul(ps[:, 7, 0:P], is_sb, u_sb, start=True, stop=True).then_inc(sig("g_done"), 1)
            pe.wait_ge(sig("wt_out"), LAYERS)
            pe.transpose(ps[:, 6, 0:P], wt_sb, ident).then_inc(reach("w_turned"), 1)
            pe.wait_ge(*after("w_out_ready"))
            pe.wait_ge(sig("turned_out"), 4)
            for j in range(TILES):
                mm = pe.matmul(ps[:, j // 4, (j % 4) * P:(j % 4 + 1) * P], tile(xn_t)(j), wt_sb, start=True, stop=True)
            mm.then_inc(reach("lin_out"), 1)
            pe.wait_ge(sig("normed"), 5)
            turn(tile(xn), 2)
            pe.wait_ge(sig("u_t_ready"), 2)
            pe.wait_ge(sig("xn_low"), 1)

            def convolve(k, a, s):
                if s == 0:
                    pe.wait_ge(sig("toep_low"), k + 1)
                if not isinstance(k, int) or k >= 1:
                    for b in range(B):
                        pe.wait_ge(sig(f"filtered_{b}"), 2 * k + s - 1)
                for t in range(2):
                    for q in range(4):
                        n, first, j = HALF - P * q, (0 if s == 0 else HALF + t), 2 * q + (t ^ s)
                        for i, (x_part, row_part) in enumerate(((0, 0), (0, 1), (1, 0))):
                            mm = pe.matmul(ps[:, 2 + 2 * s + t, P * q:HALF], xn_hl[:, x_part, j * P:(j + 1) * P],
                                           toep_hl[:, a, row_part, first:first + n],
                                           start=(q + i == 0), stop=(q == 3 and i == 2))
                mm.then_inc(sig("convolved"), 1)

            def mix(k, a, first=False):
                pe.wait_ge(sig("w_work_set"), k + 1)
                for b in range(B):
                    pe.wait_ge(sig(f"filtered_{b}"), 2 * k + 2)
                for g in (3, 2, 1, 0):
                    lo, hi = SPANS[g]
                    for b in range(B):
                        mm = pe.matmul(
                            ps[64 * b:64 * b + 64, lo // 256, :].rearrange(
                                "p (t n) -> p t n", t=2)[:, :, lo % 256:lo % 256 + hi - lo],
                            w_work[:, a, g * C:(g + 1) * C],
                            filt[:, a, b, :].rearrange("p (t n) -> p t n", t=2)[:, :, lo:hi],
                            start=first and g >= 2, stop=False, skip_group_check=True)
                mm.then_inc(sig("mixed"), 1)

            convolve(0, 0, 0)
            convolve(0, 0, 1)
            convolve(1, 1, 0)
            mix(0, 0, True)
            convolve(1, 1, 1)
            with pe.Fori(1, KF // 2) as pair:
                convolve(2 * pair, 0, 0)
                mix(2 * pair - 1, 1)
                convolve(2 * pair, 0, 1)
                convolve(2 * pair + 1, 1, 0)
                mix(2 * pair, 0)
                convolve(2 * pair + 1, 1, 1)
            mix(KF - 1, 1)
            pe.wait_ge(sig("ar_added"), 4)
            pe.wait_ge(sig("u_t_zero"), 1)
            for g in (3, 2, 1, 0):
                lo, hi = SPANS[g]
                bank, at = lo // 256, lo % 256
                out_v = ps[:, bank, :].rearrange("p (t n) -> p t n", t=2)[:, :, at:at + hi - lo]
                for a, dst, src in ((0, out_v, u_t[:, :, 1 + lo:1 + hi]), (2, out_v, u_t[:, :, lo:hi]),
                                    (1, out_v[:, 0, :], u_t[:, 1, lo:hi]), (1, out_v[:, 1, :], u_t[:, 0, 1 + lo:1 + hi])):
                    mm = pe.matmul(dst, w_ar[:, g, a, :], src, start=False, stop=(g % 2 == 0 and a == 1),
                                   skip_group_check=True)
            mm.then_inc(reach("ar_done"), 1)
            pe.wait_ge(*after("filters_out"))
            flat = y_back.rearrange("p (h t q n) -> p h t q n", h=2, t=2, q=2)
            for q in range(4):
                for t in range(2):
                    j = 2 * q + t
                    mm = pe.transpose(ps[:, 2 + j // 4, (j % 4) * P:(j % 4 + 1) * P], flat[:, q // 2, t, q % 2, :], ident)
                if q % 2 == 1:
                    mm.then_inc(sig("out_turned"), 1)


def constants():
    c = np.zeros((P, NCONST), np.float32)

    def part(name):
        return c[:, CONST[name][0]:CONST[name][1]]

    p = np.arange(P)
    part("ident")[:] = np.eye(P)
    for v in range(4):
        part("red")[:, v * 32:(v + 1) * 32] = (p[:, None] // NS + 8 * v) == np.arange(32)[None, :]
    sel = np.stack([(p[:, None] % 64 - 8 * v) == p[None, :] // NS for v in range(8)], 1).astype(np.float32)
    part("pair")[:] = 0.5 * (p[:, None] // 2 == p[None, :] // 2)
    part("mean")[:] = 1.0 / P
    part("heads")[:] = p[:, None] // DH == p[None, :] // DH
    part("rank")[:] = np.arange(E, 0, -1)
    part("sign")[:, 0] = np.where(p < C, 1, -1)
    q = np.arange(64)
    for r in range(2):
        part("split")[:, r * 64:(r + 1) * 64] = p[:, None] == (q // 32 * 64 + r * 32 + q % 32)[None, :]
        for h in range(2):
            at = part("merge")[64 * h:64 * h + 64, (2 * h + r) * P:(2 * h + r + 1) * P]
            at[:] = (q // 32 * 64 + r * 32 + q % 32)[:, None] == p[None, :]
    k, t = np.arange(KK), np.arange(L)
    at = (12 + k[:, None] // 7) * (t[None, :] // W) + (12 + k[:, None] % 7) * (t[None, :] % W)
    cos, sin = np.cos(2 * np.pi * at / 32), np.sin(2 * np.pi * at / 32)
    dft = np.stack([np.concatenate([cos, sin]), np.concatenate([-sin, cos])], 1)
    return c, sel.reshape(P, 8 * P), dft.astype(np.float32)


def layouts(i):
    two = lambda a: np.concatenate([a, a], 0)
    d = list(DIRS)

    def blocks(a):
        out = np.zeros((B, C) + a.shape[1:-1] + (B, a.shape[-1]), np.float32)
        for b in range(B):
            out[b, ..., b, :] = a
        return out.reshape((P,) + a.shape[1:-1] + (B * a.shape[-1],))

    def heads(a):
        return a.reshape(LAYERS, 4, 2, C, C).transpose(2, 4, 0, 1, 3).reshape(P, LAYERS, 4, C)

    w_qkv = i["L2_attn_w_in"].T
    consts, sel, dft = constants()
    vec = np.zeros((P, NVEC), np.float32)
    vec[:, V_CONVB] = i["L0_conv_conv_b"]
    vec[:, V_D:V_D + 4] = i["L0_conv_Ds"].reshape(4, DI).T
    vec[:, V_LNW] = i["L0_conv_ln_w"]
    vec[:, V_LNB] = i["L0_conv_ln_b"]
    for col, name in ((V_BF, "bf"), (V_BI, "bi"), (V_BD, "bd")):
        vec[:, col:col + 2] = np.tile(i["L1_conv_" + name].reshape(2, C2).T, (4, 1))
    rows = np.concatenate([i["L2_attn_b_out"], i["L2_attn_ln_w"], i["L2_ffn_router_b"],
                           i["L3_ffn_log_weights"], i["L3_ffn_gumbel"]])[None]
    xp = i["L0_conv_x_proj_w"][d]
    w_dt = np.stack([xp[:, :RANK].transpose(1, 0, 2), i["L0_conv_dt_w"][d].transpose(2, 0, 1)], 1)
    bc = xp[:, RANK:].reshape(ND, 2, 1, NS, DI)
    w_bc = np.broadcast_to(bc, (ND, 2, 8, NS, DI)).reshape(ND, 2, P, DI).transpose(3, 0, 1, 2)
    par = np.zeros((P, ND, 17), np.float32)
    rates = i["L0_conv_A_logs"].reshape(4, 4, 4, 8, NS)[d]
    par[:, :, 0:16] = rates.transpose(3, 4, 0, 2, 1).reshape(P, ND, 16)
    par[:, :, 16] = i["L0_conv_dt_b"][d].T
    w_gate = np.zeros((B, C, 3, 2, B, C2), np.float32)
    for g, name in enumerate(("Wf", "Wi", "Wd")):
        for b in range(B):
            w_gate[b, :, g, :, b, :] = i["L1_conv_" + name].reshape(C, 2, C2)
    ab = np.stack([np.concatenate([i[f"L1_conv_{n}_real"].reshape(C2, KK).T,
                                   i[f"L1_conv_{n}_imag"].reshape(C2, KK).T]) for n in "AB"], 1)
    b_expert = np.zeros((UN, E, UN, C), np.float32)
    for u in range(UN):
        b_expert[u, :, u, :] = i["L2_ffn_expert_b"]
    phi = np.zeros((KF, 2, 640), np.float32)
    phi[:, :, 128:] = i["L3_ffn_phi"][:L].reshape(HALF, 2, KF).transpose(2, 1, 0)
    m_phi = np.stack([i["L3_ffn_M_phi_plus"], i["L3_ffn_M_phi_minus"]], 1)
    return {
        "x_cm": i["x"].reshape(B, L, C).transpose(0, 2, 1).reshape(P, L),
        "consts": consts, "vec": vec, "rows": rows, "sel_c": sel,
        "w_in": two(i["L0_conv_w_in"].T),
        "conv_w": i["L0_conv_conv_w"].reshape(DI, 9).T.reshape(1, 9 * DI),
        "w_dt": w_dt, "w_bc": w_bc, "par": par,
        "w_out": i["L0_conv_w_out"].T,
        "w_gate": w_gate.reshape(P, 3, 2, 64), "ab": np.concatenate([ab, ab], 2), "dft": dft,
        "w_qv": blocks(np.concatenate([w_qkv[:, :P], w_qkv[:, 2 * P:]], 1)), "w_k": blocks(w_qkv[:, P:2 * P]),
        "w_attn": i["L2_attn_w_out"].T,
        "w_router": blocks(i["L2_ffn_router_w"]),
        "w_expert": blocks(i["L2_ffn_expert_w"].transpose(1, 0, 2).reshape(C, E * C)),
        "b_expert": b_expert.reshape(P, UN * C),
        "v_t": heads(i["L3_attn_v_matrix"]).reshape(P, LAYERS, 4 * C),
        "q_t": np.repeat(heads(i["L3_attn_q_matrix"])[:, :, :, None], 2, 3).reshape(P, LAYERS, 4, P),
        "phi": phi.reshape(2 * KF, 640), "sigma": np.repeat(i["L3_ffn_sigma"], 2)[:, None],
        "m_phi": two(m_phi.transpose(3, 0, 1, 2, 4).reshape(C, 4, 2, KF * C)),
        "m_u": blocks(i["L3_ffn_M_u"].transpose(2, 0, 1, 3)).reshape(P, 4, TAPS * P),
    }


_OUT = ((P, TILES * P), "float32")


def kernel(**inputs):
    import concourse.bacc as _bacc
    from concourse.bass_utils import run_bass_kernel_spmd as _run

    arrays = {f"in_{k}_dram": np.ascontiguousarray(v) for k, v in
              layouts({k: np.asarray(v) for k, v in inputs.items()}).items()}
    nc = _bacc.Bacc("TRN2", target_bir_lowering=False, num_devices=1)
    args = [nc.dram_tensor(k, a.shape, mybir.dt.from_np(a.dtype), kind="ExternalInput").ap()
            for k, a in arrays.items()]
    out = nc.dram_tensor("out_0_dram", _OUT[0], F32, kind="ExternalOutput").ap()
    program(nc, *args, out)
    got = _run(nc, [arrays], core_ids=[0]).results[0]["out_0_dram"]
    return got[::-1].reshape(P, 4, 2, B, C).transpose(3, 1, 0, 2, 4).reshape(B, H, W, C)
```

```python
from contextlib import ExitStack

import numpy as np

import concourse.bass as bass
from concourse import mybir

F32 = mybir.dt.float32
F32R = mybir.dt.float32r
ALU = mybir.AluOpType
ACT = mybir.ActivationFunctionType
AX = mybir.AxisListType
ADD, SUB, MUL, MAX, MIN = ALU.add, ALU.subtract, ALU.mult, ALU.max, ALU.min

P = 128
B, H, W, C = 2, 32, 32, 64
L = H * W
HALF = L // 2
DI, NS, RANK = 128, 16, 8
DIRS = (1, 2, 3, 0)
ND = len(DIRS)
GROUPS = DI // (P // NS)
UNITS = ND * B * GROUPS
PER = B * GROUPS
C2 = C // 2
KK = 49
HEADS, DH = 4, 32
TILES = 8
UN = TILES * B
E = 8
LAYERS, LH = 4, 8
KF = 16
TAPS = 3
TOE = 2 * HALF + 1
SPANS = ((0, 64), (64, 128), (128, 256), (256, 512))

LOG_RATE_MAX, STEP_MIN = 69.0, 1e-28

_o = 0
CONST = {}
for _name, _n in (("ident", P), ("pair", P), ("red", 4 * 32), ("mean", P), ("center", P),
                  ("heads", P), ("split", P), ("merge", 4 * P), ("rank", E), ("sign", 1)):
    CONST[_name] = (_o, _o + _n)
    _o += _n
NCONST = _o
V_CONVB, V_D, V_LNW, V_LNB, V_BF, V_BI, V_BD, V_BOUT, NVEC = 0, 1, 5, 6, 7, 9, 11, 13, 14
R_LNW, R_RB, R_LW, R_GU, NROW = 0, 64, 72, 76, 80

STEPS = {
    "gpsimd": ("eps_set", "taps_ready", "quarter", "phi_scaled", "sel_ready"),
    "scalar": ("pick_exp", "k_exp", "k_tok_ready", "r_exp", "g_t_ready",
              "w_out_ready"),
    "vector": ("pick_logits", "picked", "x2_ready", "k_max", "ctx_ready",
              "mix_ready", "attn_done", "r_shifted", "gates_ready", "moe_done", "zeroed", "lin_done"),
    "tensor": ("l1_done", "k_done", "k_turned", "ctx_done", "mix_done",
              "attn_out", "router_done", "g_turned", "bias_done", "w_turned", "lin_out"),
}


def wait(engine, sem, value):
    if isinstance(value, int) and value <= 0:
        return
    engine.wait_ge(sem, value)


def program(nc, x_cm, consts, vec, rows, sel_c, w_in, conv_w, w_dt, w_bc, par, w_out, w_gate, ab, dft,
            w_qv, w_k, w_attn, w_router, w_expert, b_expert, v_t, q_t, phi, sigma, m_phi, m_u, out):
    with ExitStack() as ctx:
        def sb(name, shape, dtype=F32):
            return ctx.enter_context(nc.sbuf_tensor(name, shape, dtype))

        sems = {}

        def sig(name):
            if name not in sems:
                sems[name] = ctx.enter_context(nc.semaphore(name))
            return sems[name]

        steps_made = {engine: 0 for engine in STEPS}

        def step_of(name):
            return next((engine, names.index(name) + 1) for engine, names in STEPS.items() if name in names)

        def reach(name):
            engine, value = step_of(name)
            steps_made[engine] += 1
            assert steps_made[engine] == value, name
            return sig(engine + "_steps")

        def after(name):
            engine, value = step_of(name)
            return sig(engine + "_steps"), value

        ps = ctx.enter_context(nc.psum_tensor("ps", [P, 8, HALF], F32))

        def banks(a, n=2):
            return ps[:, a:a + n, :].rearrange("p a n -> p (a n)")

        cst = sb("cst", [P, NCONST])
        vecs = sb("vecs", [P, NVEC])
        rowb = sb("rowb", [P, NROW])
        eps5 = sb("eps5", [P, 1])
        eps8 = sb("eps8", [P, 1])
        x_res = sb("x_res", [P, L])
        tok = sb("tok", [P, TILES, P])

        def con(name):
            return cst[:, CONST[name][0]:CONST[name][1]]

        ident = con("ident")
        sel = sb("sel", [P, 8, P], F32R)
        stack = sb("stack", [P, B, 2, 2, L], F32R)
        red = con("red").rearrange("p (v m) -> p v m", v=4)
        merge = con("merge").rearrange("p (h r m) -> p h r m", h=2, r=2)
        split = con("split").rearrange("p (r m) -> p r m", r=2)

        AREA = 36 * L + KF
        area = sb("area", [P, AREA])
        cut = [0]

        def take(n):
            a = cut[0]
            cut[0] += n
            assert cut[0] <= AREA, cut
            return area[:, a:a + n]

        xs = take(B * 4 * L).rearrange("p (b k n) -> p b k n", b=B, k=4)
        b_rep = take(B * L).rearrange("p (b n) -> p b n", b=B)
        c_rep = take(B * L).rearrange("p (b n) -> p b n", b=B)
        decay = take(2 * L).rearrange("p (s n) -> p s n", s=2)
        drive = take(4 * L).rearrange("p (s n) -> p s n", s=4)
        state = take(8 * L).rearrange("p (s n) -> p s n", s=8)
        tz, ta, te, tw = take(L), take(L), take(L), take(L)
        ysum = (tz, ta)
        tu = tok[:].rearrange("p j n -> p (j n)")
        high = lambda t: t.bitcast(F32R)
        spec = take(2 * L).rearrange("p (r n) -> p r n", r=4)
        ai2, bi2 = (take(L).rearrange("p (r n) -> p r n", r=2) for _ in range(2))
        w_all = take(ND * 3 * P).rearrange("p (k a m) -> p k a m", k=ND, a=3)
        w_now = take(3 * P).rearrange("p (a m) -> p a m", a=3)
        x_norm = state[:, 0, :]
        response = state[:, 6, :], state[:, 7, :]
        sel_in = drive[:, 2, :]
        w_dt_sb = drive[0:RANK, 3, :].rearrange("p (a k m) -> p a k m", a=2, k=ND)
        w_front = state[:, 2:4, :].rearrange("p s n -> p (s n)")[:, 0:11 * DI]
        w_taps, w_in_sb = w_front[:, 0:9 * DI], w_front[:, 9 * DI:]
        convw_b = state[:, 4:6, :].rearrange("p s n -> p (s n)")[:, 0:9 * DI]
        ab_sb = state[0:2 * KK, 4:6, :].rearrange("p s n -> p (s n)")[:, 9 * DI:9 * DI + P].rearrange(
            "p (f m) -> p f m", f=2)
        dft_sb = state[:, 6:8, :]
        cut[0] = 0
        xn1, sp_f, sp_i, sp_r, sp_a, sp_x, sp_d, sp_o, sp_v, sp_m, sp_n, sp_s = (take(L) for _ in range(12))
        cut[0] = 0
        toep = take(KF * TOE).rearrange("p (k n) -> p k n", k=KF)
        w_seg = take(KF * 256).rearrange("p (k n) -> p k n", k=KF)
        filt = take(4 * L).rearrange("p (a b n) -> p a b n", a=2, b=B)
        later = cut[0]
        m_in = [take(2 * L).rearrange("p (s n) -> p s n", s=2) for _ in range(2)]
        m_in += [area[:, a * L:(a + 2) * L].rearrange("p (s n) -> p s n", s=2) for a in (12, 14)]
        ln_c, ln_q, xn, xn_t = take(L), take(L), take(L), take(L)
        tail = cut[0]
        cut[0] = 0
        v_tok, q_e, q_t_sb, k_e, k_tok = (take(2 * L) for _ in range(5))
        cut[0] = tail
        w_qv_sb = take(2 * 256)
        w_k_sb = take(2 * P)
        w_attn_sb = take(C)
        ctx_m = take(P)
        mix_m = take(C)
        w_exp_sb = take(2 * 512)
        w_rt_sb = take(2 * E)
        b_exp_sb = take(UN * C)
        prods = (ln_q[:, 0:512], ln_q[:, 512:L], w_qv_sb, take(512))
        cut[0] = KF * TOE + 4 * L
        v_sb = take(LAYERS * 256).rearrange("p (l n) -> p l n", l=LAYERS)
        q_sb = take(LAYERS * 4 * P).rearrange("p (l h m) -> p l h m", l=LAYERS, h=4)
        gates = take(6 * P)
        g_two = take(2 * P).rearrange("p (b m) -> p b m", b=B)
        t_sb = ln_q[:, 0:512]
        g_sb, is_sb, u_sb, wt_sb = (ln_q[:, 512 + P * a:512 + P * (a + 1)] for a in range(4))
        cut[0] = later
        w_work = take(2 * 256).rearrange("p (a n) -> p a n", a=2)
        ar_in = take(4 * TAPS * P).rearrange("p (i n) -> p i n", i=4)
        w_ar = take(4 * TAPS * P).rearrange("p (g a m) -> p g a m", g=4, a=TAPS)
        y_back = ln_q
        cut[0] = tail
        u_t = take(2 * (HALF + 1)).rearrange("p (t n) -> p t n", t=2)
        fin = ln_c

        z_gate = sb("z_gate", [P, B, L])
        w_gate_sb = sb("w_gate_sb", [P, 3, 2, 64])
        par_sb = sb("par_sb", [P, ND, 17])
        par_now = sb("par_now", [P, 16])
        bias_now = sb("bias_now", [P, 1])
        w_out_sb = sb("w_out_sb", [P, C])
        small = sb("small", [P, 352])
        phi_sb = tok[0:2 * KF, 0:5, :].rearrange("p j n -> p (j n)")
        spare = stack[:].rearrange("p b w h n -> p (b w h n)")
        pads = [spare[:, 4 * L * b:4 * L * b + 34 * 34].rearrange("p (h w) -> p h w", h=34) for b in range(B)]
        front_hl = spare[:, 4 * L + 34 * 34:4 * L + 34 * 34 + 22 * DI].rearrange("p (s n) -> p s n", s=2)
        xn_hl = spare[:, 0:2 * L].rearrange("p (s n) -> p s n", s=2)
        toep_hl = spare[:, 2 * L:2 * L + 4 * TOE].rearrange("p (a s n) -> p a s n", a=2, s=2)
        sig_sb = sb("sig_sb", [2 * KF, 4])
        phi_dram = nc.dram_tensor("phi_scaled", [2 * KF, 640], F32)

        def chainer(engine, sem):
            count = [0]

            def link(ins, hold=True):
                count[0] += 1
                ins.then_inc(sem, 1)
                if hold:
                    engine.wait_ge(sem, count[0])
            return link

        HEAD = 8

        def scan_loop(engine, slot):
            for s in range(HEAD):
                slot(0, s)
            with engine.Fori(0, ND - 1) as k:
                for s in range(HEAD, PER):
                    slot(k, s)
                for s in range(HEAD):
                    slot(k + 1, s)
            for s in range(HEAD, PER):
                slot(ND - 1, s)

        def split_slot(k, s):
            b, i = divmod(s, GROUPS)
            return B * k + b, b, i

        def following(k, b):
            return (k, 1) if b == 0 else (k + 1, 0)

        def ends(k, b):
            return isinstance(k, int) and k == ND - 1 and b == B - 1

        def image_half(u):
            b, h = divmod(u, 2)
            return b, h, slice(h * HALF, (h + 1) * HALF)

        def in_image_order(b, d, h):
            if d == 1:
                return xs[:, b, 1, ::-1][:, h * HALF:(h + 1) * HALF]
            grid = xs[:, b, d, :].rearrange("p (w h) -> p h w", w=W)
            if d == 2:
                grid = grid[:, ::-1, ::-1]
            return grid[:, 16 * h:16 * h + 16, :]

        centered_bank = (6, 7, 2, 3)
        var_bank = (0, 1, 4, 5)

        POOL_COLS = 160

        def recurrence(engine, link, cols):
            def pairs(t):
                return t.rearrange("p (r n) -> p r n", r=2)[:, :, cols]

            width = cols.stop - cols.start
            f, i, r, x, d, o, v, m, n = (pairs(t) for t in (sp_f, sp_i, sp_r, sp_x, sp_d, sp_o, sp_v, sp_m, sp_n))
            s, lg = pairs(sp_s), pairs(sp_a)

            def both(t):
                return t.unsqueeze(1).broadcast_to([P, 2, width])

            def tt(out, a, b, op, hold=True):
                link(engine.tensor_tensor(out, a, b, op), hold)

            engine.wait_ge(sig("x_out"), 1)
            tt(m, both(spec[:, 2, cols]), x, MUL, False)
            tt(n, bi2[:, :, cols], x[:, ::-1, :], MUL)
            tt(m, m, n, ADD, False)
            if engine is nc.vector:
                engine.wait_ge(sig("gates_out"), 1)
                for half_r in range(2):
                    ins = engine.tensor_scalar(sp_r[:, half_r * HALF:(half_r + 1) * HALF], ps[:, 4 + half_r, :],
                                               vecs[:, V_BD + half_r:V_BD + half_r + 1], 0.0, ADD, MAX)
                ins.then_inc(sig("relu_out"), 1)
            engine.wait_ge(sig("relu_out"), 1)
            engine.wait_ge(sig("gates_out"), 2)
            tt(v, r, lg, ADD)
            engine.wait_ge(sig("gates_out"), 4)
            tt(v, v, i, MUL, False)
            tt(d, both(spec[:, 0, cols]), f, MUL, False)
            tt(o, ai2[:, :, cols], f, MUL)
            tt(v, v, m, MUL)
            mine = "diagonal_0" if engine is nc.vector else "diagonal_1"
            engine.sem_inc(sig(mine), 1)
            squared = pairs(xn1)
            for level in range(4):
                tt(m, d, v, MUL, False)
                tt(n, o, v[:, ::-1, :], MUL)
                tt(m, m, n, ADD)
                tt(v, v, m, ADD, level == 3)
                if level < 3:
                    tt(s[:, 0, :], d[:, 0, :], d[:, 1, :], ADD, False)
                    tt(s[:, 1, :], o[:, 0, :], o[:, 1, :], MUL)
                    tt(o, o, both(s[:, 0, :]), MUL, False)
                    engine.wait_ge(sig("squared"), level + 1)
                    tt(d, squared, both(s[:, 1, :]), ADD)
                    if level < 2:
                        engine.sem_inc(sig(mine), 1)

        def units(t):
            return t.rearrange("p (u c) -> p u c", u=UN)

        def over(t, n):
            return t.unsqueeze(2).broadcast_to([P, t.shape[1], n])

        tok_flat = tok[:].rearrange("p j n -> p (j n)")
        st_sum, st_var, st_rstd, st_dif = (small[:, a:a + UN] for a in (64, 80, 96, 112))
        bn = small[:, 256:352].rearrange("p (u s) -> p u s", u=UN)

        def norm_dve(dve, link, n, src, dst):
            for u in range(UN):
                ins = dve.bn_stats(bn[:, u, :], units(src)[:, u, :])
            link(ins)
            dve.tensor_tensor(st_sum, bn[:, :, 1], bn[:, :, 4], ADD)
            link(dve.tensor_tensor(st_dif, bn[:, :, 1], bn[:, :, 4], SUB), False)
            link(dve.tensor_tensor(st_var, bn[:, :, 2], bn[:, :, 5], ADD))
            link(dve.tensor_tensor(st_dif, st_dif, st_dif, MUL))
            dve.scalar_tensor_tensor(st_var, st_dif, C / 4, st_var, MUL, ADD).then_inc(sig("norm_var"), 1)
            link(dve.scalar_tensor_tensor(units(ln_c), over(st_sum, C), -0.5, units(src), MUL, ADD))
            dve.wait_ge(sig("norm_rstd"), n)
            dve.tensor_tensor(units(dst), units(ln_c), over(st_rstd, C), MUL).then_inc(sig("normed"), 1)

        def norm_act(act, link, n):
            act.wait_ge(sig("norm_var"), n)
            link(act.activation(st_rstd, st_var, ACT.Ln, bias=eps5[:], scale=1.0 / C))
            act.activation(st_rstd, st_rstd, ACT.Exp, scale=-0.5).then_inc(sig("norm_rstd"), 1)

        def filtered(engine, k, a, s):
            wait(engine, sig("convolved"), 2 * k + s + 1)
            if s == 0 and (not isinstance(k, int) or k >= 2):
                engine.wait_ge(sig("mixed"), k - 1)
            b = 0 if engine is nc.scalar else 1
            dst, src = filt[64 * s:64 * s + 64, a, b, :], banks(2 + 2 * s)[64 * b:64 * b + 64]
            if b == 0:
                engine.activation(dst, src, ACT.Copy).then_inc(sig("filtered_0"), 1)
            else:
                engine.tensor_copy(dst, src).then_inc(sig("filtered_1"), 1)

        def filter_loop(engine, split_rows):
            def pair_of(k0, more):
                for a in range(2):
                    for s in range(2):
                        filtered(engine, k0 + a, a, s)
                    if more:
                        split_rows(k0 + 2 + a, a)
            pair_of(0, True)
            with engine.Fori(1, KF // 2 - 1) as pair:
                pair_of(2 * pair, True)
            pair_of(KF - 2, False)

        def copy_g(engine, l, copy, src):
            b = 0 if engine is nc.vector else 1
            engine.wait_ge(sig("g_done"), l + 1)
            own = slice(64 * b, 64 * b + 64)
            extra = () if b == 0 else (ACT.Copy,)
            for row in range(2):
                at = slice(64 * row, 64 * row + 64)
                copy(g_two[at, b, at], src[own, own], *extra)
            copy(g_sb[own, own], src[own, own], *extra).then_inc(sig(f"g_ready_{b}"), 1)

        def back(engine):
            engine.wait_ge(sig("mixed"), KF)
            h = 0 if engine is nc.scalar else 1
            dst = y_back[:, h * HALF:(h + 1) * HALF].rearrange("p (g n) -> p g n", n=P)[:, :, ::-1]
            src = ps[:, h, :].rearrange("p (g n) -> p g n", n=P)
            if h == 0:
                engine.activation(dst, src, ACT.Copy).then_inc(sig("back_0"), 1)
            else:
                engine.tensor_copy(dst, src).then_inc(sig("back_1"), 1)

        block = ctx.enter_context(nc.Block())

        @block.sync
        def _(sp):
            def load(name, dst, src):
                sp.dma_start(dst, src).then_inc(sig(name), 16)

            load("x_in", x_res[:], x_cm)
            load("w_in_in", w_in_sb, w_in)
            load("pair_in", cst[:, 0:2 * P], consts[:, 0:2 * P])
            load("conv_w_in", convw_b, conv_w.broadcast_to([P, 9 * DI]))
            load("vecs_in", vecs[:], vec)
            load("par_in", par_sb[:], par)
            load("w_dt_in", w_dt_sb, w_dt)
            load("w_bc_in", w_all[:, :, 1:3, :], w_bc)
            load("ab_in", ab_sb, ab)
            load("dft_in", dft_sb[0:2 * KK, :, :], dft)
            load("sel_in", sel_in, sel_c)
            load("consts_in", cst[:, 2 * P:], consts[:, 2 * P:])
            load("rows_in", rowb[:], rows.broadcast_to([P, NROW]))
            load("filters_in", phi_sb, phi)
            load("filters_in", sig_sb[:, 0:1], sigma)
            load("out_gate_in", w_out_sb[:], w_out)
            load("out_gate_in", w_gate_sb[:], w_gate)

            sp.wait_ge(*after("phi_scaled"))
            sp.dma_start(phi_dram.ap(), phi_sb).then_inc(sig("phi_out"), 16)

            def restack(n, b):
                for what, (ready, parts) in enumerate((("delta_split", (ta, te)), ("u_split", (tu, tw)))):
                    wait(sp, sig(ready), n + 1)
                    if what == 0:
                        wait(sp, sig("steps_spread"), GROUPS * (n - 1))
                    for part, src in enumerate(parts):
                        for half in range(2):
                            sp.dma_start(stack[64 * part:64 * part + 64, b, what, half, :].bitcast(F32),
                                         src[64 * half:64 * half + 64]).then_inc(sig("stacked"), 16)

            for n in range(B * ND):
                restack(n, n % B)
            sp.wait_ge(sig("l0_half"), 2)
            for i in range(4):
                load("m_in", m_in[i], m_phi[:, i])
            load("linear_weights_in", v_sb, v_t)
            load("linear_weights_in", q_sb, q_t)
            sp.wait_ge(sig("dve_recurred"), 1)
            sp.wait_ge(sig("pool_recurred"), 1)
            load("token_weights_in", w_qv_sb, w_qv)
            load("token_weights_in", w_k_sb, w_k)
            load("token_weights_in", w_attn_sb, w_attn)
            load("token_weights_in", w_rt_sb, w_router)
            load("token_weights_in", w_exp_sb, w_expert)
            load("token_weights_in", b_exp_sb, b_expert)
            sp.wait_ge(sig("m_added"), 4)
            load("ar_in", ar_in, m_u)
            sp.wait_ge(*after("attn_done"))
            sp.wait_ge(sig("phi_out"), 16)
            for odd, cols in ((0, HALF), (1, HALF + 1)):
                src = bass.AP(phi_dram, 640 * odd + 1 - odd, [[1, P], [2 * 640, KF], [1, cols]])
                sp.dma_start(toep[:, :, odd * HALF:odd * HALF + cols], src).then_inc(sig("toep_in"), 16)
            for h in range(2):
                sp.wait_ge(sig("out_ready"), h + 1)
                sp.dma_start(out[:, h * HALF:(h + 1) * HALF], fin[:, h * HALF:(h + 1) * HALF]).then_inc(sig("stored"), 16)
            sp.wait_ge(sig("stored"), 32)

        @block.gpsimd
        def _(pool):
            link = chainer(pool, sig("pool_step"))
            for pad in pads:
                pool.memset(pad.bitcast(F32), 0.0)
            pool.memset(eps8[:], 1e-8)
            pool.memset(eps5[:], 1e-5).then_inc(reach("eps_set"), 1)
            pool.wait_ge(sig("w_in_in"), 16)
            pool.wait_ge(sig("conv_w_in"), 16)
            pool.tensor_tensor(w_taps.rearrange("p (t d) -> p t d", t=9), w_in_sb[:, 0:DI].unsqueeze(1).broadcast_to([P, 9, DI]),
                               convw_b.rearrange("p (t d) -> p t d", t=9), MUL).then_inc(reach("taps_ready"), 1)
            pool.memset(sig_sb[:, 1:2], 0.25).then_inc(reach("quarter"), 1)
            pool.wait_ge(*after("quarter"))
            pool.wait_ge(sig("filters_in"), 32)
            link(pool.tensor_tensor(sig_sb[:, 2:3], sig_sb[:, 0:1], sig_sb[:, 1:2], ALU.pow))
            pool.tensor_scalar(phi_sb, phi_sb, sig_sb[:, 2:3], None, MUL).then_inc(reach("phi_scaled"), 1)
            pool.wait_ge(sig("sel_in"), 16)
            pool.tensor_copy(sel[:].rearrange("p v m -> p (v m)"), sel_in).then_inc(reach("sel_ready"), 1)
            def rest(n):
                wait(pool, sig("w_rest"), n + 1)
                pool.tensor_tensor(te, te, tw, ADD).then_inc(sig("rest_ready"), 1)

            def low(n):
                wait(pool, sig("delta_high"), n + 1)
                pool.tensor_tensor(high(te), tz, ta, SUB).then_inc(sig("delta_split"), 1)

            def slot(k, s):
                n, b, i = split_slot(k, s)
                if ends(k, b) and i >= GROUPS - 2:
                    return
                if i == 0:
                    wait(pool, sig("c_ready"), n + 1)
                wait(pool, sig("scanned"), GROUPS * n + i + 1)
                pool.tensor_tensor(state[:, i % 8, :], state[:, i % 8, :], c_rep[:, b, :],
                                   MUL).then_inc(sig("weighed"), 1)
                if i == 5 and not ends(k, b):
                    rest(n + 1)
                if i == 7 and not ends(k, b):
                    low(n + 1)

            rest(0)
            low(0)
            for dst, r, ready in ((bi2, 3, "spec_out"), (ai2, 1, "spec_ready")):
                pool.wait_ge(sig(ready), 1)
                pool.tensor_scalar(dst[:, 0, :], spec[:, r, :], -1.0, None, MUL)
                pool.tensor_copy(dst[:, 1, :], spec[:, r, :]).then_inc(sig("signed"), 1)
            scan_loop(pool, slot)
            recurrence(pool, link, slice(HALF - POOL_COLS, HALF))
            pool.sem_inc(sig("pool_recurred"), 1)
            def of_span(g):
                return w_seg.rearrange("p k (g e) -> p k g e", g=4)[:, :, g, :]

            for i in range(4):
                plus, minus = (m_in[i][:, s].rearrange("p (k e) -> p k e", k=KF) for s in range(2))
                pool.wait_ge(sig("m_weighted"), 2 * (i + 1))
                ins = pool.tensor_tensor(of_span(3 - i), plus, minus, ADD)
                if i:
                    link(ins)
                    ins = pool.tensor_tensor(of_span(3 - i), of_span(3 - i), of_span(4 - i), ADD)
                ins.then_inc(sig("m_added"), 1)
            for n, u in enumerate(range(1, UN, 2)):
                pool.wait_ge(sig("weighted"), u + 1)
                part = prods[u % 4]
                link(pool.tensor_tensor(part[:, 0:4 * C], part[:, 0:4 * C], part[:, 4 * C:8 * C], ADD))
                link(pool.tensor_tensor(part[:, 0:2 * C], part[:, 0:2 * C], part[:, 2 * C:4 * C], ADD))
                pool.tensor_tensor(units(xn)[:, u, :], part[:, 0:C], part[:, C:2 * C], ADD).then_inc(sig("odd_sum"), 1)
            for i in range(4):
                pool.wait_ge(sig("ar_weighted"), i + 1)
                new = w_ar[:, 3 - i].rearrange("p a m -> p (a m)")
                if i == 0:
                    pool.tensor_copy(new, ar_in[:, 0, :]).then_inc(sig("ar_added"), 1)
                else:
                    pool.wait_ge(sig("ar_added"), i)
                    pool.tensor_tensor(new, w_ar[:, 4 - i].rearrange("p a m -> p (a m)"), ar_in[:, i, :],
                                       ADD).then_inc(sig("ar_added"), 1)
            pool.wait_ge(*after("lin_done"))
            pool.memset(u_t[:, :, 0:1], 0.0).then_inc(sig("u_t_zero"), 1)

            def weights(k, a):
                if not isinstance(k, int) or k >= 2:
                    pool.wait_ge(sig("mixed"), k - 1)
                pool.tensor_copy(w_work[:, a:a + 1, :], w_seg[:, bass.ds(k, 1), :]).then_inc(sig("w_work_set"), 1)

            pool.wait_ge(sig("m_added"), 4)
            for a in range(2):
                weights(a, a)
            with pool.Fori(1, KF // 2) as pair:
                for a in range(2):
                    weights(2 * pair + a, a)

        @block.scalar
        def _(act):
            link = chainer(act, sig("act_step"))
            act.preload_act_table_set("natural_log_exp_and_others")
            act.wait_ge(*after("eps_set"))
            act.wait_ge(sig("gn_var"), 1)
            link(act.activation(small[:, 4:5], small[:, 3:4], ACT.Ln, bias=eps5[:]))
            act.activation(small[:, 5:6], small[:, 4:5], ACT.Exp, scale=-0.5).then_inc(sig("gn_rstd"), 1)
            act.wait_ge(sig("gn_out"), 1)
            for b in range(B):
                own = slice(64 * b, 64 * b + 64)
                act.activation(pads[b][own, 1:33, 1:33], x_norm[own].rearrange("p (h w) -> p h w", h=H),
                               ACT.Copy).then_inc(sig("x_high"), 1)
            act.wait_ge(*after("taps_ready"))
            act.activation(front_hl[:, 0, :], w_front, ACT.Copy).then_inc(sig("front_high"), 1)
            act.wait_ge(sig("w_dt_done"), 1)
            act.activation(w_all[:, :, 0, :], ps[:, 6, :].rearrange("p (a m) -> p a m", a=ND),
                           ACT.Copy).then_inc(sig("w_dt_ready"), 1)
            act.wait_ge(sig("par_min"), 1)
            act.activation(par_sb[:, :, 0:16], par_sb[:, :, 0:16], ACT.Exp).then_inc(sig("par_exp"), 1)

            act.wait_ge(*after("pick_logits"))
            act.activation(small[:, 40:44], small[:, 36:40], ACT.Exp, bias=small[:, 45:46]).then_inc(reach("pick_exp"), 1)

            def set_weights(k):
                act.activation(w_now.unsqueeze(1), w_all[:, bass.ds(k, 1), :, :],
                               ACT.Copy).then_inc(sig("w_now_set"), 1)
                act.activation(bias_now[:].unsqueeze(1), par_sb[:, bass.ds(k, 1), 16:17],
                               ACT.Copy).then_inc(sig("bias_set"), 1)

            def set_rates(k):
                wait(act, sig("decayed"), PER * k)
                act.activation(par_now[:].unsqueeze(1), par_sb[:, bass.ds(k, 1), 0:16],
                               ACT.Copy).then_inc(sig("rates_set"), 1)

            def soft(n, k, b, step):
                if step == "z":
                    wait(act, sig("projected"), 3 * n + 1)
                    wait(act, sig("stacked"), 128 * n)
                    wait(act, sig("bias_set"), k + 1)
                    act.activation(tz, banks(6), ACT.Identity, bias=bias_now[:]).then_inc(sig("tz_ready"), 1)
                    act.activation(ta, banks(6), ACT.Abs, bias=bias_now[:]).then_inc(sig("abs_ready"), 1)
                elif step == "exp":
                    wait(act, sig("abs_ready"), n + 1)
                    act.activation(te, ta, ACT.Exp, scale=-1.0).then_inc(sig("exp_ready"), 1)
                elif step == "one_plus":
                    wait(act, sig("exp_ready"), n + 1)
                    act.activation(tw, te, ACT.Identity, bias=1.0).then_inc(sig("w_ready"), 1)
                elif step == "log":
                    wait(act, sig("w_ready"), n + 1)
                    act.activation(ta, tw, ACT.Ln).then_inc(sig("log_ready"), 1)
                elif step == "rest":
                    wait(act, sig("log_ready"), n + 1)
                    act.activation(tw, tw, ACT.Identity, bias=1.0, scale=-1.0).then_inc(sig("w_rest"), 1)
                elif step == "b":
                    wait(act, sig("projected"), 3 * n + 2)
                    act.activation(b_rep[:, b, :], banks(6), ACT.Copy).then_inc(sig("b_ready"), 1)
                elif step == "delta":
                    wait(act, sig("delta_ready"), n + 1)
                    act.activation(high(ta), tz, ACT.Copy).then_inc(sig("delta_high"), 1)
                elif step == "u":
                    wait(act, sig("u_ready"), n + 1)
                    act.activation(high(tu), tw, ACT.Copy).then_inc(sig("u_high"), 1)
                elif step == "c":
                    wait(act, sig("projected"), 3 * n + 3)
                    act.activation(c_rep[:, b, :], banks(6), ACT.Copy).then_inc(sig("c_ready"), 1)

            soft_at = {2: ["z"], 3: ["exp"], 4: ["one_plus"], 5: ["log"], 6: ["rest", "b"], 8: ["delta"],
                       9: ["u"], 14: ["c"]}

            def slot(k, s):
                n, b, i = split_slot(k, s)
                wait(act, sig("steps_spread"), GROUPS * n + i + 1)
                wait(act, sig("scanned"), GROUPS * n + i - 1)
                if s == 0:
                    wait(act, sig("rates_set"), k + 1)
                act.activation(decay[:, i % 2, :], banks(0), ACT.Exp,
                               scale=par_now[:, i:i + 1]).then_inc(sig("decayed"), 1)
                nk, nb = following(k, b)
                for step in soft_at.get(i, []) if not ends(k, b) else []:
                    soft(n + 1, nk, nb, step)
                if i == 4:
                    pk, pb = (k - 1, 1) if b == 0 else (k, 0)
                    if not isinstance(pk, int) or 0 <= pk < ND - 1:
                        wait(act, sig("summed"), 4 * n)
                        act.activation(xs[:, pb, bass.ds(pk, 1), :], banks(4).unsqueeze(1),
                                       ACT.Copy).then_inc(sig("y_free"), 1)
                if s == 14 and not (isinstance(k, int) and k == ND - 1):
                    set_weights(k + 1)
                if s == PER - 1 and not (isinstance(k, int) and k == ND - 1):
                    set_rates(k + 1)

            act.wait_ge(sig("w_bc_in"), 16)
            act.wait_ge(sig("w_dt_ready"), 1)
            act.wait_ge(sig("par_neg"), 1)
            set_weights(0)
            set_rates(0)
            act.preload_act_table_set("silu_and_others")
            act.wait_ge(sig("vecs_in"), 16)

            def conv_out(b):
                act.wait_ge(sig("conv_done"), b + 1)
                act.activation(xs[:, b, 3, :], banks(0), ACT.Silu,
                               bias=vecs[:, V_CONVB:V_CONVB + 1]).then_inc(sig("xc_ready"), 1)

            def gate_out(b):
                act.wait_ge(sig("z_done"), b + 1)
                act.activation(z_gate[:, b, :], banks(6), ACT.Silu).then_inc(sig("z_ready"), 1)

            conv_out(0)
            gate_out(0)
            act.preload_act_table_set("natural_log_exp_and_others")
            for step in ("z", "exp", "one_plus", "log", "rest", "b"):
                soft(0, 0, 0, step)
            act.wait_ge(sig("spec_done"), 1)
            act.activation(spec[:, 0:2, :], ps[:, 2:4, :], ACT.Copy)
            act.activation(spec[:, 2:4, :], ps[:, 4:6, :], ACT.Copy, scale=0.1).then_inc(sig("spec_out"), 1)
            act.wait_ge(sig("spec_out"), 1)
            act.activation(response[0], spec[:, 0:2, :].rearrange("p r n -> p (r n)"),
                           ACT.Square).then_inc(sig("spec_sq"), 1)
            act.wait_ge(sig("phi_out"), 16)
            for step in ("delta", "u", "c"):
                soft(0, 0, 0, step)
            act.preload_act_table_set("silu_and_others")
            conv_out(1)
            gate_out(1)
            act.preload_act_table_set("natural_log_exp_and_others")
            act.sem_inc(sig("y_free"), 1)
            act.wait_ge(sig("mag_sq"), 1)
            mag, scale, scale_b = response[0][:, 0:HALF], response[1][:, 0:HALF], response[1][:, HALF:L]
            link(act.activation(scale, mag, ACT.Ln, bias=eps8[:]))
            link(act.activation(mag, scale, ACT.Exp, scale=0.5))
            act.activation(scale_b, mag, ACT.Ln, bias=eps8[:])
            link(act.activation(scale, mag, ACT.Exp, scale=-1.0))
            act.activation(scale, scale, ACT.Ln, bias=1.0).then_inc(sig("scale_logs"), 1)
            act.wait_ge(sig("scale_sum"), 1)
            act.activation(scale, scale, ACT.Exp, scale=-1.0).then_inc(sig("scale_exp"), 1)
            scan_loop(act, slot)
            squares = (te, tw)

            def square(u):
                b, h, cols = image_half(u)
                act.wait_ge(sig("y_centered"), u + 1)
                act.activation(squares[b][:, cols], ps[:, centered_bank[u], :], ACT.Square).then_inc(sig("y_squares"), 1)

            def root(u):
                b, h, cols = image_half(u)
                act.wait_ge(sig("y_var"), u + 1)
                link(act.activation(squares[b][:, cols], ps[:, var_bank[u], :], ACT.Ln, bias=eps5[:]))
                act.activation(squares[b][:, cols], squares[b][:, cols], ACT.Exp, scale=-0.5).then_inc(sig("y_rstd"), 1)

            def affine(u):
                b, h, cols = image_half(u)
                act.wait_ge(sig("y_normed"), u + 1)
                act.activation(ysum[b][:, cols], ysum[b][:, cols], ACT.Identity, bias=vecs[:, V_LNB:V_LNB + 1],
                               scale=vecs[:, V_LNW:V_LNW + 1]).then_inc(sig("y_affine"), 1)

            for step, u in ((square, 0), (square, 1), (root, 0), (root, 1), (affine, 0), (square, 2), (affine, 1),
                            (square, 3), (root, 2), (root, 3), (affine, 2), (affine, 3)):
                step(u)
            act.wait_ge(sig("gn_var"), 2)
            link(act.activation(small[:, 4:5], small[:, 3:4], ACT.Ln, bias=eps5[:]))
            act.activation(small[:, 5:6], small[:, 4:5], ACT.Exp, scale=-0.5).then_inc(sig("gn_rstd"), 1)

            def pairs(t):
                return t.rearrange("p (r n) -> p r n", r=2)

            act.wait_ge(sig("gates_done"), 2)
            for r in range(2):
                bias = vecs[:, V_BD + r:V_BD + r + 1]
                ins = act.activation(pairs(sp_a)[:, r, :], ps[:, 4 + r, :], ACT.Abs, bias=bias)
            ins.then_inc(sig("gates_out"), 1)
            act.wait_ge(sig("gates_out"), 1)
            link(act.activation(sp_a, sp_a, ACT.Exp, scale=-1.0))
            act.activation(sp_a, sp_a, ACT.Ln, bias=1.0).then_inc(sig("gates_out"), 1)
            act.preload_act_table_set("sigmoid_and_others")
            for g, (dst, col) in enumerate(((sp_f, None), (sp_i, V_BI))):
                act.wait_ge(sig("gates_done"), 3 + g)
                for r in range(2):
                    bias = small[:, 26 + r:27 + r] if col is None else vecs[:, col + r:col + r + 1]
                    ins = act.activation(pairs(dst)[:, r, :], ps[:, 2 * g + r, :], ACT.Sigmoid, bias=bias)
                ins.then_inc(sig("gates_out"), 1)
            act.preload_act_table_set("natural_log_exp_and_others")
            act.wait_ge(sig("m_in"), 64)
            act.wait_ge(*after("picked"))
            for i in range(4):
                if i < 3:
                    act.wait_ge(sig("diagonal_0"), i + 1)
                    act.wait_ge(sig("diagonal_1"), i + 1)
                    act.activation(xn1, sp_d, ACT.Square).then_inc(sig("squared"), 1)
                for s in range(2):
                    at = 56 + 4 * s + i
                    act.activation(m_in[i][:, s], m_in[i][:, s], ACT.Copy,
                                   scale=small[:, at:at + 1]).then_inc(sig("m_weighted"), 1)

            def to_tokens(n, dst, first=2):
                for h in range(2):
                    act.wait_ge(sig("turned"), 2 * n - 1 + h)
                    act.activation(dst[:, h * HALF:(h + 1) * HALF], ps[:, first + h, :],
                                   ACT.Copy).then_inc(sig("turned_out"), 1)

            to_tokens(1, tok_flat)
            norm_act(act, link, 1)
            to_tokens(2, xn_t, 0)
            act.wait_ge(*after("k_max"))
            act.activation(k_e, ps[:, 4:8, :].rearrange("p a n -> p (a n)"), ACT.Exp, bias=small[:, 129:130],
                           accum_out=small[:, 130:131]).then_inc(reach("k_exp"), 1)
            def v_and_q(h):
                act.wait_ge(sig("qv_done"), h + 1)
                act.activation(v_tok[:, h * L:(h + 1) * L], banks(2), ACT.Copy).then_inc(sig("v_out"), 1)
                act.wait_ge(sig("q_shifted"), h + 1)
                act.activation(q_e[:, h * L:(h + 1) * L], q_e[:, h * L:(h + 1) * L], ACT.Exp).then_inc(sig("q_exp"), 1)

            v_and_q(0)
            act.wait_ge(*after("k_turned"))
            act.activation(k_tok, ps[:, 4:8, :].rearrange("p a n -> p (a n)"), ACT.Copy).then_inc(reach("k_tok_ready"), 1)
            v_and_q(1)
            for h in range(2):
                act.wait_ge(sig("q_turned"), h + 1)
                act.activation(q_t_sb[:, h * L:(h + 1) * L], banks(2 * h), ACT.Copy).then_inc(sig("q_t_ready"), 1)
            for h in range(2):
                act.wait_ge(sig("attended"), h + 1)
                act.activation(xn[:, h * HALF:(h + 1) * HALF], ps[:, 6 + h, :], ACT.Identity,
                               bias=vecs[:, V_BOUT:V_BOUT + 1]).then_inc(sig("attended_out"), 1)
            norm_act(act, link, 2)
            norm_act(act, link, 3)
            to_tokens(3, xn_t, 0)
            act.wait_ge(*after("r_shifted"))
            act.activation(gates[:, 0:P], gates[:, 0:P], ACT.Exp).then_inc(reach("r_exp"), 1)
            act.wait_ge(*after("g_turned"))
            act.activation(gates[:, 5 * P:6 * P], ps[:, 3, 0:P], ACT.Copy).then_inc(reach("g_t_ready"), 1)
            norm_act(act, link, 4)
            to_tokens(4, xn_t, 0)
            act.wait_ge(*after("zeroed"))
            copy_g(act, 0, act.activation, ps[:, 2, 0:P])
            for l in range(LAYERS):
                act.wait_ge(sig("t_done"), l + 1)
                act.activation(t_sb, ps[:, 3, :], ACT.Copy).then_inc(sig("t_out"), 1)
                act.wait_ge(sig("wt_done"), l + 1)
                act.activation(wt_sb, ps[:, 6, 0:P], ACT.Copy).then_inc(sig("wt_out"), 1)
                if l == 0:
                    act.wait_ge(sig("ar_in"), 16)
                    for i in range(4):
                        act.activation(ar_in[:, i, :], ar_in[:, i, :], ACT.Copy,
                                       scale=small[:, 56 + i:57 + i]).then_inc(sig("ar_weighted"), 1)
                if l < LAYERS - 1:
                    copy_g(act, l + 1, act.activation, ps[:, 7, 0:P])
            act.wait_ge(*after("w_turned"))
            act.activation(wt_sb, ps[:, 6, 0:P], ACT.Copy).then_inc(reach("w_out_ready"), 1)
            def toep_high(k, a):
                if not isinstance(k, int) or k >= 2:
                    act.wait_ge(sig("convolved"), 2 * k - 2)
                act.activation(toep_hl[:, a, 0:1, :], toep[:, bass.ds(k, 1), :], ACT.Copy).then_inc(sig("toep_high"), 1)

            act.wait_ge(sig("toep_in"), 32)
            for a in range(2):
                toep_high(a, a)
            norm_act(act, link, 5)
            act.wait_ge(sig("normed"), 5)
            act.activation(xn_hl[:, 0, :], xn, ACT.Copy).then_inc(sig("xn_high"), 1)
            act.wait_ge(sig("turned"), 10)
            for t in range(2):
                act.activation(u_t[:, t, 1:HALF + 1].rearrange("p (q n) -> p q n", q=4),
                               banks(0).rearrange("p (q t n) -> p t q n", q=4, t=2)[:, t, :, ::-1],
                               ACT.Copy).then_inc(sig("u_t_ready"), 1)
            filter_loop(act, toep_high)
            back(act)

        @block.vector
        def _(dve):
            link = chainer(dve, sig("dve_step"))
            pair_ps = ps[:, 7, 0:2]

            def group_norm(x, n):
                for h in range(2):
                    link(dve.bn_stats(small[:, 8 + 6 * h:14 + 6 * h], x[:, h * HALF:(h + 1) * HALF]))
                dve.bn_aggr(small[:, 0:2], small[:, 8:20]).then_inc(sig("gn_stats"), 1)
                dve.wait_ge(sig("gn_pair"), n)
                link(dve.tensor_copy(small[:, 20:22], pair_ps))
                link(dve.tensor_tensor(small[:, 2:3], small[:, 0:1], small[:, 20:21], SUB))
                dve.scalar_tensor_tensor(small[:, 3:4], small[:, 2:3], small[:, 2:3], small[:, 21:22],
                                         MUL, ADD).then_inc(sig("gn_var"), 1)
                dve.wait_ge(sig("gn_rstd"), n)

            dve.wait_ge(sig("x_in"), 16)
            group_norm(x_res, 1)
            dve.tensor_scalar(x_norm, x_res[:], small[:, 20:21], small[:, 5:6], SUB, MUL).then_inc(sig("gn_out"), 1)
            for b in range(B):
                own, other = slice(64 * b, 64 * b + 64), slice(64 * (1 - b), 64 * (1 - b) + 64)
                dve.wait_ge(sig("x_high"), b + 1)
                dve.tensor_tensor(pads[b][other, 1:33, 1:33], x_norm[own].rearrange("p (h w) -> p h w", h=H),
                                  pads[b][own, 1:33, 1:33].bitcast(F32), SUB).then_inc(sig("x_low"), 1)
            dve.wait_ge(sig("front_high"), 1)
            dve.tensor_tensor(front_hl[:, 1, :], w_front, front_hl[:, 0, :].bitcast(F32), SUB).then_inc(sig("front_low"), 1)
            dve.wait_ge(sig("par_in"), 16)
            rates = par_sb[:, :, 0:16]
            dve.tensor_scalar(rates, rates, LOG_RATE_MAX, None, MIN).then_inc(sig("par_min"), 1)
            dve.wait_ge(sig("par_exp"), 1)
            dve.tensor_scalar(rates, rates, -1.0, None, MUL).then_inc(sig("par_neg"), 1)
            dve.wait_ge(sig("vecs_in"), 16)
            link(dve.tensor_reduce(small[:, 24:25], vecs[:, V_D:V_D + 4], AX.X, ADD))
            link(dve.tensor_scalar(small[:, 26:28], vecs[:, V_BF:V_BF + 2], 2.0, None, ADD))
            logits, peak, probs, hard = small[:, 36:40], small[:, 44:45], small[:, 40:44], small[:, 48:52]
            rank = con("rank")
            dve.wait_ge(sig("rows_in"), 16)
            dve.wait_ge(sig("consts_in"), 16)
            link(dve.tensor_tensor(logits, rowb[:, R_LW:R_LW + 4], rowb[:, R_GU:R_GU + 4], ADD))
            link(dve.tensor_reduce(peak, logits, AX.X, MAX))
            dve.tensor_scalar(small[:, 45:46], peak, -1.0, None, MUL).then_inc(reach("pick_logits"), 1)
            dve.wait_ge(*after("pick_exp"))
            link(dve.tensor_reduce(peak, probs, AX.X, ADD))
            link(dve.reciprocal(peak, peak))
            link(dve.tensor_scalar(probs, probs, peak, None, MUL))
            link(dve.tensor_reduce(peak, probs, AX.X, MAX))
            link(dve.tensor_scalar(hard, probs, peak, None, ALU.is_equal))
            link(dve.tensor_tensor(hard, hard, rank[:, 4:8], MUL))
            link(dve.tensor_reduce(peak, hard, AX.X, MAX))
            link(dve.tensor_scalar(hard, hard, peak, None, ALU.is_equal))
            link(dve.tensor_tensor(hard, hard, probs, SUB))
            link(dve.tensor_tensor(small[:, 56:60], hard, probs, ADD))
            dve.tensor_scalar(small[:, 60:64], small[:, 56:60], con("sign"), None, MUL).then_inc(reach("picked"), 1)

            def finish_soft(n, k, b, step):
                if step == 0:
                    wait(dve, sig("tz_ready"), n + 1)
                    wait(dve, sig("log_ready"), n + 1)
                    dve.scalar_tensor_tensor(tz, tz, STEP_MIN, ta, MAX, ADD).then_inc(sig("soft_sum"), 1)
                elif step == 1:
                    wait(dve, sig("soft_sum"), n + 1)
                    wait(dve, sig("rest_ready"), n + 1)
                    dve.tensor_tensor(tz, tz, te, ADD).then_inc(sig("delta_ready"), 1)
                elif step == 2:
                    wait(dve, sig("delta_ready"), n + 1)
                    dve.tensor_tensor(tw.unsqueeze(1), tz.unsqueeze(1),
                                      xs[:, b, bass.ds(k, 1), :], MUL).then_inc(sig("u_ready"), 1)
                elif step == 3:
                    wait(dve, sig("u_high"), n + 1)
                    dve.tensor_tensor(high(tw), tw, tu, SUB).then_inc(sig("u_split"), 1)

            def drive_unit(n, b, i):
                if i == 0:
                    wait(dve, sig("b_ready"), n + 1)
                wait(dve, sig("drives_spread"), GROUPS * n + i + 1)
                wait(dve, sig("scanned"), GROUPS * n + i - 3)
                dve.tensor_tensor(drive[:, i % 4, :], banks(2), b_rep[:, b, :], MUL).then_inc(sig("driven"), 1)

            def slot(k, s):
                n, b, i = split_slot(k, s)
                nk, nb = following(k, b)
                if i < GROUPS - 1:
                    drive_unit(n, b, i + 1)
                elif not ends(k, b):
                    drive_unit(n + 1, nb, 0)
                wait(dve, sig("decayed"), GROUPS * n + i + 1)
                wait(dve, sig("driven"), GROUPS * n + i + 1)
                wait(dve, sig("summed"), 4 * n + i // 4 - 1)
                dve.tensor_tensor_scan(state[:, i % 8, :], decay[:, i % 2, :], drive[:, i % 4, :], 0.0,
                                       MUL, ADD).then_inc(sig("scanned"), 1)
                if i in (6, 7, 8, 10) and not ends(k, b):
                    finish_soft(n + 1, nk, nb, {6: 0, 7: 1, 8: 2, 10: 3}[i])
                if isinstance(k, int) and k == ND - 1 and s == GROUPS + 4:
                    dve.wait_ge(sig("summed"), 4 * (B * ND - 1))
                    dve.scalar_tensor_tensor(ysum[0], xs[:, 0, 3, :], small[:, 24:25], banks(4),
                                             MUL, ADD).then_inc(sig("y_last"), 1)

            def scan_orders(b):
                dve.wait_ge(sig("xc_ready"), b + 1)
                nat = xs[:, b, 3, :]
                turned_grid = nat.rearrange("p (h w) -> p w h", h=H)
                dve.tensor_copy(xs[:, b, 0, :].rearrange("p (w h) -> p w h", w=W), turned_grid)
                dve.tensor_copy(xs[:, b, 1, :], nat[:, ::-1])
                dve.tensor_copy(xs[:, b, 2, :].rearrange("p (w h) -> p w h", w=W),
                                turned_grid[:, ::-1, ::-1]).then_inc(sig("orders_ready"), 1)

            scan_orders(0)
            dve.wait_ge(sig("orders_ready"), 1)
            for step in range(3):
                finish_soft(0, 0, 0, step)
            pair_sum = lambda t: dve.tensor_tensor(t[:, 0:HALF], t[:, 0:HALF], t[:, HALF:L], ADD)
            dve.wait_ge(sig("spec_sq"), 1)
            pair_sum(response[0]).then_inc(sig("mag_sq"), 1)
            finish_soft(0, 0, 0, 3)
            scan_orders(1)
            dve.wait_ge(sig("z_done"), 2)
            drive_unit(0, 0, 0)
            dve.wait_ge(sig("scale_logs"), 1)
            pair_sum(response[1]).then_inc(sig("scale_sum"), 1)
            dve.wait_ge(sig("scale_exp"), 1)
            for r in range(2):
                ins = dve.scalar_tensor_tensor(spec[:, r, :], response[1][:, 0:HALF], 0.95, spec[:, r, :], MUL, MUL)
            ins.then_inc(sig("spec_ready"), 1)
            scan_loop(dve, slot)
            for i in (GROUPS - 2, GROUPS - 1):
                dve.wait_ge(sig("scanned"), UNITS)
                dve.tensor_tensor(state[:, i % 8, :], state[:, i % 8, :], c_rep[:, 1, :],
                                  MUL).then_inc(sig("weighed_last"), 1)
            dve.wait_ge(sig("y_free"), B * (ND - 1) + 1)
            dve.wait_ge(sig("summed"), 4 * B * ND)
            for h in range(2):
                _, _, cols = image_half(2 + h)
                y = ysum[1][:, cols]
                grid = y.rearrange("p (h w) -> p h w", w=W)
                flipped, turned, turned_back = (in_image_order(1, d, h) for d in (1, 0, 2))
                link(dve.scalar_tensor_tensor(y, xs[:, 1, 3, cols], small[:, 24:25], ps[:, 4 + h, :], MUL, ADD))
                link(dve.tensor_tensor(y, y, flipped, ADD))
                link(dve.tensor_tensor(grid, grid, turned, ADD))
                dve.tensor_tensor(grid, grid, turned_back, ADD).then_inc(sig("y_ready"), 1)

            def normalise(u):
                b, h, cols = image_half(u)
                dve.wait_ge(sig("y_rstd"), u + 1)
                dve.tensor_tensor(ysum[b][:, cols], ps[:, centered_bank[u], :], (te, tw)[b][:, cols],
                                  MUL).then_inc(sig("y_normed"), 1)

            def gate(u):
                b, h, cols = image_half(u)
                dve.wait_ge(sig("y_affine"), u + 1)
                dve.tensor_tensor(ysum[b][:, cols], ysum[b][:, cols], z_gate[:, b, cols], MUL).then_inc(sig("y_gated"), 1)

            for step, u in ((normalise, 0), (normalise, 1), (gate, 0), (gate, 1), (normalise, 2), (normalise, 3),
                            (gate, 2), (gate, 3)):
                step(u)
            for h in range(2):
                _, _, cols = image_half(h)
                dve.wait_ge(sig("l0_half"), h + 1)
                link(dve.tensor_tensor(x_res[:, cols], x_res[:, cols], ps[:, h, :], ADD))
            group_norm(x_res, 2)
            dve.tensor_scalar(xn1, x_res[:], small[:, 20:21], small[:, 5:6], SUB, MUL).then_inc(sig("gn_out"), 1)
            dve.wait_ge(sig("gates_done"), 1)
            dve.tensor_copy(sp_x, banks(6)).then_inc(sig("x_out"), 1)
            recurrence(dve, link, slice(0, HALF - POOL_COLS))
            dve.sem_inc(sig("dve_recurred"), 1)
            dve.wait_ge(*after("l1_done"))
            quarters = lambda t: t.rearrange("p (q n t) -> p q n t", q=4, t=2)
            dve.tensor_tensor(quarters(xn_t)[:, :, ::-1, :], quarters(x_res[:]), quarters(banks(0)),
                              ADD).then_inc(reach("x2_ready"), 1)
            dve.wait_ge(sig("turned_out"), 2)
            norm_dve(dve, link, 1, tok_flat, xn)
            dve.wait_ge(*after("k_done"))
            link(dve.tensor_reduce(small[:, 128:129], ps[:, 4:8, :].rearrange("p a n -> p (a n)"), AX.X, MAX))
            dve.tensor_scalar(small[:, 129:130], small[:, 128:129], -1.0, None, MUL).then_inc(reach("k_max"), 1)
            q_banks = banks(0).rearrange("p (u h d) -> p u h d", u=8, h=HEADS)

            def q_half(h):
                st = small[:, 136 + 32 * h:168 + 32 * h]
                rep = st.rearrange("p (u h) -> p u h", u=8).unsqueeze(3).broadcast_to([P, 8, HEADS, DH])
                return st, rep, q_e[:, h * L:(h + 1) * L].rearrange("p (u h d) -> p u h d", u=8, h=HEADS)

            for h in range(2):
                st, rep, q = q_half(h)
                dve.wait_ge(sig("qv_done"), h + 1)
                link(dve.tensor_reduce(st.rearrange("p (u h) -> p u h", u=8), q_banks, AX.X, MAX))
                dve.tensor_tensor(q, q_banks, rep, SUB).then_inc(sig("q_shifted"), 1)
            dve.wait_ge(*after("k_exp"))
            link(dve.tensor_scalar(small[:, 131:132], small[:, 130:131], float(B * L * np.sqrt(DH)), None, MUL))
            link(dve.reciprocal(small[:, 131:132], small[:, 131:132]))
            for h in range(2):
                st, rep, q = q_half(h)
                dve.wait_ge(sig("q_exp"), h + 1)
                link(dve.tensor_reduce(st.rearrange("p (u h) -> p u h", u=8), q, AX.X, ADD))
                link(dve.reciprocal(st, st))
                dve.tensor_tensor(q, q, rep, MUL).then_inc(sig("q_ready"), 1)
            dve.wait_ge(*after("ctx_done"))
            dve.tensor_tensor(ctx_m, ps[:, 4, 0:P], con("heads"), MUL).then_inc(reach("ctx_ready"), 1)
            dve.wait_ge(*after("mix_done"))
            dve.tensor_scalar(mix_m, ps[:, 5, 0:C], small[:, 131:132], None, MUL).then_inc(reach("mix_ready"), 1)

            def row(col, n=C):
                return rowb[:, col:col + n].unsqueeze(1).broadcast_to([P, UN, n])

            dve.wait_ge(*after("attn_out"))
            norm_dve(dve, link, 2, banks(4), xn_t)
            dve.wait_ge(sig("normed"), 2)
            link(dve.tensor_tensor(units(xn_t), units(xn_t), row(R_LNW), MUL))
            link(dve.tensor_tensor(tok_flat, tok_flat, xn_t, ADD))
            dve.sem_inc(reach("attn_done"), 1)
            norm_dve(dve, link, 3, tok_flat, xn)
            lg, g2, g3 = (gates[:, P * a:P * (a + 1)].rearrange("p (u e) -> p u e", u=UN) for a in range(3))
            top, top2, den = gates[:, 3 * P:3 * P + UN], gates[:, 3 * P + UN:3 * P + 2 * UN], gates[:, 4 * P:4 * P + UN]
            ranks = rank.unsqueeze(1).broadcast_to([P, UN, E])
            dve.wait_ge(*after("router_done"))
            link(dve.tensor_tensor(lg, ps[:, 2, 0:P].rearrange("p (u e) -> p u e", u=UN), row(R_RB, E), ADD))
            link(dve.tensor_reduce(top, lg, AX.X, MAX))
            dve.tensor_tensor(lg, lg, over(top, E), SUB).then_inc(reach("r_shifted"), 1)
            dve.wait_ge(*after("r_exp"))

            def first_best(dst, src, best):
                link(dve.tensor_reduce(best, src, AX.X, MAX))
                link(dve.tensor_tensor(dst, src, over(best, E), ALU.is_equal))
                link(dve.tensor_tensor(dst, dst, ranks, MUL))
                link(dve.tensor_reduce(den, dst, AX.X, MAX))
                link(dve.tensor_tensor(dst, dst, over(den, E), ALU.is_equal))

            first_best(g2, lg, top)
            link(dve.scalar_tensor_tensor(lg, g2, -2.0, lg, MUL, ADD))
            first_best(g3, lg, top2)
            link(dve.tensor_tensor(g3, g3, over(top2, E), MUL))
            link(dve.tensor_tensor(g2, g2, g3, ADD))
            link(dve.tensor_scalar(den, top2, 1.0, None, ADD))
            link(dve.reciprocal(den, den))
            dve.tensor_tensor(g2, g2, over(den, E), MUL).then_inc(reach("gates_ready"), 1)
            dve.wait_ge(*after("gates_ready"))
            for u in range(UN):
                dve.wait_ge(sig("expert_done"), u + 1)
                if u >= 4 and u % 2:
                    dve.wait_ge(sig("odd_sum"), (u - 4) // 2 + 1)
                elif u >= 4:
                    dve.wait_ge(sig("even_sum"), (u - 4) // 2 + 1)
                dve.tensor_tensor(prods[u % 4].rearrange("p (e c) -> p e c", e=E),
                                  ps[:, 4 + u % 4, :].rearrange("p (e c) -> p e c", e=E),
                                  g2[:, u, :].unsqueeze(2).broadcast_to([P, E, C]), MUL).then_inc(sig("weighted"), 1)
                if u % 2 == 1:
                    dve.wait_ge(sig("weighted"), u)
                    dve.tensor_reduce(units(xn)[:, u - 1, :], prods[(u - 1) % 4].rearrange("p (e c) -> p c e", e=E),
                                      AX.X, ADD).then_inc(sig("even_sum"), 1)
            dve.wait_ge(sig("even_sum"), UN // 2)
            dve.wait_ge(sig("odd_sum"), UN // 2)
            dve.wait_ge(*after("bias_done"))
            link(dve.tensor_tensor(tok_flat, banks(0), xn, ADD))
            dve.sem_inc(reach("moe_done"), 1)
            norm_dve(dve, link, 4, tok_flat, xn)
            dve.memset(is_sb, 0.0)
            dve.memset(g_sb, 0.0)
            dve.memset(g_two, 0.0).then_inc(reach("zeroed"), 1)
            dve.wait_ge(*after("zeroed"))
            copy_g(dve, 0, dve.tensor_copy, ps[:, 2, 0:P])
            for l in range(LAYERS):
                dve.wait_ge(sig("s_done"), l + 1)
                wait(dve, sig("wt_done"), l)
                for b in range(B):
                    r = slice(64 * b, 64 * b + 64)
                    ins = dve.scalar_tensor_tensor(is_sb[r, r], ps[r, 4, r], 1.0 / (L * LH), con("ident")[r, r],
                                                   MUL, ADD)
                ins.then_inc(sig("is_ready"), 1)
                if l < LAYERS - 1:
                    dve.wait_ge(sig("gs_done"), l + 1)
                    dve.tensor_copy(u_sb, ps[:, 5, 0:P]).then_inc(sig("gs_out"), 1)
                    copy_g(dve, l + 1, dve.tensor_copy, ps[:, 7, 0:P])
            def toep_low(k, a):
                dve.wait_ge(sig("toep_high"), k + 1)
                dve.tensor_tensor(toep_hl[:, a, 1:2, :], toep[:, bass.ds(k, 1), :],
                                  toep_hl[:, a, 0:1, :].bitcast(F32), SUB).then_inc(sig("toep_low"), 1)

            for a in range(2):
                toep_low(a, a)
            dve.wait_ge(*after("lin_out"))
            link(dve.tensor_tensor(tok_flat, tok_flat, banks(0), ADD))
            dve.sem_inc(reach("lin_done"), 1)
            norm_dve(dve, link, 5, tok_flat, xn)
            dve.wait_ge(sig("xn_high"), 1)
            dve.tensor_tensor(xn_hl[:, 1, :], xn, xn_hl[:, 0, :].bitcast(F32), SUB).then_inc(sig("xn_low"), 1)

            filter_loop(dve, toep_low)
            back(dve)
            for h in range(2):
                dve.wait_ge(sig("out_turned"), h + 1)
                dve.tensor_tensor(fin[:, h * HALF:(h + 1) * HALF], tok_flat[:, h * HALF:(h + 1) * HALF],
                                  ps[:, 2 + h, :], ADD).then_inc(sig("out_ready"), 1)

        @block.tensor
        def _(pe):
            def half(ap, h):
                return ap[:, h * HALF:(h + 1) * HALF]

            def pair_mean(n):
                pe.wait_ge(sig("gn_stats"), n)
                pe.matmul(ps[:, 7, 0:2], con("pair"), small[:, 0:2], start=True, stop=True).then_inc(sig("gn_pair"), 1)

            pe.wait_ge(sig("pair_in"), 16)
            pair_mean(1)
            pe.wait_ge(sig("w_dt_in"), 16)
            for k in range(ND):
                mm = pe.matmul(ps[:, 6, k * P:(k + 1) * P], w_dt_sb[:, 0, k, :], w_dt_sb[:, 1, k, :],
                               start=True, stop=True)
            mm.then_inc(sig("w_dt_done"), 1)

            def convolution(b, h):
                for t in range(9):
                    dy, dx = divmod(t, 3)
                    for part in range(2):
                        mm = pe.matmul(ps[:, h, :], front_hl[:, part, t * DI:(t + 1) * DI],
                                       pads[b][:, 16 * h + dy:16 * h + dy + 16, dx:dx + W],
                                       start=(t + part == 0), stop=(t + part == 9))
                if h == 1:
                    mm.then_inc(sig("conv_done"), 1)

            def gate(b):
                for h in range(2):
                    for part in range(2):
                        mm = pe.matmul(ps[:, 6 + h, :], front_hl[:, part, 10 * DI:11 * DI],
                                       pads[b][:, 16 * h + 1:16 * h + 17, 1:1 + W], start=(part == 0), stop=(part == 1))
                mm.then_inc(sig("z_done"), 1)

            def project(n, k, b, what, h):
                if h == 0:
                    if what == 0:
                        wait(pe, sig("w_now_set"), k + 1)
                        wait(pe, sig("c_ready"), n)
                    else:
                        wait(pe, sig(("abs_ready", "b_ready")[what - 1]), n + 1)
                mm = pe.matmul(ps[:, 6 + h, :].unsqueeze(1), w_now[:, what, :],
                               xs[:, b, bass.ds(k, 1), h * HALF:(h + 1) * HALF], start=True, stop=True)
                if h == 1:
                    mm.then_inc(sig("projected"), 1)

            def spread(n, b, i):
                u = GROUPS * n + i
                if i == 0:
                    wait(pe, sig("stacked"), 128 * (n + 1))
                j, v = i % 4, i // 4
                for what, used, spread_out in ((1, "driven", "drives_spread"), (0, "decayed", "steps_spread")):
                    wait(pe, sig(used), u)
                    for h in range(2):
                        mm = pe.matmul(ps[:, 2 * what + h, :], sel[:, 4 * (j % 2) + v, :],
                                       stack[:, b, what, j // 2, h * HALF:(h + 1) * HALF],
                                       start=True, stop=True)
                    mm.then_inc(sig(spread_out), 1)

            def sum_states(n, b, v, h, free=None):
                if h == 0 and isinstance(n, int) and n == B * ND - 1 and v == 3:
                    pe.wait_ge(sig("weighed"), UNITS - 2)
                    pe.wait_ge(sig("weighed_last"), 2)
                elif h == 0:
                    wait(pe, sig("weighed"), GROUPS * n + 4 * v + 4)
                    if v == 0:
                        free()
                for j in range(4):
                    mm = pe.matmul(ps[32 * j:32 * j + 32, 4 + h, :], red[:, v, :],
                                   state[:, (4 * v + j) % 8, h * HALF:(h + 1) * HALF],
                                   start=(v == 0), stop=(v == 3))
                if h == 1:
                    mm.then_inc(sig("summed"), 1)

            def center_first(step):
                term, h = divmod(step, 2)
                if step == 0:
                    pe.wait_ge(sig("c_ready"), B * ND)
                    pe.wait_ge(sig("y_free"), B * (ND - 1))
                if step == 6:
                    pe.wait_ge(sig("y_last"), 1)
                src = in_image_order(0, term, h) if term < 3 else half(ysum[0], h)
                mm = pe.matmul(ps[:, centered_bank[h], :], con("center"), src, start=(term == 0), stop=(term == 3))
                if term == 3:
                    mm.then_inc(sig("y_centered"), 1)

            projecting = (0, 1, 4, 5, 8, 13)

            def slot(k, s):
                n, b, i = split_slot(k, s)
                spread(n, b, i)
                nk, nb = following(k, b)

                def free():
                    if ends(k, b):
                        pe.wait_ge(sig("y_last"), 1)
                    else:
                        wait(pe, sig("y_free"), n + 1)
                if i in projecting and not ends(k, b):
                    what, h = divmod(projecting.index(i), 2)
                    project(n + 1, nk, nb, what, h)
                elif i in (2, 3) and not (isinstance(k, int) and s < GROUPS and k == 0):
                    sum_states(n - 1, 1 - b, 3, i - 2)
                elif i in (6, 7, 10, 11, 14, 15):
                    sum_states(n, b, (i - 6) // 4, (i - 6) % 4, free)
                elif ends(k, b):
                    center_first(i // 4 * 2 + i % 4)

            pe.wait_ge(sig("front_low"), 1)
            pe.wait_ge(sig("x_low"), 1)
            for h in range(2):
                convolution(0, h)
            pe.wait_ge(sig("w_dt_ready"), 1)
            gate(0)
            pe.wait_ge(sig("ab_in"), 16)
            pe.wait_ge(sig("dft_in"), 16)
            for f in range(2):
                for r in range(2):
                    for h in range(2):
                        mm = pe.matmul(ps[64 * h:64 * h + 64, 2 + 2 * f + r, :], ab_sb[:, f, :],
                                       dft_sb[0:2 * KK, r, h * HALF:(h + 1) * HALF], start=True, stop=True)
            mm.then_inc(sig("spec_done"), 1)
            pe.wait_ge(sig("orders_ready"), 1)
            pe.wait_ge(sig("z_ready"), 1)
            for h in range(2):
                project(0, 0, 0, 0, h)
            pe.wait_ge(sig("x_low"), 2)
            convolution(1, 0)
            for h in range(2):
                project(0, 0, 0, 1, h)
            convolution(1, 1)
            for h in range(2):
                project(0, 0, 0, 2, h)
            pe.wait_ge(sig("spec_out"), 1)
            pe.wait_ge(sig("c_ready"), 1)
            gate(1)
            pe.wait_ge(sig("z_ready"), 2)
            pe.wait_ge(sig("consts_in"), 16)
            pe.wait_ge(*after("sel_ready"))
            pe.wait_ge(sig("orders_ready"), 2)
            scan_loop(pe, slot)
            for h in range(2):
                sum_states(B * ND - 1, 1, 3, h)
            def center(u):
                b, h, cols = image_half(u)
                pe.wait_ge(sig("y_ready"), h + 1)
                pe.matmul(ps[:, centered_bank[u], :], con("center"), ysum[b][:, cols],
                          start=True, stop=True).then_inc(sig("y_centered"), 1)

            def variance(u):
                b, h, cols = image_half(u)
                pe.wait_ge(sig("y_squares"), u + 1)
                pe.matmul(ps[:, var_bank[u], :], con("mean"), (te, tw)[b][:, cols],
                          start=True, stop=True).then_inc(sig("y_var"), 1)

            def project_out(u):
                b, h, cols = image_half(u)
                pe.wait_ge(sig("y_gated"), u + 1)
                mm = pe.matmul(ps[64 * b:64 * b + 64, h, :], w_out_sb[:], ysum[b][:, cols], start=True, stop=True)
                if b == 1:
                    mm.then_inc(sig("l0_half"), 1)

            pe.wait_ge(sig("out_gate_in"), 32)
            for step, u in ((variance, 0), (variance, 1), (center, 2), (center, 3), (project_out, 0), (project_out, 1),
                            (variance, 2), (variance, 3), (project_out, 2), (project_out, 3)):
                step(u)
            pair_mean(2)
            pe.wait_ge(sig("gn_out"), 2)
            for bank, lhs in ((6, split), (4, w_gate_sb[:, 2]), (0, w_gate_sb[:, 0]), (2, w_gate_sb[:, 1])):
                for r in range(2):
                    for h in range(2):
                        mm = pe.matmul(ps[64 * h:64 * h + 64, bank + r, :], lhs[:, r, :], half(xn1, h),
                                       start=True, stop=True)
                mm.then_inc(sig("gates_done"), 1)
            pe.wait_ge(sig("dve_recurred"), 1)
            pe.wait_ge(sig("pool_recurred"), 1)
            for h in range(2):
                for r in range(2):
                    mm = pe.matmul(ps[:, h, :], merge[:, h, r, :], sp_v[:, r * HALF:(r + 1) * HALF],
                                   start=(r == 0), stop=(r == 1))
            mm.then_inc(reach("l1_done"), 1)

            def turn(src, bank):
                for j in range(TILES):
                    mm = pe.transpose(ps[:, bank + j // 4, (j % 4) * P:(j % 4 + 1) * P], src(j), ident)
                    if j % 4 == 3:
                        mm.then_inc(sig("turned"), 1)

            def tile(t):
                return lambda j: t[:, j * P:(j + 1) * P]

            pe.wait_ge(*after("x2_ready"))
            turn(lambda j: xn_t.rearrange("p (q n t) -> p q t n", q=4, t=2)[:, j // 2, j % 2, :], 2)
            pe.wait_ge(sig("normed"), 1)
            turn(tile(xn), 0)
            pe.wait_ge(sig("token_weights_in"), 96)
            for h in range(2):
                pe.wait_ge(sig("turned_out"), 3 + h)
                for b in range(B):
                    mm = pe.matmul(ps[:, 4 + 2 * b + h, :], w_k_sb[:, b * P:(b + 1) * P], half(xn_t, h),
                                   start=True, stop=True)
            mm.then_inc(reach("k_done"), 1)

            def queries_and_values(h):
                for j in range(4 * h, 4 * h + 4):
                    for what in range(2):
                        mm = pe.matmul(ps[:, 2 * what + j % 4 // 2, j % 2 * 256:(j % 2 + 1) * 256], tile(xn_t)(j),
                                       w_qv_sb[:, what * 256:(what + 1) * 256], start=True, stop=True)
                mm.then_inc(sig("qv_done"), 1)

            queries_and_values(0)
            pe.wait_ge(*after("k_exp"))
            for u in range(UN):
                mm = pe.transpose(ps[:, 4 + u // 4, (u % 4) * P:(u % 4 + 1) * P], tile(k_e)(u), ident)
            mm.then_inc(reach("k_turned"), 1)
            pe.wait_ge(sig("v_out"), 1)
            pe.wait_ge(sig("q_shifted"), 1)
            queries_and_values(1)
            pe.wait_ge(*after("k_tok_ready"))
            pe.wait_ge(sig("v_out"), 2)
            for u in range(UN):
                j, b = divmod(u, B)
                mm = pe.matmul(ps[:, 4, 0:P], tile(v_tok)(u), tile(k_tok)(b * TILES + j),
                               start=(u == 0), stop=(u == UN - 1))
            mm.then_inc(reach("ctx_done"), 1)
            for h in range(2):
                pe.wait_ge(sig("q_ready"), h + 1)
                for u in range(8):
                    mm = pe.transpose(ps[:, 2 * h + u // 4, (u % 4) * P:(u % 4 + 1) * P], tile(q_e)(8 * h + u), ident)
                mm.then_inc(sig("q_turned"), 1)
            pe.wait_ge(*after("ctx_ready"))
            pe.matmul(ps[:, 5, 0:C], ctx_m, w_attn_sb, start=True, stop=True).then_inc(reach("mix_done"), 1)
            pe.wait_ge(*after("mix_ready"))
            for h in range(2):
                pe.wait_ge(sig("q_t_ready"), h + 1)
                for b in range(B):
                    mm = pe.matmul(ps[64 * b:64 * b + 64, 6 + h, :].rearrange("p (j n) -> p j n", j=4), mix_m,
                                   q_t_sb[:, h * L:(h + 1) * L].rearrange("p (j b n) -> p j b n", j=4, b=B)[:, :, b, :],
                                   start=True, stop=True)
                mm.then_inc(sig("attended"), 1)
            for h in range(2):
                pe.wait_ge(sig("attended_out"), h + 1)
                for j in range(4):
                    mm = pe.transpose(ps[:, 4 + h, j * P:(j + 1) * P], tile(xn)(4 * h + j), ident)
            mm.then_inc(reach("attn_out"), 1)
            pe.wait_ge(sig("normed"), 3)
            turn(tile(xn), 0)
            for j in range(TILES):
                if j % 4 == 0:
                    pe.wait_ge(sig("turned_out"), 5 + j // 4)
                mm = pe.matmul(ps[:, 2, j * 16:(j + 1) * 16], tile(xn_t)(j), w_rt_sb, start=True, stop=True)
            mm.then_inc(reach("router_done"), 1)
            for u in range(UN):
                if u == 4:
                    pe.wait_ge(*after("gates_ready"))
                    pe.transpose(ps[:, 3, 0:P], gates[:, P:2 * P], ident).then_inc(reach("g_turned"), 1)
                if u >= 4:
                    pe.wait_ge(sig("weighted"), u - 3)
                pe.matmul(ps[:, 4 + u % 4, :], tile(xn_t)(u // B), w_exp_sb[:, (u % B) * 512:(u % B + 1) * 512],
                          start=True, stop=True).then_inc(sig("expert_done"), 1)
            pe.wait_ge(*after("g_t_ready"))
            for h in range(2):
                pe.matmul(ps[:, h, :], gates[:, 5 * P:6 * P], half(b_exp_sb, h), start=True, stop=False)
                mm = pe.matmul(ps[:, h, :], ident, half(tok_flat, h), start=False, stop=True)
            mm.then_inc(reach("bias_done"), 1)
            pe.wait_ge(sig("normed"), 4)
            for j in range(TILES):
                mm = pe.matmul(ps[:, 2, 0:P], tile(xn)(j), tile(xn)(j), start=(j == 0), stop=(j == TILES - 1))
            mm.then_inc(sig("g_done"), 1)
            turn(tile(xn), 0)
            pe.wait_ge(sig("linear_weights_in"), 32)
            for l in range(LAYERS):
                for b in range(B):
                    pe.wait_ge(sig(f"g_ready_{b}"), l + 1)
                    mm = pe.matmul(ps[:, 3, b * 256:(b + 1) * 256], g_two[:, b, :], v_sb[:, l, :],
                                   start=True, stop=True)
                mm.then_inc(sig("t_done"), 1)
                pe.wait_ge(sig("t_out"), l + 1)
                t_pairs = t_sb.rearrange("p (b h e) -> p b h e", b=B, h=4)
                for h in range(4):
                    mm = pe.matmul(ps[:, 4, 0:P].rearrange("p (b e) -> p b e", b=B), q_sb[:, l, h, :],
                                   t_pairs[:, :, h, :], start=(h == 0), stop=(h == 3))
                mm.then_inc(sig("s_done"), 1)
                pe.wait_ge(sig("is_ready"), l + 1)
                if l < LAYERS - 1:
                    pe.matmul(ps[:, 5, 0:P], g_sb, is_sb, start=True, stop=True).then_inc(sig("gs_done"), 1)
                wait(pe, sig("wt_out"), l)
                pe.matmul(ps[:, 6, 0:P], is_sb, wt_sb if l else ident, start=True, stop=True).then_inc(sig("wt_done"), 1)
                if l < LAYERS - 1:
                    pe.wait_ge(sig("gs_out"), l + 1)
                    pe.matmul(ps[:, 7, 0:P], is_sb, u_sb, start=True, stop=True).then_inc(sig("g_done"), 1)
            pe.wait_ge(sig("wt_out"), LAYERS)
            pe.transpose(ps[:, 6, 0:P], wt_sb, ident).then_inc(reach("w_turned"), 1)
            pe.wait_ge(*after("w_out_ready"))
            pe.wait_ge(sig("turned_out"), 8)
            for j in range(TILES):
                mm = pe.matmul(ps[:, j // 4, (j % 4) * P:(j % 4 + 1) * P], tile(xn_t)(j), wt_sb, start=True, stop=True)
            mm.then_inc(reach("lin_out"), 1)
            pe.wait_ge(sig("normed"), 5)
            turn(tile(xn), 0)
            pe.wait_ge(sig("xn_low"), 1)

            def convolve(k, a, s):
                if s == 0:
                    pe.wait_ge(sig("toep_low"), k + 1)
                if not isinstance(k, int) or k >= 1:
                    for b in range(B):
                        pe.wait_ge(sig(f"filtered_{b}"), 2 * k + s - 1)
                for t in range(2):
                    for q in range(4):
                        n, first, j = HALF - P * q, (0 if s == 0 else HALF + t), 2 * q + (t ^ s)
                        for i, (x_part, row_part) in enumerate(((0, 0), (0, 1), (1, 0))):
                            mm = pe.matmul(ps[:, 2 + 2 * s + t, P * q:HALF], xn_hl[:, x_part, j * P:(j + 1) * P],
                                           toep_hl[:, a, row_part, first:first + n],
                                           start=(q + i == 0), stop=(q == 3 and i == 2))
                mm.then_inc(sig("convolved"), 1)

            def mix(k, a, first=False, last=False):
                pe.wait_ge(sig("w_work_set"), k + 1)
                for b in range(B):
                    pe.wait_ge(sig(f"filtered_{b}"), 2 * k + 2)
                for g in (3, 2, 1, 0):
                    lo, hi = SPANS[g]
                    for b in range(B):
                        mm = pe.matmul(
                            ps[64 * b:64 * b + 64, lo // 256, :].rearrange(
                                "p (t n) -> p t n", t=2)[:, :, lo % 256:lo % 256 + hi - lo],
                            w_work[:, a, g * C:(g + 1) * C],
                            filt[:, a, b, :].rearrange("p (t n) -> p t n", t=2)[:, :, lo:hi],
                            start=first and g >= 2, stop=last and g in (0, 3), skip_group_check=True)
                mm.then_inc(sig("mixed"), 1)

            convolve(0, 0, 0)
            convolve(0, 0, 1)
            convolve(1, 1, 0)
            pe.wait_ge(sig("u_t_ready"), 2)
            mix(0, 0, True)
            convolve(1, 1, 1)
            with pe.Fori(1, KF // 2) as pair:
                convolve(2 * pair, 0, 0)
                mix(2 * pair - 1, 1)
                convolve(2 * pair, 0, 1)
                convolve(2 * pair + 1, 1, 0)
                mix(2 * pair, 0)
                convolve(2 * pair + 1, 1, 1)
            pe.wait_ge(sig("ar_added"), 4)
            pe.wait_ge(sig("u_t_zero"), 1)
            for g in (3, 2, 1, 0):
                lo, hi = SPANS[g]
                bank, at = lo // 256, lo % 256
                out_v = ps[:, bank, :].rearrange("p (t n) -> p t n", t=2)[:, :, at:at + hi - lo]
                for a, dst, src in ((0, out_v, u_t[:, :, 1 + lo:1 + hi]), (2, out_v, u_t[:, :, lo:hi]),
                                    (1, out_v[:, 0, :], u_t[:, 1, lo:hi]), (1, out_v[:, 1, :], u_t[:, 0, 1 + lo:1 + hi])):
                    pe.matmul(dst, w_ar[:, g, a, :], src, start=False, stop=False,
                              skip_group_check=True)
            mix(KF - 1, 1, last=True)
            for h in range(2):
                pe.wait_ge(sig(f"back_{h}"), 1)
            flat = y_back.rearrange("p (h t q n) -> p h t q n", h=2, t=2, q=2)
            for q in range(4):
                for t in range(2):
                    j = 2 * q + t
                    mm = pe.transpose(ps[:, 2 + j // 4, (j % 4) * P:(j % 4 + 1) * P], flat[:, q // 2, t, q % 2, :], ident)
                if q % 2 == 1:
                    mm.then_inc(sig("out_turned"), 1)


def constants():
    c = np.zeros((P, NCONST), np.float32)

    def part(name):
        return c[:, CONST[name][0]:CONST[name][1]]

    p = np.arange(P)
    part("ident")[:] = np.eye(P)
    for v in range(4):
        part("red")[:, v * 32:(v + 1) * 32] = (p[:, None] // NS + 8 * v) == np.arange(32)[None, :]
    sel = np.stack([(p[:, None] % 64 - 8 * v) == p[None, :] // NS for v in range(8)], 1).astype(np.float32)
    part("pair")[:] = 0.5 * (p[:, None] // 2 == p[None, :] // 2)
    part("mean")[:] = 1.0 / P
    part("center")[:] = np.eye(P) - 1.0 / P
    part("heads")[:] = p[:, None] // DH == p[None, :] // DH
    part("rank")[:] = np.arange(E, 0, -1)
    part("sign")[:, 0] = np.where(p < C, 1, -1)
    q = np.arange(64)
    for r in range(2):
        part("split")[:, r * 64:(r + 1) * 64] = p[:, None] == (q // 32 * 64 + r * 32 + q % 32)[None, :]
        for h in range(2):
            at = part("merge")[64 * h:64 * h + 64, (2 * h + r) * P:(2 * h + r + 1) * P]
            at[:] = (q // 32 * 64 + r * 32 + q % 32)[:, None] == p[None, :]
    k, t = np.arange(KK), np.arange(L)
    at = (12 + k[:, None] // 7) * (t[None, :] // W) + (12 + k[:, None] % 7) * (t[None, :] % W)
    cos, sin = np.cos(2 * np.pi * at / 32), np.sin(2 * np.pi * at / 32)
    dft = np.stack([np.concatenate([cos, sin]), np.concatenate([-sin, cos])], 1)
    return c, sel.reshape(P, 8 * P), dft.astype(np.float32)


def layouts(i):
    two = lambda a: np.concatenate([a, a], 0)
    d = list(DIRS)

    def blocks(a):
        out = np.zeros((B, C) + a.shape[1:-1] + (B, a.shape[-1]), np.float32)
        for b in range(B):
            out[b, ..., b, :] = a
        return out.reshape((P,) + a.shape[1:-1] + (B * a.shape[-1],))

    def heads(a):
        return a.reshape(LAYERS, 4, 2, C, C).transpose(2, 4, 0, 1, 3).reshape(P, LAYERS, 4, C)

    w_qkv = i["L2_attn_w_in"].T
    consts, sel, dft = constants()
    vec = np.zeros((P, NVEC), np.float32)
    vec[:, V_CONVB] = i["L0_conv_conv_b"]
    vec[:, V_D:V_D + 4] = i["L0_conv_Ds"].reshape(4, DI).T
    vec[:, V_LNW] = i["L0_conv_ln_w"]
    vec[:, V_LNB] = i["L0_conv_ln_b"]
    for col, name in ((V_BF, "bf"), (V_BI, "bi"), (V_BD, "bd")):
        vec[:, col:col + 2] = np.tile(i["L1_conv_" + name].reshape(2, C2).T, (4, 1))
    vec[:, V_BOUT] = np.tile(i["L2_attn_b_out"], 2)
    rows = np.concatenate([i["L2_attn_ln_w"], i["L2_ffn_router_b"],
                           i["L3_ffn_log_weights"], i["L3_ffn_gumbel"]])[None]
    xp = i["L0_conv_x_proj_w"][d]
    w_dt = np.stack([xp[:, :RANK].transpose(1, 0, 2), i["L0_conv_dt_w"][d].transpose(2, 0, 1)], 1)
    bc = xp[:, RANK:].reshape(ND, 2, 1, NS, DI)
    w_bc = np.broadcast_to(bc, (ND, 2, 8, NS, DI)).reshape(ND, 2, P, DI).transpose(3, 0, 1, 2)
    par = np.zeros((P, ND, 17), np.float32)
    rates = i["L0_conv_A_logs"].reshape(4, 4, 4, 8, NS)[d]
    par[:, :, 0:16] = rates.transpose(3, 4, 0, 2, 1).reshape(P, ND, 16)
    par[:, :, 16] = i["L0_conv_dt_b"][d].T
    w_gate = np.zeros((B, C, 3, 2, B, C2), np.float32)
    for g, name in enumerate(("Wf", "Wi", "Wd")):
        for b in range(B):
            w_gate[b, :, g, :, b, :] = i["L1_conv_" + name].reshape(C, 2, C2)
    ab = np.stack([np.concatenate([i[f"L1_conv_{n}_real"].reshape(C2, KK).T,
                                   i[f"L1_conv_{n}_imag"].reshape(C2, KK).T]) for n in "AB"], 1)
    b_expert = np.zeros((UN, E, UN, C), np.float32)
    for u in range(UN):
        b_expert[u, :, u, :] = i["L2_ffn_expert_b"]
    phi = np.zeros((KF, 2, 640), np.float32)
    phi[:, :, 128:] = i["L3_ffn_phi"][:L].reshape(HALF, 2, KF).transpose(2, 1, 0)
    m_phi = np.stack([i["L3_ffn_M_phi_plus"], i["L3_ffn_M_phi_minus"]], 1)
    return {
        "x_cm": i["x"].reshape(B, L, C).transpose(0, 2, 1).reshape(P, L),
        "consts": consts, "vec": vec, "rows": rows, "sel_c": sel,
        "w_in": two(i["L0_conv_w_in"].T),
        "conv_w": i["L0_conv_conv_w"].reshape(DI, 9).T.reshape(1, 9 * DI),
        "w_dt": w_dt, "w_bc": w_bc, "par": par,
        "w_out": i["L0_conv_w_out"].T,
        "w_gate": w_gate.reshape(P, 3, 2, 64), "ab": np.concatenate([ab, ab], 2), "dft": dft,
        "w_qv": np.concatenate([blocks(w_qkv[:, :P]), blocks(w_qkv[:, 2 * P:])], 1), "w_k": blocks(w_qkv[:, P:2 * P]),
        "w_attn": i["L2_attn_w_out"].T,
        "w_router": blocks(i["L2_ffn_router_w"]),
        "w_expert": blocks(i["L2_ffn_expert_w"].transpose(1, 0, 2).reshape(C, E * C)),
        "b_expert": b_expert.reshape(P, UN * C),
        "v_t": heads(i["L3_attn_v_matrix"]).reshape(P, LAYERS, 4 * C),
        "q_t": np.repeat(heads(i["L3_attn_q_matrix"])[:, :, :, None], 2, 3).reshape(P, LAYERS, 4, P),
        "phi": phi.reshape(2 * KF, 640), "sigma": np.repeat(i["L3_ffn_sigma"], 2)[:, None],
        "m_phi": two(m_phi.transpose(3, 0, 1, 2, 4).reshape(C, 4, 2, KF * C)),
        "m_u": blocks(i["L3_ffn_M_u"].transpose(2, 0, 1, 3)).reshape(P, 4, TAPS * P),
    }


_OUT = ((P, TILES * P), "float32")


def kernel(**inputs):
    import concourse.bacc as _bacc
    from concourse.bass_utils import run_bass_kernel_spmd as _run

    arrays = {f"in_{k}_dram": np.ascontiguousarray(v) for k, v in
              layouts({k: np.asarray(v) for k, v in inputs.items()}).items()}
    nc = _bacc.Bacc("TRN2", target_bir_lowering=False, num_devices=1)
    args = [nc.dram_tensor(k, a.shape, mybir.dt.from_np(a.dtype), kind="ExternalInput").ap()
            for k, a in arrays.items()]
    out = nc.dram_tensor("out_0_dram", _OUT[0], F32, kind="ExternalOutput").ap()
    program(nc, *args, out)
    got = _run(nc, [arrays], core_ids=[0]).results[0]["out_0_dram"]
    return got[::-1].reshape(P, 4, 2, B, C).transpose(3, 1, 0, 2, 4).reshape(B, H, W, C)
```
